# Optimizing a Trainium2 kernel written in Bass

```python
import numpy as np
import jax
import jax.numpy as jnp

def _softmax(x, axis=-1):
    return jax.nn.softmax(x, axis=axis)

def _gelu(x):
    return jax.nn.gelu(x, approximate=True)

def _silu(x):
    return jax.nn.silu(x)

def _sigmoid(x):
    return jax.nn.sigmoid(x)

def _layernorm(x, axis=-1, eps=1e-05):
    m = jnp.mean(x, axis=axis, keepdims=True)
    v = jnp.var(x, axis=axis, keepdims=True)
    return (x - m) / jnp.sqrt(v + eps)

def _scatter_add(tgt, idx, src, axis=0):
    return tgt.at[idx].add(src)

def _segment_sum(src, seg, n):
    return jax.ops.segment_sum(src, seg, n)
kernel_name = 'mk_xattn_ffn_d4_seqx_r8_860b36'

def setup_inputs(seed: int=0):
    np.random.seed(seed)
    _w = jnp.asarray

    def _rec_inputs():
        import jax
        import jax.numpy as jnp
        _rk = jax.random.key(seed)
        x = 7.22e-05 + 1 * jax.random.normal(jax.random.fold_in(_rk, 1), (16, 64, 256), jnp.float32)
        _lenS = 64 - jax.random.randint(jax.random.fold_in(_rk, 7), (16,), 0, max(1, 64 // 4) + 1, jnp.int32)
        _lenS2 = 64 - jax.random.randint(jax.random.fold_in(_rk, 8), (16,), 0, max(1, 64 // 4) + 1, jnp.int32)
        _ctx_2048P = jax.random.normal(jax.random.fold_in(_rk, 11), (16, 16, 256), jnp.float32)
        _ctx_2048c = jax.random.dirichlet(jax.random.fold_in(_rk, 511), 0.3 * jnp.ones((16,), jnp.float32), (16, 64))
        _ctx_2048t = jnp.einsum('bsk,bkd->bsd', _ctx_2048c, _ctx_2048P)
        _ctx_2048t = _ctx_2048t * jax.lax.rsqrt(jnp.mean(jnp.square(_ctx_2048t)) + 1e-12) * 0.953939
        ctx_2048 = 4.13588e-05 + 0.999923 * (_ctx_2048t + 0.3 * jax.random.normal(jax.random.fold_in(_rk, 611), (16, 64, 256), jnp.float32))
        _validS = jnp.arange(64)[None, :] < _lenS[:, None]
        _validS2 = jnp.arange(64)[None, :] < _lenS2[:, None]
        _causal = jnp.tril(jnp.ones((64, 64), dtype=bool))
        mask_BxSxS2_ff0 = jnp.where(jnp.ones((16, 64, 64), dtype=bool), 0.0, -1000000000.0).astype(jnp.float32)
        return (x, ctx_2048, mask_BxSxS2_ff0)
    x, ctx_2048, mask_BxSxS2_ff0 = _rec_inputs()

    def _L0_xattn_setup():
        import jax, jax.numpy as jnp
        import numpy as np
        N_HEAD = 8
        key = jax.random.key(seed)
        k1, k2, k3 = jax.random.split(key, 3)
        b, d, m = (4, 128, 256)
        c, n = (128, 256)
        q = jax.random.normal(k1, (b, d, m), dtype=jnp.float32)
        k = jax.random.normal(k2, (d // d * b, d, n), dtype=jnp.float32).reshape(b, d, n)
        v = jax.random.normal(k3, (b, c, n), dtype=jnp.float32)
        return {'q': q, 'k': k, 'v': v}
    _L0_xattn_all = _L0_xattn_setup()
    _L0_xattn_in = {k: v for k, v in _L0_xattn_all.items() if k in ()}
    del _L0_xattn_all

    def _L0_ffn_setup():
        import jax, jax.numpy as jnp
        import numpy as np
        DIM = 256
        INNER = 4 * DIM
        EPS = 1e-05

        def simple_rms_norm(x):
            d = x.shape[-1]
            n = jnp.linalg.norm(x, axis=-1, keepdims=True)
            return x / jnp.maximum(n, 1e-12) * jnp.sqrt(jnp.asarray(d, x.dtype))

        def activation_quant(x):
            scale = 127.0 / jnp.clip(jnp.max(jnp.abs(x), axis=-1, keepdims=True), EPS)
            return jnp.clip(jnp.round(x * scale), -128, 127) / scale

        def weight_quant(w):
            scale = 1.0 / jnp.clip(jnp.mean(jnp.abs(w)), EPS)
            return jnp.clip(jnp.round(w * scale), -1, 1) / scale

        def ste(x, q):
            return x + jax.lax.stop_gradient(q - x)

        def bitlinear158(x, w):
            xn = simple_rms_norm(x)
            xq = ste(xn, activation_quant(xn))
            wq = ste(w, weight_quant(w))
            return jnp.einsum('bsi,oi->bso', xq, wq)
        key = jax.random.key(seed)
        k1, k2, k3 = jax.random.split(key, 3)
        x = jax.random.normal(k1, (4, 256, DIM), dtype=jnp.float32)
        w1 = jax.random.normal(k2, (INNER, DIM), dtype=jnp.float32) * DIM ** (-0.5)
        w2 = jax.random.normal(k3, (DIM, INNER), dtype=jnp.float32) * INNER ** (-0.5)
        return {'x': x, 'w1': w1, 'w2': w2}
    _L0_ffn_all = _L0_ffn_setup()
    _L0_ffn_in = {k: v for k, v in _L0_ffn_all.items() if k in ('w1', 'w2')}
    del _L0_ffn_all

    def _L1_xattn_setup():
        import jax, jax.numpy as jnp
        import numpy as np
        N_HEAD = 8
        ALPHA = 5.0
        EPS = 1e-12

        def _l2norm(x, axis):
            n = jnp.sqrt(jnp.sum(x * x, axis=axis, keepdims=True))
            return x / jnp.maximum(n, EPS)
        key = jax.random.key(seed)
        kq, kk, kv = jax.random.split(key, 3)
        B, D, T = (4, 128, 256)
        q = jax.random.normal(kq, (B, D, T), dtype=jnp.float32)
        k = jax.random.normal(kk, (B, D, T), dtype=jnp.float32)
        v = jax.random.normal(kv, (B, D, T), dtype=jnp.float32)
        return {'q': q, 'k': k, 'v': v}
    _L1_xattn_all = _L1_xattn_setup()
    _L1_xattn_in = {k: v for k, v in _L1_xattn_all.items() if k in ()}
    del _L1_xattn_all

    def _L1_ffn_setup():
        import jax, jax.numpy as jnp
        import numpy as np
        B, S, D = (4, 64, 256)
        E, K, H = (8, 2, 176)
        HS = 2 * 176
        ALPHA = 0.001
        W_SCALE = 0.02

        def _moe_forward(hidden_states, gate_w, w_gate, w_up, w_down, sw_gate, sw_up, sw_down):
            b, s, d = hidden_states.shape
            x = hidden_states.reshape(-1, d)
            T = x.shape[0]
            logits = x @ gate_w
            scores = jax.nn.softmax(logits, axis=-1)
            topk_w, topk_idx = jax.lax.top_k(scores, K)
            mask = jax.nn.one_hot(topk_idx, E, dtype=scores.dtype).sum(axis=1)
            ce = mask.mean(axis=0)
            Pi = scores.mean(axis=0)
            aux_loss = (Pi * ce * E).sum() * ALPHA
            comb = jnp.zeros((T, E), dtype=x.dtype)
            comb = comb.at[jnp.arange(T)[:, None], topk_idx].add(topk_w)
            g = jax.nn.silu(jnp.einsum('td,edh->teh', x, w_gate)) * jnp.einsum('td,edh->teh', x, w_up)
            routed = jnp.einsum('teh,ehd,te->td', g, w_down, comb)
            shared = jax.nn.silu(x @ sw_gate) * (x @ sw_up) @ sw_down
            out = (routed + shared).reshape(b, s, d)
            return (out, aux_loss)
        key = jax.random.key(seed)
        ks = jax.random.split(key, 8)
        rn = lambda k, sh: jax.random.normal(k, sh, dtype=jnp.float32)
        return {'hidden_states': rn(ks[0], (B, S, D)), 'gate_w': rn(ks[1], (D, E)) * W_SCALE, 'w_gate': rn(ks[2], (E, D, H)) * W_SCALE, 'w_up': rn(ks[3], (E, D, H)) * W_SCALE, 'w_down': rn(ks[4], (E, H, D)) * W_SCALE, 'sw_gate': rn(ks[5], (D, HS)) * W_SCALE, 'sw_up': rn(ks[6], (D, HS)) * W_SCALE, 'sw_down': rn(ks[7], (HS, D)) * W_SCALE}
    _L1_ffn_all = _L1_ffn_setup()
    _L1_ffn_in = {k: v for k, v in _L1_ffn_all.items() if k in ('gate_w', 'w_gate', 'w_up', 'w_down', 'sw_gate', 'sw_up', 'sw_down')}
    del _L1_ffn_all

    def _L2_xattn_setup():
        import jax, jax.numpy as jnp
        import numpy as np
        N_HEAD = 8
        key = jax.random.key(seed)
        k1, k2, k3 = jax.random.split(key, 3)
        B, D, L = (4, 128, 256)
        q = jax.random.normal(k1, (B, D, L), dtype=jnp.float32)
        k = jax.random.normal(k2, (B, D, L), dtype=jnp.float32)
        v = jax.random.normal(k3, (B, D, L), dtype=jnp.float32)
        gamma = jnp.ones((), dtype=jnp.float32)
        return {'q': q, 'k': k, 'v': v, 'gamma': gamma}
    _L2_xattn_all = _L2_xattn_setup()
    _L2_xattn_in = {k: v for k, v in _L2_xattn_all.items() if k in ('gamma',)}
    del _L2_xattn_all

    def _L2_ffn_setup():
        import jax, jax.numpy as jnp
        import numpy as np
        B, S, H = (2, 256, 256)
        E, G, TKG, K = (32, 8, 4, 8)
        I, SI = (128, 256)
        ROUTED_SCALE = 2.5

        def _moe_forward(hidden_states, router_w, router_bias, w_gate, w_up, w_down, sw_gate, sw_up, sw_down):
            x = hidden_states.reshape(-1, H)
            T = x.shape[0]
            logits = x.astype(jnp.float32) @ router_w.astype(jnp.float32)
            scores = jax.nn.sigmoid(logits)
            scores_grouped = (scores + router_bias).reshape(T, G, E // G)
            top2, _ = jax.lax.top_k(scores_grouped, 2)
            group_scores = top2.sum(-1)
            _, top_groups = jax.lax.top_k(group_scores, TKG)
            mask = jnp.ones((T, G), bool).at[jnp.arange(T)[:, None], top_groups].set(False)
            masked = jnp.where(mask[:, :, None], 0.0, scores_grouped).reshape(T, E)
            _, top_k_index = jax.lax.top_k(masked, K)
            tkw = jnp.take_along_axis(scores, top_k_index, axis=-1)
            tkw = tkw / tkw.sum(-1, keepdims=True)
            tkw = (tkw * ROUTED_SCALE).astype(hidden_states.dtype)
            flat_idx = top_k_index.reshape(-1)
            sort_idx = jnp.argsort(flat_idx)
            xs = jnp.repeat(x, K, axis=0)[sort_idx]
            group_sizes = jnp.bincount(flat_idx, length=E).astype(jnp.int32)
            gate = jax.lax.ragged_dot(xs, w_gate, group_sizes)
            up = jax.lax.ragged_dot(xs, w_up, group_sizes)
            down = jax.lax.ragged_dot(jax.nn.silu(gate) * up, w_down, group_sizes)
            unsort = jnp.argsort(sort_idx)
            routed = (down[unsort].reshape(T, K, H) * tkw[..., None]).sum(axis=1)
            shared = jax.nn.silu(x @ sw_gate) * (x @ sw_up) @ sw_down
            return (routed + shared).reshape(hidden_states.shape)
        key = jax.random.key(seed)
        ks = jax.random.split(key, 9)

        def w(k, shape, fan_in):
            return jax.random.normal(k, shape, jnp.float32) / np.float32(np.sqrt(fan_in))
        return dict(hidden_states=jax.random.normal(ks[0], (B, S, H), jnp.float32), router_w=w(ks[1], (H, E), H), router_bias=jnp.zeros((E,), jnp.float32), w_gate=w(ks[2], (E, H, I), H), w_up=w(ks[3], (E, H, I), H), w_down=w(ks[4], (E, I, H), I), sw_gate=w(ks[5], (H, SI), H), sw_up=w(ks[6], (H, SI), H), sw_down=w(ks[7], (SI, H), SI))
    _L2_ffn_all = _L2_ffn_setup()
    _L2_ffn_in = {k: v for k, v in _L2_ffn_all.items() if k in ('router_w', 'router_bias', 'w_gate', 'w_up', 'w_down', 'sw_gate', 'sw_up', 'sw_down')}
    del _L2_ffn_all

    def _L3_xattn_setup():
        import jax, jax.numpy as jnp
        import numpy as np
        NUM_HEADS = 16
        EPS = 1e-08

        def _dyn_quant(x):
            s = jnp.maximum(jnp.max(jnp.abs(x), axis=-1, keepdims=True) / 127.0, EPS)
            q = jnp.clip(jnp.round(x / s), -127.0, 127.0)
            return (q, s)

        def _quant_weight(w):
            s = jnp.maximum(jnp.max(jnp.abs(w), axis=1, keepdims=True) / 127.0, EPS)
            q = jnp.clip(jnp.round(w / s), -127.0, 127.0)
            return (q, s)

        def _w8a8_linear(x, w, b):
            qx, sx = _dyn_quant(x)
            qw, sw = _quant_weight(w)
            y = jnp.einsum('bnc,oc->bno', qx, qw) * (sx * sw[:, 0])
            return y + b
        key = jax.random.key(seed)
        ks = jax.random.split(key, 9)
        B, N, L, C = (2, 512, 64, 256)
        sc = 0.02
        return {'x': jax.random.normal(ks[0], (B, N, C), jnp.float32), 'cond': jax.random.normal(ks[1], (B, L, C), jnp.float32), 'mask': jnp.zeros((B, N, L), jnp.float32), 'wq': jax.random.normal(ks[2], (C, C), jnp.float32) * sc, 'bq': jnp.zeros((C,), jnp.float32), 'wk': jax.random.normal(ks[3], (C, C), jnp.float32) * sc, 'bk': jnp.zeros((C,), jnp.float32), 'wv': jax.random.normal(ks[4], (C, C), jnp.float32) * sc, 'bv': jnp.zeros((C,), jnp.float32), 'wo': jax.random.normal(ks[5], (C, C), jnp.float32) * sc, 'bo': jnp.zeros((C,), jnp.float32)}
    _L3_xattn_all = _L3_xattn_setup()
    _L3_xattn_in = {k: v for k, v in _L3_xattn_all.items() if k in ('wq', 'bq', 'wk', 'bk', 'wv', 'bv', 'wo', 'bo')}
    del _L3_xattn_all

    def _L3_ffn_setup():
        import jax, jax.numpy as jnp
        import numpy as np
        TOP_K = 4

        def _silu_and_mul(gu):
            g, u = jnp.split(gu, 2, axis=-1)
            return jax.nn.silu(g) * u
        key = jax.random.key(seed)
        ks = jax.random.split(key, 7)
        H, E, I, Is = (256, 16, 176, 704)
        s = 0.02
        return {'hidden_states': jax.random.normal(ks[0], (4, 128, H), dtype=jnp.float32), 'gate_w': jax.random.normal(ks[1], (E, H), dtype=jnp.float32) * s, 'sgate_w': jax.random.normal(ks[2], (1, H), dtype=jnp.float32) * s, 'w13': jax.random.normal(ks[3], (E, 2 * I, H), dtype=jnp.float32) * s, 'w2': jax.random.normal(ks[4], (E, H, I), dtype=jnp.float32) * s, 'shared_gate_up_w': jax.random.normal(ks[5], (2 * Is, H), dtype=jnp.float32) * s, 'shared_down_w': jax.random.normal(ks[6], (H, Is), dtype=jnp.float32) * s}
    _L3_ffn_all = _L3_ffn_setup()
    _L3_ffn_in = {k: v for k, v in _L3_ffn_all.items() if k in ('gate_w', 'sgate_w', 'w13', 'w2', 'shared_gate_up_w', 'shared_down_w')}
    del _L3_ffn_all
    return {'x': x, 'ctx_2048': ctx_2048, 'mask_BxSxS2_ff0': mask_BxSxS2_ff0, 'L0_ffn_w1': _L0_ffn_in['w1'], 'L0_ffn_w2': _L0_ffn_in['w2'], 'L1_ffn_gate_w': _L1_ffn_in['gate_w'], 'L1_ffn_w_gate': _L1_ffn_in['w_gate'], 'L1_ffn_w_up': _L1_ffn_in['w_up'], 'L1_ffn_w_down': _L1_ffn_in['w_down'], 'L1_ffn_sw_gate': _L1_ffn_in['sw_gate'], 'L1_ffn_sw_up': _L1_ffn_in['sw_up'], 'L1_ffn_sw_down': _L1_ffn_in['sw_down'], 'L2_xattn_gamma': _L2_xattn_in['gamma'], 'L2_ffn_router_w': _L2_ffn_in['router_w'], 'L2_ffn_router_bias': _L2_ffn_in['router_bias'], 'L2_ffn_w_gate': _L2_ffn_in['w_gate'], 'L2_ffn_w_up': _L2_ffn_in['w_up'], 'L2_ffn_w_down': _L2_ffn_in['w_down'], 'L2_ffn_sw_gate': _L2_ffn_in['sw_gate'], 'L2_ffn_sw_up': _L2_ffn_in['sw_up'], 'L2_ffn_sw_down': _L2_ffn_in['sw_down'], 'L3_xattn_wq': _L3_xattn_in['wq'], 'L3_xattn_bq': _L3_xattn_in['bq'], 'L3_xattn_wk': _L3_xattn_in['wk'], 'L3_xattn_bk': _L3_xattn_in['bk'], 'L3_xattn_wv': _L3_xattn_in['wv'], 'L3_xattn_bv': _L3_xattn_in['bv'], 'L3_xattn_wo': _L3_xattn_in['wo'], 'L3_xattn_bo': _L3_xattn_in['bo'], 'L3_ffn_gate_w': _L3_ffn_in['gate_w'], 'L3_ffn_sgate_w': _L3_ffn_in['sgate_w'], 'L3_ffn_w13': _L3_ffn_in['w13'], 'L3_ffn_w2': _L3_ffn_in['w2'], 'L3_ffn_shared_gate_up_w': _L3_ffn_in['shared_gate_up_w'], 'L3_ffn_shared_down_w': _L3_ffn_in['shared_down_w']}

def reference(x, ctx_2048, mask_BxSxS2_ff0, L0_ffn_w1, L0_ffn_w2, L1_ffn_gate_w, L1_ffn_w_gate, L1_ffn_w_up, L1_ffn_w_down, L1_ffn_sw_gate, L1_ffn_sw_up, L1_ffn_sw_down, L2_xattn_gamma, L2_ffn_router_w, L2_ffn_router_bias, L2_ffn_w_gate, L2_ffn_w_up, L2_ffn_w_down, L2_ffn_sw_gate, L2_ffn_sw_up, L2_ffn_sw_down, L3_xattn_wq, L3_xattn_bq, L3_xattn_wk, L3_xattn_bk, L3_xattn_wv, L3_xattn_bv, L3_xattn_wo, L3_xattn_bo, L3_ffn_gate_w, L3_ffn_sgate_w, L3_ffn_w13, L3_ffn_w2, L3_ffn_shared_gate_up_w, L3_ffn_shared_down_w):
    import jax
    import jax.numpy as jnp

    def _L0_xattn_ref(q, k, v):
        import jax, jax.numpy as jnp
        import numpy as np
        N_HEAD = 8
        b, d, m = q.shape
        c = v.shape[1]
        h = N_HEAD
        qh = q.reshape(b * h, d // h, m)
        kh = k.reshape(b * h, d // h, -1)
        vh = v.reshape(b * h, c // h, -1)
        scale = 1.0 / jnp.sqrt(jnp.asarray(d // h, dtype=q.dtype))
        qk = jnp.einsum('bdm,bdn->bmn', qh, kh) * scale
        sm = jax.nn.softmax(qk, axis=-1)
        ret = jnp.einsum('bmn,bcn->bcm', sm, vh)
        return ret.reshape(b, c, m)

    def _L0_ffn_ref(x, w1, w2):
        import jax, jax.numpy as jnp
        import numpy as np
        DIM = 256
        INNER = 4 * DIM
        EPS = 1e-05

        def simple_rms_norm(x):
            d = x.shape[-1]
            n = jnp.linalg.norm(x, axis=-1, keepdims=True)
            return x / jnp.maximum(n, 1e-12) * jnp.sqrt(jnp.asarray(d, x.dtype))

        def activation_quant(x):
            scale = 127.0 / jnp.clip(jnp.max(jnp.abs(x), axis=-1, keepdims=True), EPS)
            return jnp.clip(jnp.round(x * scale), -128, 127) / scale

        def weight_quant(w):
            scale = 1.0 / jnp.clip(jnp.mean(jnp.abs(w)), EPS)
            return jnp.clip(jnp.round(w * scale), -1, 1) / scale

        def ste(x, q):
            return x + jax.lax.stop_gradient(q - x)

        def bitlinear158(x, w):
            xn = simple_rms_norm(x)
            xq = ste(xn, activation_quant(xn))
            wq = ste(w, weight_quant(w))
            return jnp.einsum('bsi,oi->bso', xq, wq)
        h = jax.nn.gelu(bitlinear158(x, w1), approximate=False)
        h = jax.nn.gelu(h, approximate=False)
        return bitlinear158(h, w2)

    def _L1_xattn_ref(q, k, v):
        import jax, jax.numpy as jnp
        import numpy as np
        N_HEAD = 8
        ALPHA = 5.0
        EPS = 1e-12

        def _l2norm(x, axis):
            n = jnp.sqrt(jnp.sum(x * x, axis=axis, keepdims=True))
            return x / jnp.maximum(n, EPS)
        B, D, Tq = q.shape
        Tk = k.shape[-1]
        Dv = v.shape[-2]
        h = N_HEAD
        d = D // h
        dv = Dv // h
        qh = q.reshape(B, h, d, Tq)
        kh = k.reshape(B, h, d, Tk)
        vh = v.reshape(B, h, dv, Tk)
        qn = _l2norm(qh, axis=-2)
        kn = _l2norm(kh, axis=-2)
        qk = ALPHA * jnp.einsum('bhdq,bhdk->bhqk', qn, kn)
        sm = jax.nn.softmax(qk, axis=-1)
        out = jnp.einsum('bhqk,bhdk->bhdq', sm, vh)
        return out.reshape(B, Dv, Tq)

    def _L1_ffn_ref(hidden_states, gate_w, w_gate, w_up, w_down, sw_gate, sw_up, sw_down):
        import jax, jax.numpy as jnp
        import numpy as np
        B, S, D = (4, 64, 256)
        E, K, H = (8, 2, 176)
        HS = 2 * 176
        ALPHA = 0.001
        W_SCALE = 0.02

        def _moe_forward(hidden_states, gate_w, w_gate, w_up, w_down, sw_gate, sw_up, sw_down):
            b, s, d = hidden_states.shape
            x = hidden_states.reshape(-1, d)
            T = x.shape[0]
            logits = x @ gate_w
            scores = jax.nn.softmax(logits, axis=-1)
            topk_w, topk_idx = jax.lax.top_k(scores, K)
            mask = jax.nn.one_hot(topk_idx, E, dtype=scores.dtype).sum(axis=1)
            ce = mask.mean(axis=0)
            Pi = scores.mean(axis=0)
            aux_loss = (Pi * ce * E).sum() * ALPHA
            comb = jnp.zeros((T, E), dtype=x.dtype)
            comb = comb.at[jnp.arange(T)[:, None], topk_idx].add(topk_w)
            g = jax.nn.silu(jnp.einsum('td,edh->teh', x, w_gate)) * jnp.einsum('td,edh->teh', x, w_up)
            routed = jnp.einsum('teh,ehd,te->td', g, w_down, comb)
            shared = jax.nn.silu(x @ sw_gate) * (x @ sw_up) @ sw_down
            out = (routed + shared).reshape(b, s, d)
            return (out, aux_loss)
        out, _aux = _moe_forward(hidden_states, gate_w, w_gate, w_up, w_down, sw_gate, sw_up, sw_down)
        return out

    def _L2_xattn_ref(q, k, v, gamma):
        import jax, jax.numpy as jnp
        import numpy as np
        N_HEAD = 8
        B, Dq, Lq = q.shape
        Dv, Lk = (v.shape[-2], v.shape[-1])
        h = N_HEAD
        dq = Dq // h
        dv = Dv // h
        qh = q.reshape(B, h, dq, Lq)
        kh = k.reshape(B, h, dq, Lk)
        vh = v.reshape(B, h, dv, Lk)
        scale = 1.0 / jnp.sqrt(jnp.asarray(dq, dtype=q.dtype))
        qk = jnp.einsum('bhdq,bhdl->bhql', qh, kh) * scale
        sm = jax.nn.softmax(qk, axis=-1)
        ret = jnp.einsum('bhql,bhdl->bhdq', sm, vh)
        ret = ret.reshape(B, Dv, Lq)
        return gamma * ret

    def _L2_ffn_ref(hidden_states, router_w, router_bias, w_gate, w_up, w_down, sw_gate, sw_up, sw_down):
        import jax, jax.numpy as jnp
        import numpy as np
        B, S, H = (2, 256, 256)
        E, G, TKG, K = (32, 8, 4, 8)
        I, SI = (128, 256)
        ROUTED_SCALE = 2.5

        def _moe_forward(hidden_states, router_w, router_bias, w_gate, w_up, w_down, sw_gate, sw_up, sw_down):
            x = hidden_states.reshape(-1, H)
            T = x.shape[0]
            logits = x.astype(jnp.float32) @ router_w.astype(jnp.float32)
            scores = jax.nn.sigmoid(logits)
            scores_grouped = (scores + router_bias).reshape(T, G, E // G)
            top2, _ = jax.lax.top_k(scores_grouped, 2)
            group_scores = top2.sum(-1)
            _, top_groups = jax.lax.top_k(group_scores, TKG)
            mask = jnp.ones((T, G), bool).at[jnp.arange(T)[:, None], top_groups].set(False)
            masked = jnp.where(mask[:, :, None], 0.0, scores_grouped).reshape(T, E)
            _, top_k_index = jax.lax.top_k(masked, K)
            tkw = jnp.take_along_axis(scores, top_k_index, axis=-1)
            tkw = tkw / tkw.sum(-1, keepdims=True)
            tkw = (tkw * ROUTED_SCALE).astype(hidden_states.dtype)
            flat_idx = top_k_index.reshape(-1)
            sort_idx = jnp.argsort(flat_idx)
            xs = jnp.repeat(x, K, axis=0)[sort_idx]
            group_sizes = jnp.bincount(flat_idx, length=E).astype(jnp.int32)
            gate = jax.lax.ragged_dot(xs, w_gate, group_sizes)
            up = jax.lax.ragged_dot(xs, w_up, group_sizes)
            down = jax.lax.ragged_dot(jax.nn.silu(gate) * up, w_down, group_sizes)
            unsort = jnp.argsort(sort_idx)
            routed = (down[unsort].reshape(T, K, H) * tkw[..., None]).sum(axis=1)
            shared = jax.nn.silu(x @ sw_gate) * (x @ sw_up) @ sw_down
            return (routed + shared).reshape(hidden_states.shape)
        return _moe_forward(hidden_states, router_w, router_bias, w_gate, w_up, w_down, sw_gate, sw_up, sw_down)

    def _L3_xattn_ref(x, cond, mask, wq, bq, wk, bk, wv, bv, wo, bo):
        import jax, jax.numpy as jnp
        import numpy as np
        NUM_HEADS = 16
        EPS = 1e-08

        def _dyn_quant(x):
            s = jnp.maximum(jnp.max(jnp.abs(x), axis=-1, keepdims=True) / 127.0, EPS)
            q = jnp.clip(jnp.round(x / s), -127.0, 127.0)
            return (q, s)

        def _quant_weight(w):
            s = jnp.maximum(jnp.max(jnp.abs(w), axis=1, keepdims=True) / 127.0, EPS)
            q = jnp.clip(jnp.round(w / s), -127.0, 127.0)
            return (q, s)

        def _w8a8_linear(x, w, b):
            qx, sx = _dyn_quant(x)
            qw, sw = _quant_weight(w)
            y = jnp.einsum('bnc,oc->bno', qx, qw) * (sx * sw[:, 0])
            return y + b
        B, N, C = x.shape
        L = cond.shape[1]
        H = NUM_HEADS
        D = C // H
        inv_sqrt_d = np.float32(1.0 / np.sqrt(D))
        q = _w8a8_linear(x, wq, bq).reshape(B, N, H, D).transpose(0, 2, 1, 3)
        k = (cond @ wk.T + bk).reshape(B, L, H, D).transpose(0, 2, 1, 3)
        v = (cond @ wv.T + bv).reshape(B, L, H, D).transpose(0, 2, 1, 3)
        scores = jnp.einsum('bhnd,bhld->bhnl', q, k) * inv_sqrt_d + mask[:, None]
        attn = jax.nn.softmax(scores, axis=-1)
        o = jnp.einsum('bhnl,bhld->bhnd', attn, v)
        o = o.transpose(0, 2, 1, 3).reshape(B, N, C)
        return _w8a8_linear(o, wo, bo)

    def _L3_ffn_ref(hidden_states, gate_w, sgate_w, w13, w2, shared_gate_up_w, shared_down_w):
        import jax, jax.numpy as jnp
        import numpy as np
        TOP_K = 4

        def _silu_and_mul(gu):
            g, u = jnp.split(gu, 2, axis=-1)
            return jax.nn.silu(g) * u
        B, S, H = hidden_states.shape
        x = hidden_states.reshape(-1, H)
        E = gate_w.shape[0]
        shared = _silu_and_mul(x @ shared_gate_up_w.T) @ shared_down_w.T
        shared = shared * jax.nn.sigmoid(x @ sgate_w.T)
        router_logits = x @ gate_w.T
        routing_weights = jax.nn.softmax(router_logits.astype(jnp.float32), axis=-1)
        topk_w, topk_ids = jax.lax.top_k(routing_weights, TOP_K)

        def body(acc, ew):
            w13_e, w2_e, e = ew
            coef = jnp.sum(jnp.where(topk_ids == e, topk_w, 0.0), axis=-1)
            h = _silu_and_mul(x @ w13_e.T)
            acc = acc + (h @ w2_e.T).astype(jnp.float32) * coef[:, None]
            return (acc, None)
        init = jnp.zeros((x.shape[0], H), dtype=jnp.float32)
        sparse_out, _ = jax.lax.scan(body, init, (w13, w2, jnp.arange(E)))
        out = shared + sparse_out.astype(x.dtype)
        return out.reshape(B, S, H)
    x = x + _L0_xattn_ref(_layernorm(x, axis=-1), ctx_2048, ctx_2048)
    x = x + _L0_ffn_ref(_layernorm(x, axis=-1), L0_ffn_w1, L0_ffn_w2)
    x = x + _L1_xattn_ref(_layernorm(x, axis=-1), ctx_2048, ctx_2048)
    x = x + _L1_ffn_ref(_layernorm(x, axis=-1), L1_ffn_gate_w, L1_ffn_w_gate, L1_ffn_w_up, L1_ffn_w_down, L1_ffn_sw_gate, L1_ffn_sw_up, L1_ffn_sw_down)
    x = x + _L2_xattn_ref(_layernorm(x, axis=-1), ctx_2048, ctx_2048, L2_xattn_gamma)
    x = x + _L2_ffn_ref(_layernorm(x, axis=-1), L2_ffn_router_w, L2_ffn_router_bias, L2_ffn_w_gate, L2_ffn_w_up, L2_ffn_w_down, L2_ffn_sw_gate, L2_ffn_sw_up, L2_ffn_sw_down)
    x = x + _L3_xattn_ref(_layernorm(x, axis=-1), ctx_2048, mask_BxSxS2_ff0, L3_xattn_wq, L3_xattn_bq, L3_xattn_wk, L3_xattn_bk, L3_xattn_wv, L3_xattn_bv, L3_xattn_wo, L3_xattn_bo)
    x = x + _L3_ffn_ref(_layernorm(x, axis=-1), L3_ffn_gate_w, L3_ffn_sgate_w, L3_ffn_w13, L3_ffn_w2, L3_ffn_shared_gate_up_w, L3_ffn_shared_down_w)
    return x

_drawn_inputs = setup_inputs


def setup_inputs(seed=0):
    import zlib

    import numpy as np

    out = dict(_drawn_inputs(seed))
    spreads = {'L2_ffn_router_bias': (0.0, 0.1),
     'L3_xattn_bq': (0.0, 0.8),
     'L3_xattn_bk': (0.0, 2.0),
     'L3_xattn_bv': (0.0, 0.692),
     'L3_xattn_bo': (0.0, 0.331)}
    factors = {'L1_ffn_gate_w': 7.888,
     'L1_ffn_w_gate': 8.0,
     'L1_ffn_w_up': 8.0,
     'L1_ffn_w_down': 8.0,
     'L1_ffn_sw_gate': 2.73,
     'L1_ffn_sw_up': 2.978,
     'L1_ffn_sw_down': 2.788,
     'L3_xattn_wq': 8.0,
     'L3_xattn_wk': 8.0,
     'L3_xattn_wv': 2.969,
     'L3_ffn_gate_w': 8.0,
     'L3_ffn_sgate_w': 8.0,
     'L3_ffn_w13': 8.0,
     'L3_ffn_w2': 8.0,
     'L3_ffn_shared_gate_up_w': 8.0,
     'L3_ffn_shared_down_w': 8.0}
    for name, (base, spread) in spreads.items():
        noise = np.random.default_rng([zlib.crc32(name.encode()), seed]).standard_normal(out[name].shape)
        drawn = base * np.exp(spread * noise) if base else spread * noise
        out[name] = jnp.asarray(drawn.astype(out[name].dtype))
    for name, factor in factors.items():
        out[name] = (out[name] * factor).astype(out[name].dtype)
    return out
```

```python
import numpy as np
from contextlib import ExitStack

import concourse.bass as bass
from concourse import mybir

F32 = mybir.dt.float32
F32R = mybir.dt.float32r
BF16 = mybir.dt.bfloat16
ALU = mybir.AluOpType
ACT = mybir.ActivationFunctionType
AX = mybir.AxisListType

P = 128
B, S, D = 16, 64, 256
T = B * S
NI = T // P
NK = D // P
HEADS, CH = 8, 8
LN_EPS = 1e-5
PAD = -1e30
ROUND = 1.5 * 2.0 ** 23


class Link:

    def __init__(self, eng, sem):
        self.eng, self.sem, self.count = eng, sem, 0

    def __call__(self, instruction):
        self.count += 1
        instruction.then_inc(self.sem, 1)
        self.eng.wait_ge(self.sem, self.count)


class Stage:

    def __init__(self, nc, ctx, name):
        self.nc, self.ctx, self.name = nc, ctx, name

    def sb(self, name, shape, dt=F32):
        return self.ctx.enter_context(self.nc.sbuf_tensor(f"{self.name}_{name}", shape, dt))

    def ps(self, name, shape=(P, 512)):
        return self.ctx.enter_context(self.nc.psum_tensor(f"{self.name}_{name}", list(shape), F32))

    def sem(self, name):
        handle = self.nc.alloc_semaphore(f"{self.name}_{name}")
        Stage.held.append(handle)
        return handle

    held = []

    @staticmethod
    def recycle(nc):
        nc.all_engine_barrier()
        nc.clear_and_free_semaphores(Stage.held)
        nc.all_engine_barrier()
        Stage.held = []


class Step:

    def __init__(self, g, r, n):
        self.g, self.r, self.n = g, r, n

    def __add__(self, by):
        return Step(self.g, self.r + by, self.n)


def lin(b, times, plus):
    return b.g * (b.n * times) + (b.r * times + plus) if isinstance(b, Step) else times * b + plus


def half(b):
    return b.g * (b.n // 2) + b.r // 2 if isinstance(b, Step) else b // 2


def slot(b, n):
    return (b.r if isinstance(b, Step) else b) % n


def uses(b, n):
    return b.g * (b.n // n) + b.r // n if isinstance(b, Step) else b // n


def wait(eng, sem, b, times, plus):
    value = lin(b, times, plus)
    if isinstance(b, Step) or value > 0:
        eng.wait_ge(sem, value)


def bc(ap, *dims):
    return bass.AP(ap.tensor, ap.offset, [list(ap.ap[0])] + [list(d) for d in dims])



class Norm:

    def __init__(self, st, x, xn):
        self.nc, self.x, self.xn = st.nc, x, xn
        self.stats = st.sb("ln_stats", [P, NI, 6])
        self.mv = st.sb("ln_mv", [P, NI, 2])
        self.var = st.sb("ln_var", [P, NI])
        self.root = st.sb("ln_root", [P, NI])
        self.tmp = st.sb("ln_tmp", [P, NI])
        self.var_ready = st.sem("ln_var_ready")
        self.root_ready = st.sem("ln_root_ready")
        self.xn_ready = st.sem("ln_xn_ready")

    def scalar(self, act):
        act.wait_ge(self.var_ready, 1)
        self.nc.scalar.activation(self.root[:], self.var[:], ACT.Sqrt).then_inc(self.root_ready, 1)

    def vector(self, dve, link):
        v = self.nc.vector
        for i in range(NI):
            last = v.bn_stats(self.stats[:, i, :], self.x[:, i, :])
        link(last)
        for i in range(NI):
            last = v.bn_aggr(self.mv[:, i, :], self.stats[:, i, :])
        link(last)
        v.tensor_scalar(self.var[:], self.mv[:, :, 1], LN_EPS, None, ALU.add).then_inc(self.var_ready, 1)
        dve.wait_ge(self.root_ready, 1)
        link(v.reciprocal(self.tmp[:], self.root[:]))
        link(v.tensor_tensor(self.tmp[:], self.tmp[:], self.var[:], ALU.mult))
        link(v.tensor_tensor(self.tmp[:], self.tmp[:], self.root[:], ALU.add))
        link(v.tensor_scalar(self.tmp[:], self.tmp[:], 0.5, None, ALU.mult))
        link(v.reciprocal(self.root[:], self.tmp[:]))
        for i in range(NI):
            v.tensor_scalar(self.xn[:, i, :], self.x[:, i, :], self.mv[:, i, 0:1], self.root[:, i:i + 1],
                            ALU.subtract, ALU.mult).then_inc(self.xn_ready, 1)
        dve.wait_ge(self.xn_ready, NI)



class Parts:

    def __init__(self, st, tag, dram, copies):
        self.nc, self.dram, self.copies = st.nc, dram, copies
        self.part = st.sb(f"{tag}_part", [P, 3, NI, D], BF16)
        self.rest = st.sb(f"{tag}_rest", [P, NI, D])
        self.hi_ready = st.sem(f"{tag}_hi_ready")
        self.rest_ready = st.sem(f"{tag}_rest_ready")
        self.mid_ready = st.sem(f"{tag}_mid_ready")
        self.lo_ready = st.sem(f"{tag}_lo_ready")
        self.stored = st.sem(f"{tag}_stored")

    HALF = NI // 2

    def scalar(self, act, src, src_ready):
        for n in range(2):
            t = slice(n * self.HALF, (n + 1) * self.HALF)
            if src_ready is not None:
                act.wait_ge(src_ready[0], src_ready[1])
            self.nc.scalar.activation(self.part[:, 0, t, :], src[:, t, :], ACT.Copy).then_inc(self.hi_ready, 1)
        for n in range(2):
            t = slice(n * self.HALF, (n + 1) * self.HALF)
            act.wait_ge(self.rest_ready, n + 1)
            self.nc.scalar.activation(self.part[:, 1, t, :], self.rest[:, t, :], ACT.Copy).then_inc(self.mid_ready, 1)

    def vector(self, dve, src):
        for n in range(2):
            t = slice(n * self.HALF, (n + 1) * self.HALF)
            dve.wait_ge(self.hi_ready, n + 1)
            self.nc.vector.tensor_tensor(self.rest[:, t, :], src[:, t, :], self.part[:, 0, t, :],
                                         ALU.subtract).then_inc(self.rest_ready, 1)
        for n in range(2):
            t = slice(n * self.HALF, (n + 1) * self.HALF)
            dve.wait_ge(self.mid_ready, n + 1)
            self.nc.vector.tensor_tensor(self.part[:, 2, t, :], self.rest[:, t, :], self.part[:, 1, t, :],
                                         ALU.subtract).then_inc(self.lo_ready, 1)

    def sync(self, sp):
        row = HEADS * CH * D
        n_blocks = len(self.copies)
        ready = [(self.hi_ready, 2), (self.mid_ready, 2), (self.lo_ready, 2)]
        count = 0
        for part in range(3):
            sp.wait_ge(*ready[part])
            for block in [n for n, p in enumerate(self.copies) if p == part]:
                for b2 in range(2):
                    dst = bass.AP(self.dram.tensor, self.dram.offset + (b2 * n_blocks + block) * row,
                                  [[D, HEADS * CH], [2 * n_blocks * row, NI], [1, D]])
                    sp.dma_start(dst, self.part[64 * b2:64 * b2 + 64, part, :, :]).then_inc(self.stored, 16)
                    count += 16
        sp.wait_ge(self.stored, count)


class HeadNorm:

    EPS2 = 1e-24

    def __init__(self, st, tag, src, out, same_head):
        self.nc, self.src, self.out, self.same_head = st.nc, src, out, same_head
        self.square = st.sb(f"{tag}_square", [P, NI, D])
        self.length = st.sb(f"{tag}_length", [P, NI, D])
        self.total = [st.ps(f"{tag}_total{n}") for n in range(4)]
        self.square_ready = st.sem(f"{tag}_square_ready")
        self.total_ready = st.sem(f"{tag}_total_ready")
        self.clamped = st.sem(f"{tag}_clamped")
        self.root_ready = st.sem(f"{tag}_root_ready")
        self.inverse_ready = st.sem(f"{tag}_inverse_ready")
        self.out_ready = st.sem(f"{tag}_out_ready")

    def vector(self, dve):
        v = self.nc.vector
        for n in range(4):
            t = slice(2 * n, 2 * n + 2)
            v.tensor_tensor(self.square[:, t, :], self.src[:, t, :], self.src[:, t, :],
                            ALU.mult).then_inc(self.square_ready, 1)
        for n in range(4):
            t = slice(2 * n, 2 * n + 2)
            dve.wait_ge(self.total_ready, n + 1)
            v.tensor_scalar(self.length[:, t, :], self.total[n][:].rearrange("p (i d) -> p i d", i=2),
                            self.EPS2, None, ALU.max).then_inc(self.clamped, 1)
        for n in range(4):
            t = slice(2 * n, 2 * n + 2)
            dve.wait_ge(self.root_ready, n + 1)
            v.reciprocal(self.square[:, t, :], self.length[:, t, :]).then_inc(self.inverse_ready, 1)
        for n in range(4):
            t = slice(2 * n, 2 * n + 2)
            dve.wait_ge(self.inverse_ready, n + 1)
            v.tensor_tensor(self.out[:, t, :], self.src[:, t, :], self.square[:, t, :],
                            ALU.mult).then_inc(self.out_ready, 1)

    def tensor(self, pe):
        for n in range(4):
            pe.wait_ge(self.square_ready, n + 1)
            self.nc.tensor.matmul(self.total[n][:], self.same_head[:],
                                  self.square[:, 2 * n:2 * n + 2, :].rearrange("p i d -> p (i d)"),
                                  start=True, stop=True).then_inc(self.total_ready, 1)

    def scalar(self, act):
        for n in range(4):
            t = slice(2 * n, 2 * n + 2)
            act.wait_ge(self.clamped, n + 1)
            self.nc.scalar.activation(self.length[:, t, :], self.length[:, t, :],
                                      ACT.Sqrt).then_inc(self.root_ready, 1)


K_COPIES = [0, 1, 2, 0, 1]
Q_COPIES = [0, 1, 2]
ROWS = 9 * CH
ROWS_MAX = ROWS + 3


def prepare(nc, m, a):
    with ExitStack() as ctx:
        st = Stage(nc, ctx, "prep")
        ctx_t = st.sb("ctx", [P, NI, D])
        ctx_n = st.sb("ctxn", [P, NI, D])
        loaded = st.sem("loaded")
        ctx_loaded = st.sem("ctx_loaded")
        plain = Parts(st, "kp", m.k_plain, K_COPIES)
        unit = Parts(st, "ku", m.k_unit, K_COPIES)
        hn = HeadNorm(st, "kn", ctx_t, ctx_n, m.same_head)
        with nc.Block() as block:
            @block.sync
            def _(sp):
                sp.dma_start(ctx_t[:], a["ctx"]).then_inc(ctx_loaded, 16)
                sp.dma_start(m.x[:], a["x"]).then_inc(loaded, 16)
                sp.dma_start(m.same_head[:], a["same_head"]).then_inc(loaded, 16)
                sp.dma_start(m.ident[:], a["ident"]).then_inc(loaded, 16)
                sp.dma_start(m.select[:], a["select"]).then_inc(loaded, 16)
                sp.dma_start(m.gamma[:], bass.AP(a["gamma"].tensor, 0, [[0, P], [1, 1]])).then_inc(loaded, 16)
                plain.sync(sp)
                unit.sync(sp)
                sp.wait_ge(loaded, 5 * 16)

            @block.scalar
            def _(act):
                act.wait_ge(ctx_loaded, 16)
                plain.scalar(act, ctx_t, None)
                hn.scalar(act)
                unit.scalar(act, ctx_n, (hn.out_ready, 4))

            @block.vector
            def _(dve):
                dve.wait_ge(ctx_loaded, 16)
                plain.vector(dve, ctx_t)
                hn.vector(dve)
                unit.vector(dve, ctx_n)
                dve.wait_ge(loaded, 5 * 16)
                nc.vector.tensor_copy(m.ident_bf[:], m.ident[:])

            @block.tensor
            def _(pe):
                pe.wait_ge(loaded, 5 * 16)
                hn.tensor(pe)


def attention(nc, m, a, layer):
    with_max = layer != 1
    rows = ROWS_MAX if with_max else ROWS
    scale = 5.0 if layer == 1 else CH ** -0.5
    k_dram = m.k_unit if layer == 1 else m.k_plain
    NB = 4
    PAIRS = HEADS // 2

    with ExitStack() as ctx:
        st = Stage(nc, ctx, f"q{layer}")
        norm = Norm(st, m.x, m.xn)
        parts = Parts(st, "q", m.q_parts, Q_COPIES)
        chain = st.sem("chain")
        hn = HeadNorm(st, "qn", m.xn, m.xn, m.same_head) if layer == 1 else None
        with nc.Block() as block:
            @block.sync
            def _(sp):
                parts.sync(sp)

            @block.scalar
            def _(act):
                norm.scalar(act)
                if hn:
                    hn.scalar(act)
                parts.scalar(act, m.xn, (hn.out_ready, 4) if hn else (norm.xn_ready, NI))

            @block.vector
            def _(dve):
                norm.vector(dve, Link(dve, chain))
                if hn:
                    hn.vector(dve)
                parts.vector(dve, m.xn)

            @block.tensor
            def _(pe):
                if hn:
                    hn.tensor(pe)

    with ExitStack() as ctx:
        st = Stage(nc, ctx, f"a{layer}")
        q = [st.sb(f"q{n}", [ROWS_MAX, HEADS, D], BF16) for n in range(NB)]
        k = [st.sb(f"k{n}", [ROWS_MAX, HEADS, D], BF16) for n in range(NB)]
        v = [st.sb(f"v{n}", [P, NK, HEADS, 32]) for n in range(NB)]
        probs = [st.sb(f"probs{n}", [P, HEADS, NK, D]) for n in range(2)]
        maxes = [st.sb(f"maxes{n}", [P, HEADS * NK]) for n in range(2)]
        neg = [st.sb(f"neg{n}", [HEADS * NK, 3, P], BF16) for n in range(2)]
        rest = st.sb("rest", [HEADS * NK, 2, P])
        out = [st.sb(f"out{n}", [P, D]) for n in range(2)]
        inv = st.sb("inv", [P, D])
        prod = st.sb("prod", [P, D])
        p_max = [st.ps(f"p_max{n}") for n in range(2)]
        p_sc = [st.ps(f"p_sc{n}", [P, 2, 512]) for n in range(2)]
        p_out = st.ps("p_out")
        p_misc = st.ps("p_misc")

        ones_set = st.sem("ones_set")
        loaded = [st.sem(f"loaded{n}") for n in range(NB)]
        neg_loaded = [st.sem(f"neg_loaded{n}") for n in range(2)]
        max_scored = st.sem("max_scored")
        max_taken = st.sem("max_taken")
        turned = st.sem("turned")
        neg_hi = st.sem("neg_hi")
        neg_r1 = st.sem("neg_r1")
        neg_mid = st.sem("neg_mid")
        neg_r2 = st.sem("neg_r2")
        neg_done = st.sem("neg_done")
        scored = st.sem("scored")
        exp_done = st.sem("exp_done")
        pv_done = st.sem("pv_done")
        out_copied = st.sem("out_copied")
        placed = st.sem("placed")
        added = st.sem("added")
        inv_done = st.sem("inv_done")
        prod_done = st.sem("prod_done")

        row = CH * HEADS * D
        LOOPS = B // NB - 1

        with nc.Block() as block:
            @block.sync
            def _(sp):
                def load(b, first):
                    n = slot(b, NB)
                    if isinstance(b, Step):
                        at = sp.snap(lin(b, 1, 0))
                        q_used, v_used = sp.snap(lin(b, PAIRS, -PAIRS * (NB - 1))), sp.snap(lin(b, 1, 2 - NB))
                    else:
                        at = b
                    qd = m.q_parts[bass.ds(at, 1), :, :]
                    kd = m.k_dram_of(layer)[bass.ds(at, 1), :, :]
                    qd = bass.AP(qd.tensor, qd.offset, [[0, 3], [HEADS * D, 3 * CH], [1, HEADS * D]])
                    kd = bass.AP(kd.tensor, kd.offset, [[row, 3], [HEADS * D, 3 * CH], [1, HEADS * D]])
                    if not first:
                        sp.wait_ge(scored, q_used)
                    sp.dma_start(q[n][0:ROWS, :, :], qd).then_inc(loaded[n], 16)
                    if first and with_max:
                        sp.wait_ge(ones_set, n + 1)
                    sp.dma_start(k[n][0:ROWS, :, :], kd).then_inc(loaded[n], 16)
                    if not first:
                        sp.wait_ge(pv_done, v_used)
                    sp.dma_start(v[n][:].rearrange("p k h c -> p (k h c)"),
                                 a["v"][bass.ds(at, 1), :, :].rearrange("b p c -> p (b c)")).then_inc(loaded[n], 16)

                def load_neg(b):
                    n = slot(b, NB)
                    wait(sp, neg_done, b, 1, 1)
                    for part in range(3):
                        sp.dma_start(q[n][ROWS + part:ROWS + part + 1, :, :].rearrange("a h (t m) -> a (h t) m", m=P),
                                     neg[slot(b, 2)][:, part, :]).then_inc(neg_loaded[slot(b, 2)], 16)

                for b in range(NB):
                    load(b, True)
                if with_max:
                    load_neg(0)
                with sp.Fori(0, LOOPS) as g:
                    for r in range(NB):
                        if with_max:
                            load_neg(Step(g, r + 1, NB))
                        load(Step(g, r + NB, NB), False)
                if with_max:
                    for b in range(B - NB + 1, B):
                        load_neg(b)

            @block.gpsimd
            def _(pool):
                if with_max:
                    for n in range(NB):
                        nc.gpsimd.memset(k[n][64:ROWS_MAX, :, :], 1.0).then_inc(ones_set, 1)

            @block.tensor
            def _(pe):
                def max_scores(b, h):
                    if h == 0:
                        n = slot(b, NB)
                        u = uses(b, NB)
                        pe.wait_ge(loaded[n], u * 48 + 48)
                    wait(pe, max_taken, b, HEADS, h - 1)
                    for t in range(NK):
                        last = nc.tensor.matmul(p_max[h % 2][:, t * D:(t + 1) * D],
                                                q[slot(b, NB)][0:ROWS, h, t * P:(t + 1) * P],
                                                k[slot(b, NB)][0:ROWS, h, :], start=True, stop=True)
                    last.then_inc(max_scored, 1)

                def turn_maxima(b):
                    wait(pe, max_taken, b, HEADS, HEADS)
                    wait(pe, neg_done, b, 1, 0)
                    if slot(b, 2) == 1 and (isinstance(b, Step) or b > 1):
                        pe.wait_ge(added, half(b) + 1)
                    nc.tensor.transpose(p_misc[0:HEADS * NK, 0:P], maxes[slot(b, 2)][:],
                                        m.ident[:]).then_inc(turned, 1)

                def scores(b, h):
                    if h == 0:
                        if with_max:
                            pe.wait_ge(neg_loaded[slot(b, 2)], uses(b, 2) * 48 + 48)
                        else:
                            pe.wait_ge(loaded[slot(b, NB)], uses(b, NB) * 48 + 48)
                    pair = h // 2
                    if h % 2 == 0:
                        wait(pe, exp_done, b, PAIRS, pair - 1)
                    for t in range(NK):
                        last = nc.tensor.matmul(p_sc[pair % 2][:, h % 2, t * D:(t + 1) * D],
                                                k[slot(b, NB)][0:rows, h, t * P:(t + 1) * P],
                                                q[slot(b, NB)][0:rows, h, :], start=True, stop=True)
                    if h % 2 == 1:
                        last.then_inc(scored, 1)

                def weigh(b):
                    wait(pe, exp_done, b, PAIRS, PAIRS)
                    wait(pe, out_copied, b, 1, 1)
                    for odd in range(2):
                        for t in range(NK):
                            for j in range(4):
                                h = 2 * j + odd
                                last = nc.tensor.matmul(p_out[32 * j:32 * j + 32, 0:D],
                                                        v[slot(b, NB)][:, t, h, :],
                                                        probs[slot(b, 2)][:, h, t, :],
                                                        start=(odd == 0 and t == 0),
                                                        stop=(odd == 1 and t == NK - 1))
                    last.then_inc(pv_done, 1)

                def place(b):
                    wait(pe, out_copied, b, 1, 2)
                    if with_max and (isinstance(b, Step) or b + 1 < B):
                        wait(pe, neg_done, b, 1, 2)
                    pe.wait_ge(added, half(b) + 1)
                    for b2 in range(2):
                        for part in range(2):
                            last = nc.tensor.matmul(p_misc[:, part * D:(part + 1) * D],
                                                    m.select[:, b2, part, :], out[b2][:],
                                                    start=(b2 == 0 and part == 0), stop=(b2 == 1 and part == 1),
                                                    skip_group_check=True)
                    last.then_inc(placed, 1)

                def step(b, nxt, before):
                    for h in range(2):
                        if nxt is not None:
                            max_scores(nxt, h)
                    if before is not None:
                        weigh(before)
                    for h in range(HEADS):
                        if h + 2 < HEADS and nxt is not None:
                            max_scores(nxt, h + 2)
                        scores(b, h)
                        if h == 2 and before is not None and slot(before, 2) == 1:
                            place(before)
                    if nxt is not None:
                        turn_maxima(nxt)

                pe.sem_inc(pv_done, 1)
                pe.sem_inc(placed, 1)
                if with_max:
                    for h in range(HEADS):
                        max_scores(0, h)
                    turn_maxima(0)
                nxt = (lambda b: b + 1) if with_max else (lambda b: None)
                step(0, nxt(0), None)
                with pe.Fori(0, LOOPS) as g:
                    for r in range(1, NB + 1):
                        step(Step(g, r, NB), nxt(Step(g, r, NB)), Step(g, r - 1, NB))
                for b in range(B - NB + 1, B):
                    step(b, nxt(b) if b + 1 < B else None, b - 1)
                weigh(B - 1)
                place(B - 1)

            @block.scalar
            def _(act):
                def exps(b):
                    for pair in range(PAIRS):
                        wait(act, scored, b, PAIRS, pair + 1)
                        if pair == 0:
                            wait(act, pv_done, b, 1, 0)
                        nc.scalar.activation(
                            probs[slot(b, 2)][:, 2 * pair:2 * pair + 2, :, :].rearrange("p h t d -> p h (t d)"),
                            p_sc[pair % 2][:], ACT.Exp, scale=scale).then_inc(exp_done, 1)
                        if pair == 0:
                            copy_out(b + -1)

                def copy_out(b):
                    if not isinstance(b, Step) and b < 0:
                        return
                    wait(act, pv_done, b, 1, 2)
                    act.wait_ge(placed, half(b) + 1)
                    nc.scalar.activation(out[slot(b, 2)][:], p_out[:, 0:D], ACT.Copy).then_inc(out_copied, 1)

                act.sem_inc(out_copied, 1)
                exps(0)
                with act.Fori(0, LOOPS) as g:
                    for r in range(1, NB + 1):
                        exps(Step(g, r, NB))
                for b in range(B - NB + 1, B):
                    exps(b)
                copy_out(B - 1)

            @block.vector
            def _(dve):
                def take_max(b, h):
                    wait(dve, max_scored, b, HEADS, h + 1)
                    if h == 0:
                        wait(dve, turned, b, 1, -1)
                    nc.vector.tensor_reduce(maxes[slot(b, 2)][:, NK * h:NK * h + NK],
                                            p_max[h % 2][:].rearrange("p (t d) -> p t d", t=NK),
                                            axis=AX.X, op=ALU.max, negate=True).then_inc(max_taken, 1)

                def split_max(b):
                    s = slot(b, 2)
                    wait(dve, turned, b, 1, 1)
                    if isinstance(b, Step) or b > 1:
                        dve.wait_ge(neg_loaded[s], uses(b, 2) * 48)
                    t = p_misc[0:HEADS * NK, 0:P]
                    nc.vector.tensor_copy(neg[s][:, 0, :], t).then_inc(neg_hi, 1)
                    wait(dve, neg_hi, b, 1, 1)
                    nc.vector.tensor_tensor(rest[:, 0, :], t, neg[s][:, 0, :], ALU.subtract).then_inc(neg_r1, 1)
                    wait(dve, neg_r1, b, 1, 1)
                    nc.vector.tensor_copy(neg[s][:, 1, :], rest[:, 0, :]).then_inc(neg_mid, 1)
                    wait(dve, neg_mid, b, 1, 1)
                    nc.vector.tensor_tensor(neg[s][:, 2, :], rest[:, 0, :], neg[s][:, 1, :],
                                            ALU.subtract).then_inc(neg_done, 1)

                def add_tile(b):
                    i = half(b)
                    dve.wait_ge(placed, i + 2)
                    nc.vector.reciprocal(inv[:], p_misc[:, D:2 * D]).then_inc(inv_done, 1)
                    dve.wait_ge(inv_done, i + 1)
                    dve.wait_ge(added, i + 1)
                    nc.vector.tensor_tensor(prod[:], p_misc[:, 0:D], inv[:], ALU.mult).then_inc(prod_done, 1)
                    dve.wait_ge(prod_done, i + 1)
                    x_i = m.x[:, bass.ds(i, 1), :].rearrange("p a d -> p (a d)")
                    gain = m.gamma[:, 0:1] if layer == 2 else 1.0
                    nc.vector.scalar_tensor_tensor(x_i, prod[:], gain, x_i, ALU.mult, ALU.add).then_inc(added, 1)

                def step(b, nxt, before):
                    for h in range(HEADS):
                        if nxt is not None:
                            take_max(nxt, h)
                        if h == 5 and before is not None and slot(before, 2) == 1:
                            add_tile(before)
                    if nxt is not None:
                        split_max(nxt)

                dve.sem_inc(added, 1)
                if with_max:
                    for h in range(HEADS):
                        take_max(0, h)
                    split_max(0)
                nxt = (lambda b: b + 1) if with_max else (lambda b: None)
                step(0, nxt(0), None)
                with dve.Fori(0, LOOPS) as g:
                    for r in range(1, NB + 1):
                        step(Step(g, r, NB), nxt(Step(g, r, NB)), Step(g, r - 1, NB))
                for b in range(B - NB + 1, B):
                    step(b, nxt(b) if b + 1 < B else None, b - 1)
                add_tile(B - 1)



class Mixture:

    def __init__(self, experts, top, hidden, shared):
        self.experts, self.top, self.hidden = experts, top, hidden
        self.shared_tiles = -(-shared // P)
        self.routed_tiles = experts * hidden // P
        self.tiles = self.shared_tiles + self.routed_tiles
        assert experts * hidden % P == 0 and self.tiles % 2 == 0

    def rows(self, t):
        if t < self.shared_tiles:
            return [(0, P, self.experts)]
        at = (t - self.shared_tiles) * P
        cuts = []
        for e in range(self.experts):
            lo, hi = max(at, e * self.hidden), min(at + P, (e + 1) * self.hidden)
            if lo < hi:
                cuts.append((lo - at, hi - at, e))
        return cuts


MIXTURES = {1: Mixture(8, 2, 176, 352), 2: Mixture(32, 8, 128, 256), 3: Mixture(16, 4, 176, 704)}
GROUPS, TOP_GROUPS, ROUTED_SCALE = 8, 4, 2.5
UP = NK * 2 * P


def rank_top(nc, link, padded, eight, picked, n, top):
    for i in range(NI):
        last = nc.vector.max(eight[:, i, :], padded[:, i, :])
    link(last)
    if top < 8:
        link(nc.vector.memset(eight[:, :, top:8], PAD))
    for i in range(NI):
        last = nc.vector.match_replace(picked[:, i, :], eight[:, i, :], padded[:, i, :], PAD)
    link(last)


def mixture(nc, m, a, layer):
    mx = MIXTURES[layer]
    E, E1, NT = mx.experts, mx.experts + 1, mx.tiles
    n_logits = E1 if layer == 3 else E
    pad = 8 if mx.top < 8 else 0
    with ExitStack() as outer:
        st = Stage(nc, outer, f"f{layer}")
        x_hi = st.sb("x_hi", [P, NK, T], F32R)
        x_lo = st.sb("x_lo", [P, NK, T], F32R)

        with ExitStack() as ctx:
            st = Stage(nc, ctx, f"r{layer}")
            norm = Norm(st, m.x, m.xn)
            x_t = st.sb("x_t", [P, NK, T])
            router = st.sb("router", [P, NK, n_logits])
            scores = st.sb("scores", [P, NI, E1])
            ranked = st.sb("ranked", [P, NI, E + pad])
            picked = st.sb("picked", [P, NI, E + pad])
            eight = st.sb("eight", [P, NI, 8])
            coef = st.sb("coef", [P, NI, E1])
            total = st.sb("total", [P, NI])
            coef_t = st.sb("coef_t", [E1, T])
            p_x = [[st.ps(f"p_x{k}{n}") for n in range(2)] for k in range(NK)]
            p_l = st.ps("p_l")
            p_c = [st.ps(f"p_c{n}") for n in range(2)]
            chain = st.sem("chain")
            loaded = st.sem("loaded")
            turned = st.sem("turned")
            x_t_ready = st.sem("x_t_ready")
            x_hi_ready = st.sem("x_hi_ready")
            logits = st.sem("logits")
            shifted = st.sem("shifted")
            scored = st.sem("scored")
            coef_ready = st.sem("coef_ready")
            coef_turned = st.sem("coef_turned")
            coef_t_ready = st.sem("coef_t_ready")
            stored = st.sem("stored")
            n_loads = 2 if layer == 2 else 1
            p_logits = p_l[:, 0:NI * n_logits].rearrange("p (i e) -> p i e", i=NI)
            if layer == 2:
                bias = st.sb("bias", [P, E])
                pair_hi = st.sb("pair_hi", [P, NI * GROUPS, 2])
                pair_lo = st.sb("pair_lo", [P, NI * GROUPS, 2])
                best = st.sb("best", [P, NI * GROUPS, 3])
                g_ranked = st.sb("g_ranked", [P, NI, GROUPS + 8])
                g_picked = st.sb("g_picked", [P, NI, GROUPS + 8])

            with nc.Block() as block:
                @block.sync
                def _(sp):
                    sp.dma_start(router[:], a[f"router{layer}"]).then_inc(loaded, 16)
                    if layer == 2:
                        src = a["router_bias"]
                        sp.dma_start(bias[:], bass.AP(src.tensor, src.offset, [[0, P], [1, E]])).then_inc(loaded, 16)
                    sp.wait_ge(coef_t_ready, 2)
                    sp.dma_start(m.coef[0:E1, :], coef_t[:]).then_inc(stored, 16)
                    sp.wait_ge(stored, 16)

                @block.tensor
                def _(pe):
                    for i in range(NI):
                        pe.wait_ge(norm.xn_ready, i + 1)
                        for k in range(NK):
                            last = nc.tensor.transpose(p_x[k][i // 4][:, i % 4 * P:i % 4 * P + P],
                                                       m.xn[:, i, k * P:(k + 1) * P], m.ident[:])
                        if i % 4 == 3:
                            last.then_inc(turned, 1)
                    pe.wait_ge(loaded, 16 * n_loads)
                    for i in range(NI):
                        pe.wait_ge(x_t_ready, 2 * (i // 4) + 2)
                        for k in range(NK):
                            last = nc.tensor.matmul(p_l[:, i * n_logits:(i + 1) * n_logits],
                                                    x_t[:, k, i * P:(i + 1) * P], router[:, k, :],
                                                    start=(k == 0), stop=(k == NK - 1))
                    last.then_inc(logits, 1)
                    pe.wait_ge(coef_ready, 1)
                    for i in range(NI):
                        last = nc.tensor.transpose(p_c[i // 4][0:E1, i % 4 * P:i % 4 * P + P], coef[:, i, :],
                                                   m.ident[:])
                        if i % 4 == 3:
                            last.then_inc(coef_turned, 1)

                @block.scalar
                def _(act):
                    norm.scalar(act)
                    for n in range(4):
                        act.wait_ge(x_t_ready, n + 1)
                        at = (slice(None), n % 2, slice(n // 2 * 512, n // 2 * 512 + 512))
                        nc.scalar.activation(x_hi[at], x_t[at], ACT.Copy).then_inc(x_hi_ready, 1)
                    if layer == 2:
                        act.wait_ge(logits, 1)
                        nc.scalar.activation(scores[:, :, 0:E], p_logits, ACT.Sigmoid).then_inc(scored, 1)
                    else:
                        act.wait_ge(shifted, 1)
                        nc.scalar.activation(scores[:, :, 0:E], scores[:, :, 0:E], ACT.Exp).then_inc(scored, 1)
                        if layer == 3:
                            nc.scalar.activation(coef[:, :, E:E1], coef[:, :, E:E1], ACT.Sigmoid).then_inc(scored, 1)
                    for n in range(2):
                        act.wait_ge(coef_turned, n + 1)
                        nc.scalar.activation(coef_t[:, n * 512:(n + 1) * 512], p_c[n][0:E1, :],
                                             ACT.Copy).then_inc(coef_t_ready, 1)

                @block.vector
                def _(dve):
                    v = nc.vector
                    link = Link(dve, chain)
                    norm.vector(dve, link)
                    if pad:
                        link(v.memset(ranked[:, :, E:E + pad], PAD))
                    for n in range(2):
                        dve.wait_ge(turned, n + 1)
                        for k in range(NK):
                            v.tensor_copy(x_t[:, k, n * 512:(n + 1) * 512], p_x[k][n][:]).then_inc(x_t_ready, 1)
                    for n in range(4):
                        at = (slice(None), n % 2, slice(n // 2 * 512, n // 2 * 512 + 512))
                        dve.wait_ge(x_hi_ready, n + 1)
                        last = v.tensor_tensor(x_lo[at], x_t[at], x_hi[at], ALU.subtract)
                    link(last)
                    sc = scores[:, :, 0:E]
                    row = list(total[:].ap[0])
                    total_b = bass.AP(total[:].tensor, total[:].offset, [row, [1, NI], [0, E]])
                    dve.wait_ge(logits, 1)
                    if layer != 2:
                        link(v.tensor_reduce(total[:], p_logits[:, :, 0:E], axis=AX.X, op=ALU.max))
                        if layer == 3:
                            link(v.tensor_copy(coef[:, :, E:E1], p_logits[:, :, E:E1]))
                        v.tensor_tensor(sc, p_logits[:, :, 0:E], total_b, ALU.subtract).then_inc(shifted, 1)
                        dve.wait_ge(scored, 2 if layer == 3 else 1)
                        link(v.tensor_reduce(total[:], sc, axis=AX.X, op=ALU.add))
                        link(v.reciprocal(total[:], total[:]))
                        link(v.tensor_tensor(sc, sc, total_b, ALU.mult))
                        link(v.tensor_copy(ranked[:, :, 0:E], sc))
                        rank_top(nc, link, ranked, eight, picked, E, mx.top)
                        link(v.tensor_scalar(picked[:, :, 0:E], picked[:, :, 0:E], PAD / 2, None, ALU.is_lt))
                        ins = v.tensor_tensor(coef[:, :, 0:E], picked[:, :, 0:E], sc, ALU.mult)
                    else:
                        dve.wait_ge(scored, 1)
                        dve.wait_ge(loaded, 16 * n_loads)
                        bias_b = bass.AP(bias[:].tensor, bias[:].offset, [list(bias[:].ap[0]), [0, NI], [1, E]])
                        link(v.tensor_tensor(ranked[:], sc, bias_b, ALU.add))
                        quad = ranked[:].rearrange("p i (g q) -> p (i g) q", q=4)
                        link(v.tensor_tensor(pair_hi[:], quad[:, :, 0:2], quad[:, :, 2:4], ALU.max))
                        link(v.tensor_tensor(pair_lo[:], quad[:, :, 0:2], quad[:, :, 2:4], ALU.min))
                        link(v.tensor_tensor(best[:, :, 0:1], pair_hi[:, :, 0:1], pair_hi[:, :, 1:2], ALU.max))
                        link(v.tensor_tensor(best[:, :, 1:2], pair_hi[:, :, 0:1], pair_hi[:, :, 1:2], ALU.min))
                        link(v.tensor_tensor(best[:, :, 2:3], pair_lo[:, :, 0:1], pair_lo[:, :, 1:2], ALU.max))
                        link(v.tensor_tensor(best[:, :, 1:2], best[:, :, 1:2], best[:, :, 2:3], ALU.max))
                        link(v.memset(g_ranked[:, :, GROUPS:], PAD))
                        link(v.tensor_tensor(g_ranked[:, :, 0:GROUPS],
                                             best[:, :, 0].rearrange("p (i g) -> p i g", i=NI),
                                             best[:, :, 1].rearrange("p (i g) -> p i g", i=NI), ALU.add))
                        rank_top(nc, link, g_ranked, eight, g_picked, GROUPS, TOP_GROUPS)
                        link(v.tensor_scalar(g_picked[:], g_picked[:], PAD / 2, None, ALU.is_lt))
                        for q in range(4):
                            part = ranked[:].rearrange("p i (g q) -> p i g q", q=4)[:, :, :, q]
                            last = v.tensor_tensor(part, part, g_picked[:, :, 0:GROUPS], ALU.mult)
                        link(last)
                        link(v.tensor_scalar(ranked[:], ranked[:], 0.0, None, ALU.add))
                        rank_top(nc, link, ranked, eight, picked, E, mx.top)
                        link(v.tensor_scalar(picked[:], picked[:], PAD / 2, None, ALU.is_lt))
                        link(v.tensor_tensor(picked[:], picked[:], sc, ALU.mult))
                        link(v.tensor_reduce(total[:], picked[:], axis=AX.X, op=ALU.add))
                        link(v.reciprocal(total[:], total[:]))
                        link(v.tensor_scalar(total[:], total[:], ROUTED_SCALE, None, ALU.mult))
                        ins = v.tensor_tensor(coef[:, :, 0:E], picked[:], total_b, ALU.mult)
                    if layer != 3:
                        link(ins)
                        ins = v.memset(coef[:, :, E:E1], 1.0)
                    ins.then_inc(coef_ready, 1)

        with ExitStack() as ctx:
            st = Stage(nc, ctx, f"e{layer}")
            w = [st.sb(f"w{n}", [P, UP + D]) for n in range(2)]
            up_hi = [st.sb(f"up_hi{n}", [P, UP], F32R) for n in range(2)]
            up_lo = [st.sb(f"up_lo{n}", [P, UP], F32R) for n in range(2)]
            down_hi = [st.sb(f"down_hi{n}", [P, D], F32R) for n in range(2)]
            down_lo = [st.sb(f"down_lo{n}", [P, D], F32R) for n in range(2)]
            coef = [st.sb(f"coef{n}", [P, T]) for n in range(2)]
            act_g = [st.sb(f"act_g{c}", [P, 512]) for c in range(2)]
            gated = [st.sb(f"gated{c}", [P, 512]) for c in range(2)]
            hid = [st.sb(f"hid{c}", [P, 512]) for c in range(2)]
            hid_hi = [[st.sb(f"hid_hi{n}{c}", [P, 512], F32R) for c in range(2)] for n in range(2)]
            hid_lo = [[st.sb(f"hid_lo{n}{c}", [P, 512], F32R) for c in range(2)] for n in range(2)]
            y_t = st.sb("y_t", [P, NK, T])
            p_g = [st.ps(f"p_g{c}") for c in range(2)]
            p_u = [st.ps(f"p_u{c}") for c in range(2)]
            p_y = [[st.ps(f"p_y{o}{c}") for c in range(2)] for o in range(NK)]
            w_loaded = [st.sem(f"w_loaded{n}") for n in range(2)]
            coef_loaded = [st.sem(f"coef_loaded{n}") for n in range(2)]
            up_hi_ready = st.sem("up_hi_ready")
            up_lo_ready = st.sem("up_lo_ready")
            down_hi_ready = st.sem("down_hi_ready")
            down_lo_ready = st.sem("down_lo_ready")
            g_done = st.sem("g_done")
            u_done = st.sem("u_done")
            silu_done = st.sem("silu_done")
            gated_done = st.sem("gated_done")
            hid_done = st.sem("hid_done")
            hid_hi_done = st.sem("hid_hi_done")
            hid_lo_done = st.sem("hid_lo_done")
            down_done = st.sem("down_done")
            y_copied = st.sem("y_copied")
            y_turned = st.sem("y_turned")
            turn_in = [p_g[0], p_g[1], p_u[0], p_u[1]]
            n_coef = [len(mx.rows(t)) for t in range(NT)]
            ROUNDS = NT // 2 - 1

            with nc.Block() as block:
                @block.sync
                def _(sp):
                    coef_count = [0, 0]
                    for t in range(NT):
                        wait(sp, down_lo_ready, t, 1, -1)
                        sp.dma_start(w[t % 2][:], a[f"w{layer}"][t, :, :]).then_inc(w_loaded[t % 2], 16)
                        wait(sp, hid_done, t, 2, -2)
                        for p0, p1, e in mx.rows(t):
                            src = m.coef[e:e + 1, :]
                            sp.dma_start(coef[t % 2][p0:p1, :],
                                         bass.AP(src.tensor, src.offset, [[0, p1 - p0], [1, T]])
                                         ).then_inc(coef_loaded[t % 2], 16)
                        if n_coef[t] == 1:
                            sp.sem_inc(coef_loaded[t % 2], 16)

                @block.tensor
                def _(pe):
                    def gate_up(t):
                        n = slot(t, 2)
                        for c in range(2):
                            tok = slice(c * 512, (c + 1) * 512)
                            wait(pe, gated_done, t, 2, c - 1)
                            if c == 0:
                                wait(pe, up_hi_ready, t, 1, 1)
                                wait(pe, up_lo_ready, t, 1, 1)
                            for s, (p, done) in enumerate(((p_g[c], g_done), (p_u[c], u_done))):
                                passes = [(w_, x_, k) for w_, x_ in ((up_hi, x_hi), (up_hi, x_lo), (up_lo, x_hi))
                                          for k in range(NK)]
                                for i, (w_, x_, k) in enumerate(passes):
                                    last = nc.tensor.matmul(p[:], w_[n][:, (2 * k + s) * P:(2 * k + s + 1) * P],
                                                            x_[:, k, tok], start=(i == 0), stop=(i == len(passes) - 1))
                                last.then_inc(done, 1)

                    def down(t, start=False, stop=False):
                        n = slot(t, 2)
                        for c in range(2):
                            wait(pe, hid_lo_done, t, 2, c + 1)
                            if c == 0:
                                wait(pe, down_lo_ready, t, 1, 1)
                            for o in range(NK):
                                passes = [(down_hi, hid_hi), (down_hi, hid_lo), (down_lo, hid_hi)]
                                for i, (w_, h_) in enumerate(passes):
                                    last = nc.tensor.matmul(p_y[o][c][:], w_[n][:, o * P:(o + 1) * P], h_[n][c][:],
                                                            start=start and i == 0, stop=stop and i == len(passes) - 1,
                                                            skip_group_check=True)
                            last.then_inc(down_done, 1)

                    pe.sem_inc(down_done, 1)
                    gate_up(0)
                    gate_up(1)
                    down(0, start=True)
                    with pe.Fori(0, ROUNDS) as g:
                        for r in range(2):
                            gate_up(Step(g, r + 2, 2))
                            down(Step(g, r + 1, 2))
                    down(NT - 1, stop=True)
                    for n in range(4):
                        pe.wait_ge(y_copied, 4 if n >= 2 else 2)
                        for i in (2 * n, 2 * n + 1):
                            for o in range(NK):
                                last = nc.tensor.transpose(turn_in[n][:, i % 2 * D + o * P:i % 2 * D + (o + 1) * P],
                                                           y_t[:, o, i * P:(i + 1) * P], m.ident[:])
                        last.then_inc(y_turned, 1)

                @block.scalar
                def _(act):
                    def split_up(t):
                        act.wait_ge(w_loaded[slot(t, 2)], uses(t, 2) * 16 + 16)
                        nc.scalar.activation(up_hi[slot(t, 2)][:], w[slot(t, 2)][:, 0:UP],
                                             ACT.Copy).then_inc(up_hi_ready, 1)

                    def split_down(t):
                        wait(act, down_done, t, 2, -1)
                        nc.scalar.activation(down_hi[slot(t, 2)][:], w[slot(t, 2)][:, UP:UP + D],
                                             ACT.Copy).then_inc(down_hi_ready, 1)

                    def silu(t, c):
                        wait(act, g_done, t, 2, c + 1)
                        nc.scalar.activation(act_g[c][:], p_g[c][:], ACT.Silu).then_inc(silu_done, 1)

                    def high(t, c):
                        wait(act, hid_done, t, 2, c + 1)
                        nc.scalar.activation(hid_hi[slot(t, 2)][c][:], hid[c][:], ACT.Copy).then_inc(hid_hi_done, 1)

                    def tile(t, more=True):
                        silu(t, 0)
                        if more:
                            split_up(t + 1)
                        silu(t, 1)
                        high(t, 0)
                        high(t, 1)
                        if more:
                            split_down(t + 1)

                    split_up(0)
                    split_down(0)
                    with act.Fori(0, ROUNDS) as g:
                        for r in range(2):
                            tile(Step(g, r, 2))
                    tile(NT - 2)
                    tile(NT - 1, more=False)
                    act.wait_ge(down_done, 2 * NT)
                    for o in range(NK):
                        nc.scalar.activation(y_t[:, o, 0:512], p_y[o][0][:], ACT.Copy).then_inc(y_copied, 1)

                @block.gpsimd
                def _(pool):
                    def split(t, hi, lo, cols, hi_ready, lo_ready):
                        wait(pool, hi_ready, t, 1, 1)
                        nc.gpsimd.tensor_tensor(lo[slot(t, 2)][:], w[slot(t, 2)][:, cols], hi[slot(t, 2)][:],
                                                ALU.subtract).then_inc(lo_ready, 1)

                    def split_up(t):
                        split(t, up_hi, up_lo, slice(0, UP), up_hi_ready, up_lo_ready)

                    def split_down(t):
                        split(t, down_hi, down_lo, slice(UP, UP + D), down_hi_ready, down_lo_ready)

                    def weigh(t, c):
                        if c == 0:
                            pool.wait_ge(coef_loaded[slot(t, 2)], uses(t, 2) * 32 + 32)
                        wait(pool, gated_done, t, 2, c + 1)
                        nc.gpsimd.tensor_tensor(hid[c][:], gated[c][:], coef[slot(t, 2)][:, c * 512:(c + 1) * 512],
                                                ALU.mult).then_inc(hid_done, 1)

                    def tile(t, more=True):
                        weigh(t, 0)
                        if more:
                            split_up(t + 1)
                        weigh(t, 1)
                        if more:
                            split_down(t + 1)

                    split_up(0)
                    split_down(0)
                    with pool.Fori(0, ROUNDS) as g:
                        for r in range(2):
                            tile(Step(g, r, 2))
                    tile(NT - 2)
                    tile(NT - 1, more=False)

                @block.vector
                def _(dve):
                    def gate(t, c):
                        wait(dve, silu_done, t, 2, c + 1)
                        wait(dve, u_done, t, 2, c + 1)
                        nc.vector.tensor_tensor(gated[c][:], act_g[c][:], p_u[c][:], ALU.mult).then_inc(gated_done, 1)

                    def low(t, c):
                        wait(dve, hid_hi_done, t, 2, c + 1)
                        nc.vector.tensor_tensor(hid_lo[slot(t, 2)][c][:], hid[c][:], hid_hi[slot(t, 2)][c][:],
                                                ALU.subtract).then_inc(hid_lo_done, 1)

                    def tile(t):
                        gate(t, 0)
                        gate(t, 1)
                        low(t, 0)
                        low(t, 1)

                    with dve.Fori(0, ROUNDS + 1) as g:
                        for r in range(2):
                            tile(Step(g, r, 2))
                    dve.wait_ge(down_done, 2 * NT + 1)
                    dve.wait_ge(y_copied, 2)
                    for o in range(NK):
                        nc.vector.tensor_copy(y_t[:, o, 512:1024], p_y[o][1][:]).then_inc(y_copied, 1)
                    for n in range(4):
                        dve.wait_ge(y_turned, n + 1)
                        nc.vector.tensor_tensor(m.x[:, 2 * n:2 * n + 2, :], m.x[:, 2 * n:2 * n + 2, :],
                                                turn_in[n][:].rearrange("p (i d) -> p i d", i=2),
                                                ALU.add)



def turn_and_multiply(nc, st, src_bf, m, weights, n_out, emit):
    nk = src_bf.shape[2] // P
    turned_sb = [st.sb(f"turned{n}", [P, nk, P], BF16) for n in range(2)]
    p_t = [st.ctx.enter_context(nc.psum_tensor(f"{st.name}_p_t{n}", [P, nk, P], BF16)) for n in range(2)]
    p_y = [st.ps(f"p_y{n}") for n in range(2)]
    turned = st.sem("turned")
    copied = st.sem("copied")
    product = st.sem("product")
    emitted = st.sem("emitted")

    def tensor(pe, ready):
        def turn(i):
            pe.wait_ge(*ready(i))
            if i >= 2:
                pe.wait_ge(copied, i - 1)
            for k in range(nk):
                last = nc.tensor.transpose(p_t[i % 2][:, k, :], src_bf[:, i, k * P:(k + 1) * P], m.ident_bf[:])
            last.then_inc(turned, 1)

        turn(0)
        for i in range(NI):
            if i + 1 < NI:
                turn(i + 1)
            pe.wait_ge(copied, i + 1)
            if i >= 2:
                pe.wait_ge(emitted, i - 1)
            for k in range(nk):
                last = nc.tensor.matmul(p_y[i % 2][:, 0:n_out], turned_sb[i % 2][:, k, :], weights[:, k, :],
                                        start=(k == 0), stop=(k == nk - 1))
            last.then_inc(product, 1)

    def scalar(act):
        for i in range(NI):
            act.wait_ge(turned, i + 1)
            if i >= 2:
                act.wait_ge(product, i - 1)
            nc.scalar.activation(turned_sb[i % 2][:], p_t[i % 2][:], ACT.Copy).then_inc(copied, 1)

    def vector(dve):
        for i in range(NI):
            dve.wait_ge(product, i + 1)
            emit(i, p_y[i % 2][:, 0:n_out]).then_inc(emitted, 1)

    return tensor, scalar, vector


def round_clip(nc, link, out, tmp, src, factor, low, high, last_inc=None):
    v = nc.vector
    link(v.tensor_scalar(tmp, src, factor, low, ALU.mult, ALU.max))
    link(v.tensor_scalar(tmp, tmp, high, ROUND, ALU.min, ALU.add))
    ins = v.tensor_scalar(out, tmp, -ROUND, None, ALU.add)
    if last_inc is None:
        link(ins)
    else:
        ins.then_inc(last_inc, 1)


INNER = 4 * D
NH = INNER // P


def ternary_feed_forward(nc, m, a):
    with ExitStack() as outer:
        st0 = Stage(nc, outer, "b0")
        w1 = st0.sb("w1", [P, NK, INNER], BF16)
        w2 = st0.sb("w2", [P, NH, D], BF16)
        w_mean = st0.sb("w_mean", [P, 2])
        xq = st0.sb("xq", [P, NI, D], BF16)
        deq = st0.sb("deq", [P, NI])
        h = st0.sb("h", [P, NI, INNER])
        hq = st0.sb("hq", [P, NI, INNER], BF16)
        square_sum = st0.sb("square_sum", [P, NI])
        largest = st0.sb("largest", [P, NI])
        root = st0.sb("root", [P, NI])
        tmp_v = st0.sb("tmp_v", [P, NI])
        factor = st0.sb("factor", [P, NI])

        def activation_scale(link, root_in, root_ready, dve, width, w):
            v = nc.vector
            v.tensor_scalar(root_in[:], square_sum[:], 1e-24, None, ALU.max).then_inc(root_ready[0], 1)
            dve.wait_ge(root_ready[1], 1)
            link(v.reciprocal(tmp_v[:], root[:]))
            link(v.tensor_tensor(tmp_v[:], tmp_v[:], root_in[:], ALU.mult))
            link(v.tensor_tensor(tmp_v[:], tmp_v[:], root[:], ALU.add))
            link(v.tensor_scalar(tmp_v[:], tmp_v[:], 0.5, None, ALU.mult))
            link(v.reciprocal(tmp_v[:], tmp_v[:]))
            link(v.tensor_scalar(tmp_v[:], tmp_v[:], float(width) ** 0.5, None, ALU.mult))
            link(v.tensor_tensor(largest[:], largest[:], tmp_v[:], ALU.mult))
            link(v.tensor_scalar(largest[:], largest[:], 1e-5, None, ALU.max))
            link(v.reciprocal(factor[:], largest[:]))
            link(v.tensor_scalar(factor[:], factor[:], 127.0, None, ALU.mult))
            link(v.tensor_tensor(factor[:], factor[:], tmp_v[:], ALU.mult))
            link(v.tensor_scalar(deq[:], largest[:], 1.0 / 127.0, w_mean[:, w:w + 1], ALU.mult, ALU.mult))

        with ExitStack() as ctx:
            st = Stage(nc, ctx, "b1")
            raw = [st.sb(f"raw{n}", [P, 2 * INNER]) for n in range(2)]
            sums = st.sb("sums", [P, 2])
            ones = st.sb("ones", [P, P])
            tmp = st.sb("tmp", [P, 2 * INNER])
            junk = st.sb("junk", [P, INNER])
            turned_sb = [st.sb(f"turned{n}", [P, NK, P], BF16) for n in range(2)]
            norm = Norm(st, m.x, m.xn)
            p_mean = st.ps("p_mean")
            p_t = [ctx.enter_context(nc.psum_tensor(f"b1_p_t{n}", [P, NK, P], BF16)) for n in range(2)]
            p_h = [st.ps(f"p_h{n}", [P, 2, 512]) for n in range(2)]
            root_in = st.sb("root_in", [P, NI])
            chain = st.sem("chain")
            loaded = [st.sem(f"loaded{n}") for n in range(2)]
            ones_set = st.sem("ones_set")
            summed = st.sem("summed")
            meaned = st.sem("meaned")
            squared = st.sem("squared")
            to_root = (st.sem("root_in_ready"), st.sem("root_ready"))
            xq_ready = st.sem("xq_ready")
            turned = st.sem("turned")
            copied = st.sem("copied")
            product = st.sem("product")
            gelu1 = st.sem("gelu1")
            gelu2 = st.sem("gelu2")
            h_squared = st.sem("h_squared")
            with nc.Block() as block:
                @block.sync
                def _(sp):
                    for n in range(2):
                        sp.dma_start(raw[n][:], a[f"ternary{n}"]).then_inc(loaded[n], 16)

                @block.gpsimd
                def _(pool):
                    nc.gpsimd.memset(ones[:], 1.0).then_inc(ones_set, 1)

                @block.tensor
                def _(pe):
                    pe.wait_ge(ones_set, 1)
                    pe.wait_ge(summed, 1)
                    nc.tensor.matmul(p_mean[:, 0:2], ones[:], sums[:], start=True, stop=True).then_inc(meaned, 1)
                    for i in range(NI):
                        pe.wait_ge(xq_ready, i + 1)
                        if i >= 2:
                            pe.wait_ge(copied, i - 1)
                        for k in range(NK):
                            last = nc.tensor.transpose(p_t[i % 2][:, k, :], xq[:, i, k * P:(k + 1) * P], m.ident_bf[:])
                        last.then_inc(turned, 1)
                        pe.wait_ge(copied, i + 1)
                        if i >= 2:
                            pe.wait_ge(gelu1, i - 1)
                        for c in range(2):
                            for k in range(NK):
                                last = nc.tensor.matmul(p_h[i % 2][:, c, :], turned_sb[i % 2][:, k, :],
                                                        w1[:, k, c * 512:(c + 1) * 512],
                                                        start=(k == 0), stop=(k == NK - 1))
                        last.then_inc(product, 1)

                @block.scalar
                def _(act):
                    norm.scalar(act)
                    for i in range(NI):
                        act.wait_ge(norm.xn_ready, i + 1)
                        nc.scalar.activation(junk[:, 0:D], m.xn[:, i, :], ACT.Square,
                                             accum_out=square_sum[:, i:i + 1]).then_inc(squared, 1)
                        act.wait_ge(squared, i + 1)
                    act.wait_ge(to_root[0], 1)
                    nc.scalar.activation(root[:], root_in[:], ACT.Sqrt).then_inc(to_root[1], 1)

                    def first(i):
                        act.wait_ge(product, i + 1)
                        nc.scalar.activation(h[:, i, :].rearrange("p (c n) -> p c n", c=2), p_h[i % 2][:], ACT.Gelu,
                                             scale=deq[:, i:i + 1]).then_inc(gelu1, 1)

                    def second(i):
                        act.wait_ge(gelu1, i + 1)
                        nc.scalar.activation(h[:, i, :], h[:, i, :], ACT.Gelu).then_inc(gelu2, 1)

                    def square(i):
                        act.wait_ge(gelu2, i + 1)
                        act.wait_ge(h_squared, i)
                        nc.scalar.activation(junk[:], h[:, i, :], ACT.Square,
                                             accum_out=square_sum[:, i:i + 1]).then_inc(h_squared, 1)

                    for i in range(NI + 1):
                        if i < NI:
                            first(i)
                        if i >= 1:
                            if i >= 2:
                                square(i - 2)
                            second(i - 1)
                    square(NI - 1)

                @block.vector
                def _(dve):
                    v = nc.vector
                    link = Link(dve, chain)
                    for n in range(2):
                        dve.wait_ge(loaded[n], 16)
                        last = v.tensor_reduce(sums[:, n:n + 1], raw[n][:], axis=AX.X, op=ALU.add,
                                               apply_absolute_value=True)
                    last.then_inc(summed, 1)
                    norm.vector(dve, link)
                    dve.wait_ge(meaned, 1)
                    link(v.tensor_scalar(w_mean[:], p_mean[:, 0:2], 1.0 / (D * INNER), 1e-5, ALU.mult, ALU.max))
                    link(v.reciprocal(sums[:], w_mean[:]))
                    for n, w in enumerate((w1, w2)):
                        round_clip(nc, link, w[:].rearrange("p k n -> p (k n)"), tmp[:], raw[n][:],
                                   sums[:, n:n + 1], -1.0, 1.0)
                    link(v.tensor_reduce(largest[:], m.xn[:], axis=AX.X, op=ALU.max, apply_absolute_value=True))
                    dve.wait_ge(squared, NI)
                    activation_scale(link, root_in, to_root, dve, D, 0)
                    for i in range(NI):
                        round_clip(nc, link, xq[:, i, :], tmp[:, 0:D], m.xn[:, i, :], factor[:, i:i + 1],
                                   -128.0, 127.0, xq_ready)
                        dve.wait_ge(turned, i + 1)
                        if i >= 2:
                            dve.wait_ge(product, i - 1)
                        v.tensor_copy(turned_sb[i % 2][:], p_t[i % 2][:]).then_inc(copied, 1)
                    for i in range(NI):
                        dve.wait_ge(gelu2, i + 1)
                        last = v.tensor_reduce(largest[:, i:i + 1], h[:, i, :], axis=AX.X, op=ALU.max,
                                               apply_absolute_value=True)
                    link(last)

        with ExitStack() as ctx:
            st = Stage(nc, ctx, "b2")
            tmp = [st.sb(f"tmp{n}", [P, INNER]) for n in range(2)]
            root_in = st.sb("root_in", [P, NI])
            chain = st.sem("chain")
            to_root = (st.sem("root_in_ready"), st.sem("root_ready"))
            hq_ready = st.sem("hq_ready")

            def emit(i, y):
                return nc.vector.scalar_tensor_tensor(m.x[:, i, :], y, deq[:, i:i + 1], m.x[:, i, :],
                                                      ALU.mult, ALU.add)

            tensor, scalar, vector = turn_and_multiply(nc, st, hq, m, w2, D, emit)
            with nc.Block() as block:
                @block.tensor
                def _(pe):
                    tensor(pe, lambda i: (hq_ready, i + 1))

                @block.scalar
                def _(act):
                    act.wait_ge(to_root[0], 1)
                    nc.scalar.activation(root[:], root_in[:], ACT.Sqrt).then_inc(to_root[1], 1)
                    scalar(act)

                @block.vector
                def _(dve):
                    link = Link(dve, chain)
                    activation_scale(link, root_in, to_root, dve, INNER, 1)
                    for i in range(NI):
                        round_clip(nc, link, hq[:, i, :], tmp[i % 2][:], h[:, i, :], factor[:, i:i + 1],
                                   -128.0, 127.0, hq_ready)
                    vector(dve)



XH, XC, L = 16, 16, 64
PAIR = 2 * XC + 2


def token_scale(nc, link, largest, deq, factor):
    link(nc.vector.tensor_scalar(deq, largest, 1.0 / 127.0, 1e-8, ALU.mult, ALU.max))
    link(nc.vector.reciprocal(factor, deq))


def quantized_attention(nc, m, a):
    with ExitStack() as outer:
        st0 = Stage(nc, outer, "c0")
        w_q = [st0.sb(f"w_q{n}", [P, NK, D], BF16) for n in range(2)]
        w_s = [st0.sb(f"w_s{n}", [P, D]) for n in range(2)]
        bias = [st0.sb(f"bias{n}", [P, D]) for n in range(3)]
        mask = st0.sb("mask", [P, NI, L])
        k_heads = st0.sb("k_heads", [P, NK, B, 8, L])
        v_pairs = st0.sb("v_pairs", [P, B, 8, PAIR])
        o = st0.sb("o", [P, NI, D])
        xq = st0.sb("xq", [P, NI, D], BF16)
        largest = st0.sb("largest", [P, NI])
        deq = st0.sb("deq", [P, NI])
        factor = st0.sb("factor", [P, NI])

        with ExitStack() as ctx:
            st = Stage(nc, ctx, "c1")
            raw = [st.sb(f"raw{n}", [P, NK, D]) for n in range(2)]
            whole = [st.sb(f"whole{n}", [P, NK, D], BF16) for n in range(2)]
            tmp = st.sb("tmp", [P, NK, D])
            w_largest = st.sb("w_largest", [P, 2, NK])
            w_deq = st.sb("w_deq", [P, 2, NK])
            w_factor = st.sb("w_factor", [P, 2, NK])
            cond = st.sb("cond", [P, NK, T])
            wk = st.sb("wk", [P, NK, D])
            wv = st.sb("wv", [P, NK, D])
            bk = st.sb("bk", [P, NK])
            own = st.sb("own", [P, 8])
            bk_own = st.sb("bk_own", [P, NK, 8])
            p_w = [ctx.enter_context(nc.psum_tensor(f"c1_p_w{n}", [P, NK, D], BF16)) for n in range(2)]
            p_k = [st.ps(f"p_k{n}") for n in range(4)]
            p_v = [st.ps(f"p_v{n}") for n in range(2)]
            chain = st.sem("chain")
            w_loaded = st.sem("w_loaded")
            c_loaded = st.sem("c_loaded")
            b_loaded = st.sem("b_loaded")
            whole_ready = st.sem("whole_ready")
            turned = st.sem("turned")
            scale_stored = st.sem("scale_stored")
            scale_ready = st.sem("scale_ready")
            k_done = st.sem("k_done")
            v_done = st.sem("v_done")
            v_copied = st.sem("v_copied")
            zeroed = st.sem("zeroed")
            bk_ready = st.sem("bk_ready")
            with nc.Block() as block:
                @block.sync
                def _(sp):
                    for n in range(2):
                        sp.dma_start(raw[n][:], a[("xq_w", "xo_w")[n]]).then_inc(w_loaded, 16)
                    for t, name in ((cond, "cond"), (wk, "xk_w"), (wv, "xv_w")):
                        sp.dma_start(t[:], a[name]).then_inc(c_loaded, 16)
                    for t, name in ((bk, "xk_b"), (own, "own"), (mask, "mask")):
                        sp.dma_start(t[:], a[name]).then_inc(b_loaded, 16)
                    for n, name in enumerate(("xq_b", "xo_b", "xv_b")):
                        src = a[name]
                        sp.dma_start(bias[n][:], bass.AP(src.tensor, src.offset, [[0, P], [1, D]])
                                     ).then_inc(b_loaded, 16)
                    sp.wait_ge(scale_ready, 1)
                    with nc.allow_non_contiguous_dma(reason="512 scales, once"):
                        for n in range(2):
                            for k in range(NK):
                                dst = m.scales[n:n + 1, k * P:(k + 1) * P]
                                sp.dma_start(bass.AP(dst.tensor, dst.offset, [[1, P], [1, 1]]),
                                             w_deq[:, n, k:k + 1]).then_inc(scale_stored, 16)
                    sp.wait_ge(scale_stored, 4 * 16)
                    for n in range(2):
                        src = m.scales[n:n + 1, :]
                        sp.dma_start(w_s[n][:], bass.AP(src.tensor, src.offset, [[0, P], [1, D]])
                                     ).then_inc(scale_stored, 16)
                    sp.wait_ge(scale_stored, 6 * 16)

                @block.gpsimd
                def _(pool):
                    nc.gpsimd.memset(v_pairs[:], 0.0).then_inc(zeroed, 1)
                    pool.wait_ge(zeroed, 1)
                    for odd in range(2):
                        nc.gpsimd.memset(v_pairs[64 * odd:64 * odd + 64, :, :, 2 * XC + odd], 1.0).then_inc(zeroed, 1)

                @block.tensor
                def _(pe):
                    pe.wait_ge(c_loaded, 3 * 16)
                    for k2 in range(NK):
                        for n in range(2):
                            for k in range(NK):
                                last = nc.tensor.matmul(p_k[2 * k2 + n][:], wk[:, k, k2 * P:(k2 + 1) * P],
                                                        cond[:, k, n * 512:(n + 1) * 512],
                                                        start=(k == 0), stop=(k == NK - 1))
                            last.then_inc(k_done, 1)
                    for pair in range(B // 2):
                        if pair >= 2:
                            pe.wait_ge(v_copied, 2 * (pair - 1))
                        for b2 in range(2):
                            b = 2 * pair + b2
                            for k in range(NK):
                                for odd in range(2):
                                    last = nc.tensor.matmul(p_v[pair % 2][64 * odd:64 * odd + 64, b2 * D:(b2 + 1) * D],
                                                            cond[:, k, b * L:(b + 1) * L], wv[:, k, :],
                                                            start=(k == 0), stop=(k == NK - 1))
                        last.then_inc(v_done, 1)
                    for n in range(2):
                        pe.wait_ge(whole_ready, n + 1)
                        for o2 in range(NK):
                            for k in range(NK):
                                last = nc.tensor.transpose(p_w[n][:, k, o2 * P:(o2 + 1) * P],
                                                           whole[n][:, o2, k * P:(k + 1) * P], m.ident_bf[:])
                        last.then_inc(turned, 1)

                @block.scalar
                def _(act):
                    act.wait_ge(b_loaded, 6 * 16)
                    act.wait_ge(bk_ready, 1)
                    for n4 in range(2 * NK):
                        k2, n = n4 // 2, n4 % 2
                        act.wait_ge(k_done, n4 + 1)
                        for h in range(8):
                            nc.scalar.activation(k_heads[:, k2, 8 * n:8 * n + 8, h, :],
                                                 p_k[n4][:].rearrange("p (b l) -> p b l", l=L), ACT.Identity,
                                                 bias=bk_own[:, k2, h:h + 1], scale=own[:, h:h + 1])

                @block.vector
                def _(dve):
                    v = nc.vector
                    link = Link(dve, chain)
                    dve.wait_ge(b_loaded, 6 * 16)
                    for k in range(NK):
                        last = v.tensor_scalar(bk_own[:, k, :], own[:], bk[:, k:k + 1], None, ALU.mult)
                    last.then_inc(bk_ready, 1)
                    dve.wait_ge(w_loaded, 32)
                    for n in range(2):
                        last = v.tensor_reduce(w_largest[:, n, :], raw[n][:], axis=AX.X, op=ALU.max,
                                               apply_absolute_value=True)
                    link(last)
                    link(v.tensor_scalar(w_deq[:], w_largest[:], 1.0 / 127.0, 1e-8, ALU.mult, ALU.max))
                    v.reciprocal(w_factor[:], w_deq[:]).then_inc(scale_ready, 1)
                    dve.wait_ge(scale_ready, 1)
                    for n in range(2):
                        for k in range(NK):
                            inc = whole_ready if k == NK - 1 else None
                            round_clip(nc, link, whole[n][:, k, :], tmp[:, k, :], raw[n][:, k, :],
                                       w_factor[:, n, k:k + 1], -127.0, 127.0, inc)
                    dve.wait_ge(zeroed, 3)
                    for pair in range(B // 2):
                        dve.wait_ge(v_done, pair + 1)
                        for odd in range(2):
                            part = slice(64 * odd, 64 * odd + 64)
                            src = p_v[pair % 2][part, :].rearrange("p (b q s c) -> p b q s c", b=2, s=2, c=XC)
                            b_v = bias[2][part, :].rearrange("p (q s c) -> p q s c", s=2, c=XC)
                            for b2 in range(2):
                                last = v.tensor_tensor(v_pairs[part, 2 * pair + b2, :, XC * odd:XC * odd + XC],
                                                       src[:, b2, :, odd, :], b_v[:, :, odd, :], ALU.add)
                            last.then_inc(v_copied, 1)
                    for n in range(2):
                        dve.wait_ge(turned, n + 1)
                        v.tensor_copy(w_q[n][:], p_w[n][:])

        with ExitStack() as ctx:
            st = Stage(nc, ctx, "c2")
            norm = Norm(st, m.x, m.xn)
            tmp = st.sb("tmp", [P, NI, D])
            chain = st.sem("chain")
            xq_ready = st.sem("xq_ready")
            scaled = st.sem("scaled")

            def emit(i, y):
                nc.vector.scalar_tensor_tensor(m.xn[:, i, :], y, deq[:, i:i + 1], w_s[0][:],
                                               ALU.mult, ALU.mult).then_inc(scaled, 1)
                nc.vector.wait_ge(scaled, i + 1)
                return nc.vector.tensor_tensor(m.xn[:, i, :], m.xn[:, i, :], bias[0][:], ALU.add)

            tensor, scalar, vector = turn_and_multiply(nc, st, xq, m, w_q[0], D, emit)
            with nc.Block() as block:
                @block.tensor
                def _(pe):
                    tensor(pe, lambda i: (xq_ready, i + 1))

                @block.scalar
                def _(act):
                    norm.scalar(act)
                    scalar(act)

                @block.vector
                def _(dve):
                    link = Link(dve, chain)
                    norm.vector(dve, link)
                    link(nc.vector.tensor_reduce(largest[:], m.xn[:], axis=AX.X, op=ALU.max,
                                                 apply_absolute_value=True))
                    token_scale(nc, link, largest[:], deq[:], factor[:])
                    for i in range(NI):
                        round_clip(nc, link, xq[:, i, :], tmp[:, i, :], m.xn[:, i, :], factor[:, i:i + 1],
                                   -127.0, 127.0, xq_ready)
                    vector(dve)

        with ExitStack() as ctx:
            st = Stage(nc, ctx, "c3")
            q_t = [st.sb(f"q_t{n}", [P, NK, P]) for n in range(2)]
            s = [st.sb(f"s{n}", [P, XH, L]) for n in range(2)]
            top = [st.sb(f"top{n}", [P, XH]) for n in range(2)]
            probs_t = [st.sb(f"probs_t{n}", [P, 8, P]) for n in range(2)]
            inv = [st.sb(f"inv{n}", [P, 8, 2]) for n in range(2)]
            p_q = st.ps("p_q")
            p_s = st.ps("p_s", [P, NK, 512])
            p_p = [st.ps(f"p_p{n}") for n in range(4)]
            p_o = st.ps("p_o")
            q_turned = st.sem("q_turned")
            q_copied = st.sem("q_copied")
            s_done = st.sem("s_done")
            masked = st.sem("masked")
            topped = st.sem("topped")
            shifted = st.sem("shifted")
            exped = st.sem("exped")
            p_turned = st.sem("p_turned")
            p_copied = st.sem("p_copied")
            weighed = st.sem("weighed")
            inverted = st.sem("inverted")
            o_done = st.sem("o_done")
            with nc.Block() as block:
                @block.tensor
                def _(pe):
                    def scores(i):
                        if i >= 1:
                            pe.wait_ge(q_copied, i)
                        for k in range(NK):
                            last = nc.tensor.transpose(p_q[:, k * P:(k + 1) * P], m.xn[:, i, k * P:(k + 1) * P],
                                                       m.ident[:])
                        last.then_inc(q_turned, 1)
                        pe.wait_ge(q_copied, i + 1)
                        if i >= 1:
                            pe.wait_ge(masked, 2 * i)
                        for k in range(NK):
                            for b2 in range(2):
                                last = nc.tensor.matmul(
                                    p_s[64 * b2:64 * b2 + 64, k, :], q_t[i % 2][:, k, 64 * b2:64 * b2 + 64],
                                    k_heads[:, k, 2 * i + b2, :, :].rearrange("p h l -> p (h l)"),
                                    start=True, stop=True)
                        last.then_inc(s_done, 1)

                    def weigh(i):
                        pe.wait_ge(exped, i + 1)
                        for n in range(2):
                            if i >= 2:
                                pe.wait_ge(p_copied, 2 * (i - 2) + n + 1)
                            for pair in range(4 * n, 4 * n + 4):
                                last = nc.tensor.transpose(
                                    p_p[2 * (i % 2) + n][:, pair % 4 * P:pair % 4 * P + P],
                                    s[i % 2][:, 2 * pair:2 * pair + 2, :].rearrange("p h l -> p (h l)"), m.ident[:])
                            last.then_inc(p_turned, 1)
                        if i >= 1:
                            pe.wait_ge(o_done, i)
                        pe.wait_ge(p_copied, 2 * i + 2)
                        for pair in range(8):
                            for b2 in range(2):
                                last = nc.tensor.matmul(p_o[64 * b2:64 * b2 + 64, pair * PAIR:(pair + 1) * PAIR],
                                                        probs_t[i % 2][:, pair, 64 * b2:64 * b2 + 64],
                                                        v_pairs[:, 2 * i + b2, pair, :], start=True, stop=True)
                        last.then_inc(weighed, 1)

                    scores(0)
                    for i in range(NI):
                        if i + 1 < NI:
                            scores(i + 1)
                        weigh(i)

                @block.scalar
                def _(act):
                    def copy_q(i):
                        act.wait_ge(q_turned, i + 1)
                        nc.scalar.activation(q_t[i % 2][:].rearrange("p k t -> p (k t)"), p_q[:, 0:D],
                                             ACT.Copy).then_inc(q_copied, 1)

                    def exps(i):
                        act.wait_ge(shifted, i + 1)
                        nc.scalar.activation(s[i % 2][:], s[i % 2][:], ACT.Exp).then_inc(exped, 1)

                    def copy_p(i):
                        for n in range(2):
                            act.wait_ge(p_turned, 2 * i + n + 1)
                            if i >= 2 and n == 0:
                                act.wait_ge(weighed, i - 1)
                            nc.scalar.activation(probs_t[i % 2][:, 4 * n:4 * n + 4, :],
                                                 p_p[2 * (i % 2) + n][:].rearrange("p (h t) -> p h t", h=4),
                                                 ACT.Copy).then_inc(p_copied, 1)

                    copy_q(0)
                    for i in range(NI):
                        if i + 1 < NI:
                            copy_q(i + 1)
                        exps(i)
                        copy_p(i)

                @block.vector
                def _(dve):
                    v = nc.vector

                    def soften(i):
                        n = i % 2
                        dve.wait_ge(s_done, i + 1)
                        if i >= 2:
                            dve.wait_ge(p_turned, 2 * (i - 1))
                        m_i = mask[:, i, :]
                        m_b = bass.AP(m_i.tensor, m_i.offset, [list(m_i.ap[0]), [0, 8], [1, L]])
                        for k in range(NK):
                            v.scalar_tensor_tensor(s[n][:, 8 * k:8 * k + 8, :],
                                                   p_s[:, k, :].rearrange("p (h l) -> p h l", h=8), XC ** -0.5,
                                                   m_b, ALU.mult, ALU.add).then_inc(masked, 1)
                        dve.wait_ge(masked, 2 * i + 2)
                        v.tensor_reduce(top[n][:], s[n][:], axis=AX.X, op=ALU.max).then_inc(topped, 1)
                        dve.wait_ge(topped, i + 1)
                        t = top[n][:]
                        v.tensor_tensor(s[n][:], s[n][:], bass.AP(t.tensor, t.offset, [list(t.ap[0]), [1, XH], [0, L]]),
                                        ALU.subtract).then_inc(shifted, 1)

                    def divide(i):
                        dve.wait_ge(weighed, i + 1)
                        y = p_o[:, 0:8 * PAIR].rearrange("p (q c) -> p q c", q=8)
                        r = inv[i % 2]
                        v.reciprocal(r[:], y[:, :, 2 * XC:PAIR]).then_inc(inverted, 1)
                        dve.wait_ge(inverted, i + 1)
                        for odd in range(2):
                            w = r[:, :, odd:odd + 1]
                            w = bass.AP(w.tensor, w.offset, [list(w.ap[0]), [2, 8], [0, XC]])
                            dst = o[:, i, :].rearrange("p (q s c) -> p q s c", s=2, c=XC)[:, :, odd, :]
                            last = v.tensor_tensor(dst, y[:, :, XC * odd:XC * odd + XC], w, ALU.mult)
                        last.then_inc(o_done, 1)

                    soften(0)
                    for i in range(NI):
                        if i + 1 < NI:
                            soften(i + 1)
                        divide(i)

        with ExitStack() as ctx:
            st = Stage(nc, ctx, "c4")
            tmp = st.sb("tmp", [P, NI, D])
            y_sb = st.sb("y", [P, NI, D])
            chain = st.sem("chain")
            oq_ready = st.sem("oq_ready")
            scaled = st.sem("scaled")

            def emit(i, y):
                nc.vector.scalar_tensor_tensor(y_sb[:, i, :], y, deq[:, i:i + 1], w_s[1][:],
                                               ALU.mult, ALU.mult).then_inc(scaled, 1)
                nc.vector.wait_ge(scaled, 2 * i + 1)
                nc.vector.tensor_tensor(y_sb[:, i, :], y_sb[:, i, :], bias[1][:], ALU.add).then_inc(scaled, 1)
                nc.vector.wait_ge(scaled, 2 * i + 2)
                return nc.vector.tensor_tensor(m.x[:, i, :], m.x[:, i, :], y_sb[:, i, :], ALU.add)

            tensor, scalar, vector = turn_and_multiply(nc, st, xq, m, w_q[1], D, emit)
            with nc.Block() as block:
                @block.tensor
                def _(pe):
                    tensor(pe, lambda i: (oq_ready, i + 1))

                @block.scalar
                def _(act):
                    scalar(act)

                @block.vector
                def _(dve):
                    link = Link(dve, chain)
                    link(nc.vector.tensor_reduce(largest[:], o[:], axis=AX.X, op=ALU.max, apply_absolute_value=True))
                    token_scale(nc, link, largest[:], deq[:], factor[:])
                    for i in range(NI):
                        round_clip(nc, link, xq[:, i, :], tmp[:, i, :], o[:, i, :], factor[:, i:i + 1],
                                   -127.0, 127.0, oq_ready)
                    vector(dve)



class Memory:

    def k_dram_of(self, layer):
        return self.k_unit if layer == 1 else self.k_plain


def program(nc, a, out, stages):
    with ExitStack() as ctx:
        st = Stage(nc, ctx, "all")
        m = Memory()
        m.x = st.sb("x", [P, NI, D])
        m.xn = st.sb("xn", [P, NI, D])
        m.ident = st.sb("ident", [P, P])
        m.ident_bf = st.sb("ident_bf", [P, P], BF16)
        m.same_head = st.sb("same_head", [P, P])
        m.select = st.sb("select", [P, 2, 2, P])
        m.gamma = st.sb("gamma", [P, 1])
        row = CH * HEADS * D
        m.k_plain = nc.dram_tensor("k_plain", [B, len(K_COPIES), row], BF16).ap()
        m.k_unit = nc.dram_tensor("k_unit", [B, len(K_COPIES), row], BF16).ap()
        m.q_parts = nc.dram_tensor("q_parts", [B, len(Q_COPIES), row], BF16).ap()
        m.coef = nc.dram_tensor("coef", [max(mx.experts for mx in MIXTURES.values()) + 1, T], F32).ap()
        m.scales = nc.dram_tensor("scales", [2, D], F32).ap()
        Stage.held = []
        prepare(nc, m, a)
        for stage in stages:
            kind, layer = stage
            if kind == "xattn" and layer < 3:
                attention(nc, m, a, layer)
            elif kind == "xattn":
                quantized_attention(nc, m, a)
            elif layer == 0:
                ternary_feed_forward(nc, m, a)
            else:
                mixture(nc, m, a, layer)
            if kind == "ffn":
                Stage.recycle(nc)
        stored = st.sem("stored")
        with nc.Block() as block:
            @block.sync
            def _(sp):
                sp.dma_start(out, m.x[:]).then_inc(stored, 16)
                sp.wait_ge(stored, 16)



def tokens_in(x):
    n = x.shape[-1]
    return x.reshape(NI, 2, HEADS, CH, n).transpose(1, 3, 2, 0, 4).reshape(P, NI, n)


def tokens_out(y):
    return y.reshape(2, CH, HEADS, NI, D).transpose(3, 0, 2, 1, 4).reshape(B, S, D)


def pack_experts(layer, gate, up, down, s_gate, s_up, s_down):
    mx = MIXTURES[layer]
    gap = np.zeros((mx.shared_tiles * P - s_down.shape[0], D), np.float32)
    down = np.concatenate([s_down, gap, down], 0)
    gu = np.stack([np.concatenate([s_gate, gap.T, gate], 1), np.concatenate([s_up, gap.T, up], 1)], 0)
    gu = gu.reshape(2, NK, P, mx.tiles, P).transpose(3, 2, 1, 0, 4).reshape(mx.tiles, P, UP)
    return np.concatenate([gu, down.reshape(mx.tiles, P, D)], 2)


def width_first(w):
    return w.reshape(NK, P, -1).transpose(1, 0, 2)


def layout(inputs):
    f = np.float32
    I = {n: np.asarray(v) for n, v in inputs.items()}
    x, ctx = np.asarray(inputs["x"]), np.asarray(inputs["ctx_2048"])
    arrays = {"x": tokens_in(x), "ctx": tokens_in(ctx)}
    arrays["gamma"] = np.asarray(inputs["L2_xattn_gamma"]).reshape(1)
    arrays["ident"] = np.eye(P, dtype=f)
    p = np.arange(P)
    arrays["same_head"] = ((p[:, None] // 64 == p[None] // 64) & (p[:, None] % HEADS == p[None] % HEADS)).astype(f)
    v = np.zeros((B, P, NK, HEADS, 32), f)
    c4 = ctx.reshape(B, HEADS, CH, NK, P)
    for h in range(HEADS):
        v[:, :, :, h, h % 2:16:2] = c4[:, h].transpose(0, 3, 2, 1)
        v[:, :, :, h, 16 + h % 2:32:2] = 1.0
    arrays["v"] = v.reshape(B, P, NK * HEADS * 32)
    select = np.zeros((P, 2, 2, P), f)
    for j in range(4):
        for c in range(CH):
            for odd in range(2):
                for b2 in range(2):
                    for part in range(2):
                        select[32 * j + 16 * part + 2 * c + odd, b2, part, 64 * b2 + 8 * c + 2 * j + odd] = 1.0
    arrays["select"] = select

    def stack_in(w):
        return w.transpose(1, 0, 2).reshape(D, -1)

    arrays["w1"] = pack_experts(1, stack_in(I["L1_ffn_w_gate"]), stack_in(I["L1_ffn_w_up"]),
                                I["L1_ffn_w_down"].reshape(-1, D), I["L1_ffn_sw_gate"], I["L1_ffn_sw_up"],
                                I["L1_ffn_sw_down"])
    arrays["w2"] = pack_experts(2, stack_in(I["L2_ffn_w_gate"]), stack_in(I["L2_ffn_w_up"]),
                                I["L2_ffn_w_down"].reshape(-1, D), I["L2_ffn_sw_gate"], I["L2_ffn_sw_up"],
                                I["L2_ffn_sw_down"])
    w13 = I["L3_ffn_w13"].reshape(16, 2, 176, D)
    shared = I["L3_ffn_shared_gate_up_w"].reshape(2, 704, D)
    arrays["w3"] = pack_experts(3, w13[:, 0].reshape(-1, D).T, w13[:, 1].reshape(-1, D).T,
                                I["L3_ffn_w2"].transpose(0, 2, 1).reshape(-1, D), shared[0].T, shared[1].T,
                                I["L3_ffn_shared_down_w"].T)
    arrays["ternary0"] = width_first(I["L0_ffn_w1"].T).reshape(P, -1)
    arrays["ternary1"] = I["L0_ffn_w2"].T.reshape(NH, P, D).transpose(1, 0, 2).reshape(P, -1)
    arrays["xq_w"], arrays["xo_w"] = width_first(I["L3_xattn_wq"]), width_first(I["L3_xattn_wo"])
    arrays["xk_w"], arrays["xv_w"] = width_first(I["L3_xattn_wk"].T), width_first(I["L3_xattn_wv"].T)
    arrays["xq_b"], arrays["xo_b"], arrays["xv_b"] = I["L3_xattn_bq"], I["L3_xattn_bo"], I["L3_xattn_bv"]
    arrays["xk_b"] = I["L3_xattn_bk"].reshape(NK, P).T
    arrays["own"] = (p[:, None] // XC == np.arange(8)[None]).astype(f)
    arrays["cond"] = width_first(ctx.reshape(T, D).T)
    arrays["mask"] = tokens_in(I["mask_BxSxS2_ff0"])
    arrays["router1"] = width_first(I["L1_ffn_gate_w"])
    arrays["router2"] = width_first(I["L2_ffn_router_w"])
    arrays["router3"] = width_first(np.concatenate([I["L3_ffn_gate_w"], I["L3_ffn_sgate_w"]], 0).T)
    arrays["router_bias"] = I["L2_ffn_router_bias"]
    return {n: np.ascontiguousarray(v) for n, v in arrays.items()}


STAGES = [("xattn", 0), ("ffn", 0), ("xattn", 1), ("ffn", 1), ("xattn", 2), ("ffn", 2), ("xattn", 3), ("ffn", 3)]


def kernel(**inputs):
    import concourse.bacc as bacc
    from concourse.bass_utils import run_bass_kernel_spmd

    nc = bacc.Bacc("TRN2", target_bir_lowering=False, num_devices=1)
    arrays = layout(inputs)
    args = {n: nc.dram_tensor(f"in_{n}", v.shape, mybir.dt.from_np(v.dtype), kind="ExternalInput").ap()
            for n, v in arrays.items()}
    out = nc.dram_tensor("out", (P, NI, D), F32, kind="ExternalOutput").ap()
    program(nc, args, out, STAGES)
    r = run_bass_kernel_spmd(nc, [{f"in_{n}": v for n, v in arrays.items()}], core_ids=[0])
    return tokens_out(np.asarray(r.results[0]["out"]))
```

```python
import numpy as np
from contextlib import ExitStack

import concourse.bass as bass
from concourse import mybir

F32 = mybir.dt.float32
F32R = mybir.dt.float32r
BF16 = mybir.dt.bfloat16
ALU = mybir.AluOpType
ACT = mybir.ActivationFunctionType
AX = mybir.AxisListType

P = 128
B, S, D = 16, 64, 256
T = B * S
NI = T // P
NK = D // P
HEADS, CH = 8, 8
LN_EPS = 1e-5
PAD = -1e30
ROUND = 1.5 * 2.0 ** 23


class Link:

    def __init__(self, eng, sem):
        self.eng, self.sem, self.count = eng, sem, 0

    def __call__(self, instruction):
        self.count += 1
        instruction.then_inc(self.sem, 1)
        self.eng.wait_ge(self.sem, self.count)


class Stage:

    def __init__(self, nc, ctx, name):
        self.nc, self.ctx, self.name = nc, ctx, name

    def sb(self, name, shape, dt=F32):
        return self.ctx.enter_context(self.nc.sbuf_tensor(f"{self.name}_{name}", shape, dt))

    def ps(self, name, shape=(P, 512)):
        return self.ctx.enter_context(self.nc.psum_tensor(f"{self.name}_{name}", list(shape), F32))

    def sem(self, name):
        handle = self.nc.alloc_semaphore(f"{self.name}_{name}")
        Stage.held.append(handle)
        return handle

    held = []

    @staticmethod
    def recycle(nc):
        nc.all_engine_barrier()
        nc.clear_and_free_semaphores(Stage.held)
        nc.all_engine_barrier()
        Stage.held = []


class Step:

    def __init__(self, g, r, n):
        self.g, self.r, self.n = g, r, n

    def __add__(self, by):
        return Step(self.g, self.r + by, self.n)


def lin(b, times, plus):
    return b.g * (b.n * times) + (b.r * times + plus) if isinstance(b, Step) else times * b + plus


def half(b):
    return b.g * (b.n // 2) + b.r // 2 if isinstance(b, Step) else b // 2


def slot(b, n):
    return (b.r if isinstance(b, Step) else b) % n


def uses(b, n):
    return b.g * (b.n // n) + b.r // n if isinstance(b, Step) else b // n


def wait(eng, sem, b, times, plus):
    value = lin(b, times, plus)
    if isinstance(b, Step) or value > 0:
        eng.wait_ge(sem, value)


def bc(ap, *dims):
    return bass.AP(ap.tensor, ap.offset, [list(ap.ap[0])] + [list(d) for d in dims])



class Norm:

    def __init__(self, st, x, xn):
        self.nc, self.x, self.xn = st.nc, x, xn
        self.stats = st.sb("ln_stats", [P, NI, 6])
        self.mv = st.sb("ln_mv", [P, NI, 2])
        self.var = st.sb("ln_var", [P, NI])
        self.root = st.sb("ln_root", [P, NI])
        self.tmp = st.sb("ln_tmp", [P, NI])
        self.var_ready = st.sem("ln_var_ready")
        self.root_ready = st.sem("ln_root_ready")
        self.xn_ready = st.sem("ln_xn_ready")

    def scalar(self, act):
        act.wait_ge(self.var_ready, 1)
        self.nc.scalar.activation(self.root[:], self.var[:], ACT.Sqrt).then_inc(self.root_ready, 1)

    def vector(self, dve, link):
        v = self.nc.vector
        for i in range(NI):
            last = v.bn_stats(self.stats[:, i, :], self.x[:, i, :])
        link(last)
        for i in range(NI):
            last = v.bn_aggr(self.mv[:, i, :], self.stats[:, i, :])
        link(last)
        v.tensor_scalar(self.var[:], self.mv[:, :, 1], LN_EPS, None, ALU.add).then_inc(self.var_ready, 1)
        dve.wait_ge(self.root_ready, 1)
        link(v.reciprocal(self.tmp[:], self.root[:]))
        link(v.tensor_tensor(self.tmp[:], self.tmp[:], self.var[:], ALU.mult))
        link(v.tensor_tensor(self.tmp[:], self.tmp[:], self.root[:], ALU.add))
        link(v.tensor_scalar(self.tmp[:], self.tmp[:], 0.5, None, ALU.mult))
        link(v.reciprocal(self.root[:], self.tmp[:]))
        for i in range(NI):
            v.tensor_scalar(self.xn[:, i, :], self.x[:, i, :], self.mv[:, i, 0:1], self.root[:, i:i + 1],
                            ALU.subtract, ALU.mult).then_inc(self.xn_ready, 1)
        dve.wait_ge(self.xn_ready, NI)



class Parts:

    def __init__(self, st, tag, dram, copies):
        self.nc, self.dram, self.copies = st.nc, dram, copies
        self.part = st.sb(f"{tag}_part", [P, 3, NI, D], BF16)
        self.rest = st.sb(f"{tag}_rest", [P, NI, D])
        self.hi_ready = st.sem(f"{tag}_hi_ready")
        self.rest_ready = st.sem(f"{tag}_rest_ready")
        self.mid_ready = st.sem(f"{tag}_mid_ready")
        self.lo_ready = st.sem(f"{tag}_lo_ready")
        self.stored = st.sem(f"{tag}_stored")

    HALF = NI // 2

    def high(self, act, src, src_ready=None, count=0):
        for n in range(2):
            t = slice(n * self.HALF, (n + 1) * self.HALF)
            if src_ready is not None:
                act.wait_ge(src_ready, count * (n + 1) // 2)
            self.nc.scalar.activation(self.part[:, 0, t, :], src[:, t, :], ACT.Copy).then_inc(self.hi_ready, 1)

    def mid(self, act):
        for n in range(2):
            t = slice(n * self.HALF, (n + 1) * self.HALF)
            act.wait_ge(self.rest_ready, n + 1)
            self.nc.scalar.activation(self.part[:, 1, t, :], self.rest[:, t, :], ACT.Copy).then_inc(self.mid_ready, 1)

    def take_high(self, dve, src):
        for n in range(2):
            t = slice(n * self.HALF, (n + 1) * self.HALF)
            dve.wait_ge(self.hi_ready, n + 1)
            self.nc.vector.tensor_tensor(self.rest[:, t, :], src[:, t, :], self.part[:, 0, t, :],
                                         ALU.subtract).then_inc(self.rest_ready, 1)

    def take_mid(self, dve):
        for n in range(2):
            t = slice(n * self.HALF, (n + 1) * self.HALF)
            dve.wait_ge(self.mid_ready, n + 1)
            self.nc.vector.tensor_tensor(self.part[:, 2, t, :], self.rest[:, t, :], self.part[:, 1, t, :],
                                         ALU.subtract).then_inc(self.lo_ready, 1)

    def store(self, sp, part):
        row = HEADS * CH * D
        n_blocks = len(self.copies)
        ready = (self.hi_ready, self.mid_ready, self.lo_ready)[part]
        sp.wait_ge(ready, 2)
        for block in [n for n, p in enumerate(self.copies) if p == part]:
            for b2 in range(2):
                dst = bass.AP(self.dram.tensor, self.dram.offset + (b2 * n_blocks + block) * row,
                              [[D, HEADS * CH], [2 * n_blocks * row, NI], [1, D]])
                sp.dma_start(dst, self.part[64 * b2:64 * b2 + 64, part, :, :]).then_inc(self.stored, 16)

    def wait_stored(self, sp):
        sp.wait_ge(self.stored, 2 * 16 * len(self.copies))


class HeadNorm:

    EPS2 = 1e-24

    def __init__(self, st, tag, src, out, m):
        self.nc, self.src, self.out, self.m = st.nc, src, out, m
        self.square = st.sb(f"{tag}_square", [P, NI, D])
        self.length = st.sb(f"{tag}_length", [P, D])
        self.inverse = st.sb(f"{tag}_inverse", [P, D])
        self.total = st.ps(f"{tag}_total")
        self.spread = [st.ps(f"{tag}_spread{n}") for n in range(2)]
        self.square_ready = st.sem(f"{tag}_square_ready")
        self.total_ready = st.sem(f"{tag}_total_ready")
        self.clamped = st.sem(f"{tag}_clamped")
        self.root_ready = st.sem(f"{tag}_root_ready")
        self.inverse_ready = st.sem(f"{tag}_inverse_ready")
        self.spread_ready = st.sem(f"{tag}_spread_ready")
        self.out_ready = st.sem(f"{tag}_out_ready")

    def squares(self, engine):
        for n in range(4):
            t = slice(2 * n, 2 * n + 2)
            engine.tensor_tensor(self.square[:, t, :], self.src[:, t, :], self.src[:, t, :],
                                 ALU.mult).then_inc(self.square_ready, 1)

    def gather(self, pe):
        for i in range(NI):
            pe.wait_ge(self.square_ready, i // 2 + 1)
            last = self.nc.tensor.matmul(self.total[:, 0:D], self.m.gather[:, P - 16 * (i + 1):2 * P - 16 * (i + 1)],
                                         self.square[:, i, :], start=(i == 0), stop=(i == NI - 1))
        last.then_inc(self.total_ready, 1)

    def clamp(self, dve):
        dve.wait_ge(self.total_ready, 1)
        self.nc.vector.tensor_scalar(self.length[:], self.total[:, 0:D], self.EPS2, None,
                                     ALU.max).then_inc(self.clamped, 1)

    def root(self, act):
        act.wait_ge(self.clamped, 1)
        self.nc.scalar.activation(self.length[:], self.length[:], ACT.Sqrt).then_inc(self.root_ready, 1)

    def invert(self, dve):
        dve.wait_ge(self.root_ready, 1)
        self.nc.vector.reciprocal(self.inverse[:], self.length[:]).then_inc(self.inverse_ready, 1)

    def spread_out(self, pe):
        pe.wait_ge(self.inverse_ready, 1)
        for i in range(NI):
            n = i // 2
            if i % 2 == 0 and n >= 2:
                pe.wait_ge(self.out_ready, n - 1)
            last = self.nc.tensor.matmul(self.spread[n % 2][:, i % 2 * D:i % 2 * D + D], self.m.spread[:, i, :],
                                         self.inverse[:], start=True, stop=True)
            if i % 2 == 1:
                last.then_inc(self.spread_ready, 1)

    def scale(self, dve):
        for n in range(4):
            t = slice(2 * n, 2 * n + 2)
            dve.wait_ge(self.spread_ready, n + 1)
            self.nc.vector.tensor_tensor(self.out[:, t, :], self.src[:, t, :],
                                         self.spread[n % 2][:].rearrange("p (i d) -> p i d", i=2),
                                         ALU.mult).then_inc(self.out_ready, 1)


K_COPIES = [0, 1, 2, 0, 1]
Q_COPIES = [0, 1, 2]
ROWS = 9 * CH
MAX_AT = 96


def load_last_attention(sp, m, a):
    for n in range(2):
        sp.dma_start(m.raw[n][:], a[("xq_w", "xo_w")[n]]).then_inc(m.raw_loaded, 16)
    for t, name in ((m.cond, "cond"), (m.wk, "xk_w"), (m.wv, "xv_w")):
        sp.dma_start(t[:], a[name]).then_inc(m.cond_loaded, 16)


STEP_ORDER = "mtm0mpq1mw2mxm3mymz"


def load_inputs(sp, m, a):
    sp.dma_start(m.x[:], a["x"]).then_inc(m.x_loaded, 16)
    sp.dma_start(m.ident[:], a["ident"]).then_inc(m.constants_loaded, 16)
    sp.dma_start(m.select[:], a["select"]).then_inc(m.constants_loaded, 16)
    sp.dma_start(m.gamma[:], bass.AP(a["gamma"].tensor, 0, [[0, P], [1, 1]])).then_inc(m.constants_loaded, 16)


def attention(nc, m, a, layer):
    with_max = layer != 1
    scale = 5.0 if layer == 1 else CH ** -0.5
    NB = 4
    PAIRS = HEADS // 2
    row = CH * HEADS * D
    outer = ExitStack()
    st = Stage(nc, outer, f"o{layer}")
    q = [st.sb(f"q{n}", [P, HEADS, D], BF16) for n in range(NB)]
    k = [st.sb(f"k{n}", [P, HEADS, D], BF16) for n in range(NB)]
    v = [st.sb(f"v{n}", [P, NK, HEADS, 32]) for n in range(NB)]
    loaded = [st.sem(f"loaded{n}") for n in range(NB)]
    v_loaded = [st.sem(f"v_loaded{n}") for n in range(NB)]
    k_zeroed = st.sem("k_zeroed")
    k_cleared = st.sem("k_cleared")
    q_cleared = st.sem("q_cleared")

    def load_q(sp, at, n):
        src = m.q_parts[bass.ds(at, 1), :, :]
        src = bass.AP(src.tensor, src.offset, [[0, 3], [HEADS * D, 3 * CH], [1, HEADS * D]])
        sp.dma_start(q[n][0:ROWS, :, :], src).then_inc(loaded[n], 16)

    def load_k(sp, at, n):
        src = m.k_dram_of(layer)[bass.ds(at, 1), :, :]
        src = bass.AP(src.tensor, src.offset, [[row, 3], [HEADS * D, 3 * CH], [1, HEADS * D]])
        sp.dma_start(k[n][0:ROWS, :, :], src).then_inc(loaded[n], 16)

    def load_v(sp, at, n):
        sp.dma_start(v[n][:].rearrange("p k h c -> p (k h c)"),
                     a["v"][bass.ds(at, 1), :, :].rearrange("b p c -> p (b c)")).then_inc(v_loaded[n], 16)

    def clear_q(engine):
        for n in range(NB):
            engine.memset(q[n][64:P, :, :], 0.0).then_inc(q_cleared, 1)

    with ExitStack() as ctx:
        st = Stage(nc, ctx, f"q{layer}")
        norm = Norm(st, m.x, m.xn)
        parts = Parts(st, "q", m.q_parts, Q_COPIES)
        chain = st.sem("chain")
        new_keys = layer < 2
        if new_keys:
            keys = st.sb("keys", [P, NI, D])
            keys_loaded = st.sem("keys_loaded")
            key_parts = Parts(st, "k", m.k_dram_of(layer), K_COPIES)
        if layer == 1:
            masks_loaded = st.sem("masks_loaded")
            m.gather = st.sb("gather", [P, 2 * P])
            m.spread = st.sb("spread", [P, NI, P])
            unit_q = HeadNorm(st, "qn", m.xn, m.xn, m)
            unit_k = HeadNorm(st, "kn", keys, keys, m)
        with nc.Block() as block:
            @block.sync
            def _(sp):
                if layer == 0:
                    load_inputs(sp, m, a)
                if new_keys:
                    sp.dma_start(keys[:], a["ctx"]).then_inc(keys_loaded, 16)
                if layer == 1:
                    sp.dma_start(m.gather[:], a["gather"]).then_inc(masks_loaded, 16)
                    sp.dma_start(m.spread[:], a["spread"]).then_inc(masks_loaded, 16)
                for n in range(NB):
                    load_v(sp, n, n)
                if new_keys:
                    key_parts.store(sp, 0)
                    key_parts.store(sp, 1)
                else:
                    for n in range(NB):
                        sp.wait_ge(k_cleared, n + 1)
                        load_k(sp, n, n)
                parts.store(sp, 0)
                if new_keys:
                    key_parts.store(sp, 2)
                parts.store(sp, 1)
                parts.store(sp, 2)
                if new_keys:
                    key_parts.wait_stored(sp)
                parts.wait_stored(sp)
                if layer == 0:
                    sp.wait_ge(m.constants_loaded, 3 * 16)

            @block.gpsimd
            def _(pool):
                for n in range(NB):
                    nc.gpsimd.memset(k[n][64:P, :, :], 0.0).then_inc(k_zeroed, 1)
                if layer == 2:
                    clear_q(nc.gpsimd)
                    pool.wait_ge(q_cleared, NB)
                pool.wait_ge(k_zeroed, NB)
                if layer == 1:
                    pool.wait_ge(keys_loaded, 16)
                    unit_k.squares(nc.gpsimd)
                    pool.wait_ge(unit_k.square_ready, 4)
                    clear_q(nc.gpsimd)
                for n in range(NB):
                    if with_max:
                        nc.gpsimd.memset(k[n][MAX_AT:MAX_AT + 3, :, :], 1.0).then_inc(k_cleared, 1)
                    else:
                        pool.sem_inc(k_cleared, 1)

            @block.scalar
            def _(act):
                if layer == 0:
                    act.wait_ge(keys_loaded, 16)
                    key_parts.high(act, keys)
                    norm.scalar(act)
                    key_parts.mid(act)
                else:
                    norm.scalar(act)
                if layer == 1:
                    unit_k.root(act)
                    unit_q.root(act)
                    key_parts.high(act, keys, unit_k.out_ready, 4)
                    key_parts.mid(act)
                    parts.high(act, m.xn, unit_q.out_ready, 4)
                else:
                    parts.high(act, m.xn, norm.xn_ready, NI)
                parts.mid(act)

            @block.vector
            def _(dve):
                link = Link(dve, chain)
                if layer == 0:
                    clear_q(nc.vector)
                if layer == 0:
                    dve.wait_ge(m.x_loaded, 16)
                norm.vector(dve, link)
                if layer == 0:
                    key_parts.take_high(dve, keys)
                    parts.take_high(dve, m.xn)
                    key_parts.take_mid(dve)
                elif layer == 1:
                    unit_q.squares(nc.vector)
                    unit_k.clamp(dve)
                    unit_k.invert(dve)
                    unit_q.clamp(dve)
                    unit_q.invert(dve)
                    unit_k.scale(dve)
                    key_parts.take_high(dve, keys)
                    unit_q.scale(dve)
                    key_parts.take_mid(dve)
                    parts.take_high(dve, m.xn)
                else:
                    parts.take_high(dve, m.xn)
                parts.take_mid(dve)
                if layer == 0:
                    dve.wait_ge(m.constants_loaded, 3 * 16)
                    nc.vector.tensor_copy(m.ident_bf[:], m.ident[:])

            @block.tensor
            def _(pe):
                if layer == 1:
                    pe.wait_ge(masks_loaded, 32)
                    unit_k.gather(pe)
                    unit_q.gather(pe)
                    unit_k.spread_out(pe)
                    unit_q.spread_out(pe)

    with ExitStack() as ctx:
        st = Stage(nc, ctx, f"a{layer}")
        probs = [st.sb(f"probs{n}", [P, HEADS, NK, D]) for n in range(2)]
        maxes = [st.sb(f"maxes{n}", [P, HEADS * NK]) for n in range(2)]
        neg = [st.sb(f"neg{n}", [HEADS * NK, 3, P], BF16) for n in range(2)]
        max_t = st.sb("max_t", [HEADS * NK, P])
        rest = st.sb("rest", [HEADS * NK, P])
        ones = st.sb("ones", [HEADS * NK, P])
        ones_ready = st.sem("ones_ready")
        out = [st.sb(f"out{n}", [P, D]) for n in range(2)]
        inv = st.sb("inv", [P, D])
        prod = st.sb("prod", [P, D])
        p_max = [st.ps(f"p_max{n}") for n in range(2)]
        p_sc = [st.ps(f"p_sc{n}", [P, 2, 512]) for n in range(2)]
        p_out = st.ps("p_out")
        p_misc = st.ps("p_misc")

        neg_loaded = [st.sem(f"neg_loaded{n}") for n in range(2)]
        max_scored = st.sem("max_scored")
        max_taken = st.sem("max_taken")
        turned = st.sem("turned")
        max_copied = st.sem("max_copied")
        neg_hi = st.sem("neg_hi")
        neg_r1 = st.sem("neg_r1")
        neg_mid = st.sem("neg_mid")
        neg_done = st.sem("neg_done")
        scored = st.sem("scored")
        exp_done = st.sem("exp_done")
        pv_done = st.sem("pv_done")
        out_copied = st.sem("out_copied")
        placed = st.sem("placed")
        added = st.sem("added")
        inv_done = st.sem("inv_done")
        divided = st.sem("divided")

        LOOPS = B // NB - 1

        with nc.Block() as block:
            @block.sync
            def _(sp):
                def load_neg(b):
                    n = slot(b, NB)
                    wait(sp, neg_done, b, 1, 1)
                    for part in range(3):
                        sp.dma_start(q[n][MAX_AT + part:MAX_AT + part + 1, :, :].rearrange("a h (t m) -> a (h t) m", m=P),
                                     neg[slot(b, 2)][:, part, :]).then_inc(neg_loaded[slot(b, 2)], 16)

                for n in range(NB):
                    if new_keys:
                        load_k(sp, n, n)
                    load_q(sp, n, n)
                if with_max:
                    load_neg(0)
                    load_neg(1)
                with sp.Fori(0, LOOPS) as g:
                    for r in range(NB):
                        b = Step(g, r + NB, NB)
                        at, n = sp.snap(lin(b, 1, 0)), slot(b, NB)
                        q_used, v_used = sp.snap(lin(b, PAIRS, -PAIRS * (NB - 1))), sp.snap(lin(b, 1, 2 - NB))
                        sp.wait_ge(scored, q_used)
                        load_q(sp, at, n)
                        load_k(sp, at, n)
                        if with_max:
                            sp.dma_start(q[n][MAX_AT:MAX_AT + 3, :, :],
                                         q[n][MAX_AT + 3:MAX_AT + 6, :, :]).then_inc(loaded[n], 16)
                            load_neg(Step(g, r + 2, NB))
                        sp.wait_ge(pv_done, v_used)
                        load_v(sp, at, n)
                if with_max:
                    for b in range(B - NB + 2, B):
                        load_neg(b)

            @block.tensor
            def _(pe):
                def max_scores(b, h):
                    if h == 0:
                        n = slot(b, NB)
                        u = uses(b, NB)
                        pe.wait_ge(loaded[n], u * 48 + 32)
                    wait(pe, max_taken, b, HEADS, h - 1)
                    for t in range(NK):
                        last = nc.tensor.matmul(p_max[h % 2][:, t * D:(t + 1) * D],
                                                q[slot(b, NB)][:, h, t * P:(t + 1) * P],
                                                k[slot(b, NB)][:, h, :], start=True, stop=True)
                    last.then_inc(max_scored, 1)

                def turn_maxima(b):
                    wait(pe, max_taken, b, HEADS, HEADS)
                    wait(pe, max_copied, b, 1, 0)
                    if slot(b, 2) == 1 and (isinstance(b, Step) or b > 1):
                        pe.wait_ge(added, half(b))
                    nc.tensor.transpose(p_misc[0:HEADS * NK, 0:P], maxes[slot(b, 2)][:],
                                        m.ident[:]).then_inc(turned, 1)

                def scores(b, pair):
                    if pair == 0:
                        if with_max:
                            pe.wait_ge(neg_loaded[slot(b, 2)], uses(b, 2) * 48 + 48)
                        else:
                            pe.wait_ge(loaded[slot(b, NB)], uses(b, NB) * 32 + 32)
                    wait(pe, exp_done, b, PAIRS, pair - 1)
                    for h in range(2 * pair, 2 * pair + 2):
                        for t in range(NK):
                            last = nc.tensor.matmul(p_sc[pair % 2][:, h % 2, t * D:(t + 1) * D],
                                                    k[slot(b, NB)][:, h, t * P:(t + 1) * P],
                                                    q[slot(b, NB)][:, h, :], start=True, stop=True)
                    last.then_inc(scored, 1)

                def weigh(b, quarter):
                    odd, t = quarter // 2, quarter % 2
                    if quarter == 0:
                        pe.wait_ge(v_loaded[slot(b, NB)], uses(b, NB) * 16 + 16)
                        wait(pe, exp_done, b, PAIRS, PAIRS)
                        wait(pe, out_copied, b, 1, 1)
                    for j in range(4):
                        h = 2 * j + odd
                        last = nc.tensor.matmul(p_out[32 * j:32 * j + 32, 0:D],
                                                v[slot(b, NB)][:, t, h, :],
                                                probs[slot(b, 2)][:, h, t, :],
                                                start=(quarter == 0), stop=(quarter == 3))
                    if quarter == 3:
                        last.then_inc(pv_done, 1)

                def place(b, part):
                    wait(pe, out_copied, b, 1, 2)
                    if with_max:
                        if isinstance(b, Step) or b + 4 < B:
                            wait(pe, max_copied, b, 1, 4)
                        else:
                            pe.wait_ge(max_copied, B)
                    pe.wait_ge(added, half(b) + 1)
                    for b2 in range(2):
                        last = nc.tensor.matmul(p_misc[:, part * D:(part + 1) * D],
                                                m.select[:, b2, part, :], out[b2][:],
                                                start=(b2 == 0), stop=(b2 == 1), skip_group_check=True)
                    if part == 1:
                        last.then_inc(placed, 1)

                def step(b, has_next, before, placing):
                    maxima = iter(range(HEADS))
                    for what in STEP_ORDER:
                        if what == "m":
                            if with_max and has_next:
                                max_scores(b + 2, next(maxima))
                        elif what == "t":
                            if with_max and (isinstance(b, Step) or b + 1 < B):
                                turn_maxima(b + 1)
                        elif what in "pq":
                            if placing is not None and slot(placing, 2) == 1:
                                place(placing, "pq".index(what))
                        elif what in "0123":
                            scores(b, int(what))
                        elif before is not None:
                            weigh(before, "wxyz".index(what))

                pe.sem_inc(pv_done, 1)
                pe.sem_inc(placed, 1)
                if with_max:
                    for b in range(2):
                        for h in range(HEADS):
                            max_scores(b, h)
                            if b == 1 and h == 0:
                                turn_maxima(0)
                step(0, True, None, None)
                step(1, True, 0, None)
                with pe.Fori(0, LOOPS) as g:
                    for r in range(2, NB + 2):
                        step(Step(g, r, NB), True, Step(g, r - 1, NB), Step(g, r - 2, NB))
                for b in range(B - NB + 2, B):
                    step(b, False, b - 1, b - 2)
                for quarter in range(4):
                    weigh(B - 1, quarter)
                for part in range(2):
                    place(B - 1, part)

            @block.scalar
            def _(act):
                def copy_max(b):
                    if with_max:
                        wait(act, turned, b, 1, 1)
                        wait(act, neg_done, b, 1, 0)
                        nc.scalar.activation(max_t[:], p_misc[0:HEADS * NK, 0:P], ACT.Copy).then_inc(max_copied, 1)

                def exps(b):
                    if isinstance(b, Step) or b + 1 < B:
                        copy_max(b + 1)
                    for pair in range(PAIRS):
                        wait(act, scored, b, PAIRS, pair + 1)
                        if pair == 0:
                            wait(act, pv_done, b, 1, 0)
                        nc.scalar.activation(
                            probs[slot(b, 2)][:, 2 * pair:2 * pair + 2, :, :].rearrange("p h t d -> p h (t d)"),
                            p_sc[pair % 2][:], ACT.Exp, scale=scale).then_inc(exp_done, 1)

                def copy_out(b):
                    wait(act, pv_done, b, 1, 2)
                    act.wait_ge(placed, half(b) + 1)
                    nc.scalar.activation(out[slot(b, 2)][:], p_out[:, 0:D], ACT.Copy).then_inc(out_copied, 1)

                act.sem_inc(out_copied, 1)
                copy_max(0)
                exps(0)
                exps(1)
                copy_out(0)
                with act.Fori(0, LOOPS) as g:
                    for r in range(2, NB + 2):
                        exps(Step(g, r, NB))
                        copy_out(Step(g, r - 1, NB))
                for b in range(B - NB + 2, B):
                    exps(b)
                    copy_out(b - 1)
                copy_out(B - 1)

            @block.vector
            def _(dve):
                def take_max(b, h):
                    wait(dve, max_scored, b, HEADS, h + 1)
                    if h == 0:
                        wait(dve, turned, b, 1, -1)
                    nc.vector.tensor_reduce(maxes[slot(b, 2)][:, NK * h:NK * h + NK],
                                            p_max[h % 2][:].rearrange("p (t d) -> p t d", t=NK),
                                            axis=AX.X, op=ALU.max, negate=True).then_inc(max_taken, 1)

                def divide(b):
                    i = half(b)
                    dve.wait_ge(placed, i + 2)
                    nc.vector.reciprocal(inv[:], p_misc[:, D:2 * D]).then_inc(inv_done, 1)
                    dve.wait_ge(inv_done, i + 1)
                    dve.wait_ge(added, i + 1)
                    gain = m.gamma[:, 0:1] if layer == 2 else 1.0
                    nc.vector.scalar_tensor_tensor(prod[:], p_misc[:, 0:D], gain, inv[:],
                                                   ALU.mult, ALU.mult).then_inc(divided, 1)

                def step(b, has_next, placing):
                    for h in range(HEADS):
                        if with_max and has_next:
                            take_max(b + 2, h)
                        if h == 2 and placing is not None and slot(placing, 2) == 1:
                            divide(placing)

                dve.sem_inc(divided, 1)
                if with_max:
                    for b in range(2):
                        for h in range(HEADS):
                            take_max(b, h)
                step(0, True, None)
                step(1, True, None)
                with dve.Fori(0, LOOPS) as g:
                    for r in range(2, NB + 2):
                        step(Step(g, r, NB), True, Step(g, r - 2, NB))
                for b in range(B - NB + 2, B):
                    step(b, False, b - 2)
                divide(B - 1)

            @block.gpsimd
            def _(pool):
                tt = nc.gpsimd.tensor_tensor

                def split_max(b):
                    s = slot(b, 2)
                    wait(pool, max_copied, b, 1, 1)
                    if isinstance(b, Step) or b > 1:
                        pool.wait_ge(neg_loaded[s], uses(b, 2) * 48)
                    tt(neg[s][:, 0, :], max_t[:], ones[:], ALU.mult).then_inc(neg_hi, 1)
                    wait(pool, neg_hi, b, 1, 1)
                    tt(rest[:], max_t[:], neg[s][:, 0, :], ALU.subtract).then_inc(neg_r1, 1)
                    wait(pool, neg_r1, b, 1, 1)
                    tt(neg[s][:, 1, :], rest[:], ones[:], ALU.mult).then_inc(neg_mid, 1)
                    wait(pool, neg_mid, b, 1, 1)
                    tt(neg[s][:, 2, :], rest[:], neg[s][:, 1, :], ALU.subtract).then_inc(neg_done, 1)

                def add_tile(b):
                    i = half(b)
                    pool.wait_ge(divided, i + 2)
                    x_i = m.x[:, bass.ds(i, 1), :].rearrange("p a d -> p (a d)")
                    tt(x_i, x_i, prod[:], ALU.add).then_inc(added, 1)

                def step(b, placing):
                    if with_max and (isinstance(b, Step) or b + 1 < B):
                        split_max(b + 1)
                    if placing is not None and slot(placing, 2) == 1:
                        add_tile(placing)

                pool.sem_inc(added, 1)
                if with_max:
                    nc.gpsimd.memset(ones[:], 1.0).then_inc(ones_ready, 1)
                    pool.wait_ge(ones_ready, 1)
                    split_max(0)
                step(0, None)
                step(1, None)
                with pool.Fori(0, LOOPS) as g:
                    for r in range(2, NB + 2):
                        step(Step(g, r, NB), Step(g, r - 2, NB))
                for b in range(B - NB + 2, B):
                    step(b, b - 2)
                add_tile(B - 1)
    outer.close()



class Mixture:

    def __init__(self, experts, top, hidden, shared):
        self.experts, self.top, self.hidden = experts, top, hidden
        self.shared_tiles = -(-shared // P)
        self.routed_tiles = experts * hidden // P
        self.tiles = self.shared_tiles + self.routed_tiles
        assert experts * hidden % P == 0 and self.tiles % 2 == 0

    def rows(self, t):
        if t < self.shared_tiles:
            return [(0, P, self.experts)]
        at = (t - self.shared_tiles) * P
        cuts = []
        for e in range(self.experts):
            lo, hi = max(at, e * self.hidden), min(at + P, (e + 1) * self.hidden)
            if lo < hi:
                cuts.append((lo - at, hi - at, e))
        return cuts


MIXTURES = {1: Mixture(8, 2, 176, 352), 2: Mixture(32, 8, 128, 256), 3: Mixture(16, 4, 176, 704)}
GROUPS, TOP_GROUPS, ROUTED_SCALE = 8, 4, 2.5
UP = NK * 2 * P


def rank_top(nc, link, padded, eight, picked, n, top):
    for i in range(NI):
        last = nc.vector.max(eight[:, i, :], padded[:, i, :])
    link(last)
    if top < 8:
        link(nc.vector.memset(eight[:, :, top:8], PAD))
    for i in range(NI):
        last = nc.vector.match_replace(picked[:, i, :], eight[:, i, :], padded[:, i, :], PAD)
    link(last)


def mixture(nc, m, a, layer):
    mx = MIXTURES[layer]
    E, E1, NT = mx.experts, mx.experts + 1, mx.tiles
    n_logits = E1 if layer == 3 else E
    pad = 8 if mx.top < 8 else 0
    SHARED = layer != 3 and mx.shared_tiles >= 2
    with ExitStack() as ctx:
        st = Stage(nc, ctx, f"f{layer}")
        x_hi = st.sb("x_hi", [P, NK, T], F32R)
        x_lo = st.sb("x_lo", [P, NK, T], F32R)

        norm = Norm(st, m.x, m.xn)
        x_t = st.sb("x_t", [P, NK, T])
        router = st.sb("router", [P, NK, n_logits])
        scores = st.sb("scores", [P, NI, E1])
        ranked = st.sb("ranked", [P, NI, E + pad])
        picked = st.sb("picked", [P, NI, E + pad])
        eight = st.sb("eight", [P, NI, 8])
        by_token = st.sb("by_token", [P, NI, E1])
        total = st.sb("total", [P, NI])
        coef_t = st.sb("coef_t", [E1, T])
        chain = st.sem("chain")
        loaded = st.sem("loaded")
        turned = st.sem("turned")
        x_t_ready = st.sem("x_t_ready")
        x_hi_ready = st.sem("x_hi_ready")
        x_lo_ready = st.sem("x_lo_ready")
        logits = st.sem("logits")
        shifted = st.sem("shifted")
        scored = st.sem("scored")
        coef_ready = st.sem("coef_ready")
        coef_turned = st.sem("coef_turned")
        coef_t_ready = st.sem("coef_t_ready")
        stored = st.sem("stored")
        n_loads = 2 if layer == 2 else 1
        if layer == 2:
            bias = st.sb("bias", [P, E])
            pair_hi = st.sb("pair_hi", [P, NI * GROUPS, 2])
            pair_lo = st.sb("pair_lo", [P, NI * GROUPS, 2])
            best = st.sb("best", [P, NI * GROUPS, 3])
            g_ranked = st.sb("g_ranked", [P, NI, GROUPS + 8])
            g_picked = st.sb("g_picked", [P, NI, GROUPS + 8])

        w = [st.sb(f"w{n}", [P, UP + D]) for n in range(2)]
        up_hi = [st.sb(f"up_hi{n}", [P, UP], F32R) for n in range(2)]
        up_lo = [st.sb(f"up_lo{n}", [P, UP], F32R) for n in range(2)]
        down_hi = [st.sb(f"down_hi{n}", [P, D], F32R) for n in range(2)]
        down_lo = [st.sb(f"down_lo{n}", [P, D], F32R) for n in range(2)]
        coef = [st.sb(f"coef{n}", [P, T]) for n in range(2)]
        act_g = [st.sb(f"act_g{c}", [P, 512]) for c in range(2)]
        gated = [st.sb(f"gated{c}", [P, 512]) for c in range(2)]
        hid = [st.sb(f"hid{c}", [P, 512]) for c in range(2)]
        hid_hi = [[st.sb(f"hid_hi{n}{c}", [P, 512], F32R) for c in range(2)] for n in range(2)]
        hid_lo = [[st.sb(f"hid_lo{n}{c}", [P, 512], F32R) for c in range(2)] for n in range(2)]
        y_t = st.sb("y_t", [P, NK, T])
        p_g = [st.ps(f"p_g{c}") for c in range(2)]
        p_u = [st.ps(f"p_u{c}") for c in range(2)]
        p_y = [[st.ps(f"p_y{o}{c}") for c in range(2)] for o in range(NK)]
        w_loaded = [st.sem(f"w_loaded{n}") for n in range(2)]
        coef_loaded = [st.sem(f"coef_loaded{n}") for n in range(2)]
        up_hi_ready = st.sem("up_hi_ready")
        up_lo_ready = st.sem("up_lo_ready")
        down_hi_ready = st.sem("down_hi_ready")
        down_lo_ready = st.sem("down_lo_ready")
        g_done = st.sem("g_done")
        u_done = st.sem("u_done")
        silu_done = st.sem("silu_done")
        gated_done = st.sem("gated_done")
        hid_done = st.sem("hid_done")
        hid_hi_done = st.sem("hid_hi_done")
        hid_lo_done = st.sem("hid_lo_done")
        down_done = st.sem("down_done")
        y_copied = st.sem("y_copied")
        y_turned = st.sem("y_turned")
        turn_in = [p_g[0], p_g[1], p_u[0], p_u[1]]
        n_coef = [len(mx.rows(t)) for t in range(NT)]
        ROUNDS = NT // 2 - 1
        p_x, p_l, p_c = p_y, p_y[0][0], p_y[1]
        p_logits = p_l[:, 0:NI * n_logits].rearrange("p (i e) -> p i e", i=NI)

        with nc.Block() as block:
            @block.sync
            def _(sp):
                sp.dma_start(router[:], a[f"router{layer}"]).then_inc(loaded, 16)
                if layer == 2:
                    src = a["router_bias"]
                    sp.dma_start(bias[:], bass.AP(src.tensor, src.offset, [[0, P], [1, E]])).then_inc(loaded, 16)
                for t in range(2):
                    sp.dma_start(w[t][:], a[f"w{layer}"][t, :, :]).then_inc(w_loaded[t], 16)
                sp.wait_ge(coef_t_ready, 2)
                sp.dma_start(m.coef[0:E1, :], coef_t[:]).then_inc(stored, 16)
                sp.wait_ge(stored, 16)
                for t in range(NT):
                    if layer == 2 and t == NT // 2:
                        load_last_attention(sp, m, a)
                    if t >= 2:
                        wait(sp, down_lo_ready, t, 1, -1)
                        sp.dma_start(w[t % 2][:], a[f"w{layer}"][t, :, :]).then_inc(w_loaded[t % 2], 16)
                    elif SHARED:
                        continue
                    wait(sp, hid_done, t, 2, -2)
                    for p0, p1, e in mx.rows(t):
                        src = m.coef[e:e + 1, :]
                        sp.dma_start(coef[t % 2][p0:p1, :],
                                     bass.AP(src.tensor, src.offset, [[0, p1 - p0], [1, T]])
                                     ).then_inc(coef_loaded[t % 2], 16)
                    if n_coef[t] == 1:
                        sp.sem_inc(coef_loaded[t % 2], 16)

            @block.tensor
            def _(pe):
                def gate_up(t):
                    n = slot(t, 2)
                    for c in range(2):
                        tok = slice(c * 512, (c + 1) * 512)
                        wait(pe, gated_done, t, 2, c - 1)
                        if not isinstance(t, Step) and t == 0:
                            pe.wait_ge(x_lo_ready, 2 * c + 2)
                        if c == 0:
                            wait(pe, up_hi_ready, t, 1, 1)
                            wait(pe, up_lo_ready, t, 1, 1)
                        for s, (p, done) in enumerate(((p_g[c], g_done), (p_u[c], u_done))):
                            passes = [(w_, x_, k) for w_, x_ in ((up_hi, x_hi), (up_hi, x_lo), (up_lo, x_hi))
                                      for k in range(NK)]
                            for i, (w_, x_, k) in enumerate(passes):
                                last = nc.tensor.matmul(p[:], w_[n][:, (2 * k + s) * P:(2 * k + s + 1) * P],
                                                        x_[:, k, tok], start=(i == 0), stop=(i == len(passes) - 1))
                            last.then_inc(done, 1)

                def down(t, start=False, stop=False):
                    n = slot(t, 2)
                    for c in range(2):
                        wait(pe, hid_lo_done, t, 2, c + 1)
                        if c == 0:
                            wait(pe, down_lo_ready, t, 1, 1)
                        for o in range(NK):
                            passes = [(down_hi, hid_hi), (down_hi, hid_lo), (down_lo, hid_hi)]
                            for i, (w_, h_) in enumerate(passes):
                                last = nc.tensor.matmul(p_y[o][c][:], w_[n][:, o * P:(o + 1) * P], h_[n][c][:],
                                                        start=start and i == 0, stop=stop and i == len(passes) - 1,
                                                        skip_group_check=True)
                        last.then_inc(down_done, 1)

                for i in range(NI):
                    pe.wait_ge(norm.xn_ready, i + 1)
                    for k in range(NK):
                        last = nc.tensor.transpose(p_x[k][i // 4][:, i % 4 * P:i % 4 * P + P],
                                                   m.xn[:, i, k * P:(k + 1) * P], m.ident[:])
                    if i % 4 == 3:
                        last.then_inc(turned, 1)
                pe.wait_ge(loaded, 16 * n_loads)
                for i in range(NI):
                    pe.wait_ge(x_t_ready, 2 * (i // 4) + 2)
                    for k in range(NK):
                        last = nc.tensor.matmul(p_l[:, i * n_logits:(i + 1) * n_logits],
                                                x_t[:, k, i * P:(i + 1) * P], router[:, k, :],
                                                start=(k == 0), stop=(k == NK - 1))
                last.then_inc(logits, 1)
                pe.sem_inc(down_done, 1)
                gate_up(0)
                pe.wait_ge(coef_ready, 1)
                for i in range(NI):
                    last = nc.tensor.transpose(p_c[i // 4][0:E1, i % 4 * P:i % 4 * P + P], by_token[:, i, :],
                                               m.ident[:])
                    if i % 4 == 3:
                        last.then_inc(coef_turned, 1)
                gate_up(1)
                pe.wait_ge(coef_t_ready, 2)
                down(0, start=True)
                with pe.Fori(0, ROUNDS) as g:
                    for r in range(2):
                        gate_up(Step(g, r + 2, 2))
                        down(Step(g, r + 1, 2))
                down(NT - 1, stop=True)
                for n in range(4):
                    pe.wait_ge(y_copied, 4 if n >= 2 else 2)
                    for i in (2 * n, 2 * n + 1):
                        for o in range(NK):
                            last = nc.tensor.transpose(turn_in[n][:, i % 2 * D + o * P:i % 2 * D + (o + 1) * P],
                                                       y_t[:, o, i * P:(i + 1) * P], m.ident[:])
                    last.then_inc(y_turned, 1)

            @block.scalar
            def _(act):
                def split_up(t):
                    act.wait_ge(w_loaded[slot(t, 2)], uses(t, 2) * 16 + 16)
                    nc.scalar.activation(up_hi[slot(t, 2)][:], w[slot(t, 2)][:, 0:UP],
                                         ACT.Copy).then_inc(up_hi_ready, 1)

                def split_down(t):
                    wait(act, down_done, t, 2, -1)
                    nc.scalar.activation(down_hi[slot(t, 2)][:], w[slot(t, 2)][:, UP:UP + D],
                                         ACT.Copy).then_inc(down_hi_ready, 1)

                def silu(t, c):
                    wait(act, g_done, t, 2, c + 1)
                    nc.scalar.activation(act_g[c][:], p_g[c][:], ACT.Silu).then_inc(silu_done, 1)

                def high(t, c):
                    wait(act, hid_done, t, 2, c + 1)
                    nc.scalar.activation(hid_hi[slot(t, 2)][c][:], hid[c][:], ACT.Copy).then_inc(hid_hi_done, 1)

                def tile(t, more=True, between=lambda: None):
                    silu(t, 0)
                    if more:
                        split_up(t + 1)
                    silu(t, 1)
                    between()
                    high(t, 0)
                    high(t, 1)
                    if more:
                        split_down(t + 1)

                def copy_coefficients():
                    for n in range(2):
                        act.wait_ge(coef_turned, n + 1)
                        nc.scalar.activation(coef_t[:, n * 512:(n + 1) * 512], p_c[n][0:E1, :],
                                             ACT.Copy).then_inc(coef_t_ready, 1)

                split_up(0)
                split_down(0)
                norm.scalar(act)
                for n in range(4):
                    act.wait_ge(x_t_ready, n + 1)
                    at = (slice(None), n % 2, slice(n // 2 * 512, n // 2 * 512 + 512))
                    nc.scalar.activation(x_hi[at], x_t[at], ACT.Copy).then_inc(x_hi_ready, 1)
                if layer == 2:
                    act.wait_ge(logits, 1)
                    nc.scalar.activation(scores[:, :, 0:E], p_logits, ACT.Sigmoid).then_inc(scored, 1)
                else:
                    act.wait_ge(shifted, 1)
                    nc.scalar.activation(scores[:, :, 0:E], scores[:, :, 0:E], ACT.Exp).then_inc(scored, 1)
                    if layer == 3:
                        nc.scalar.activation(by_token[:, :, E:E1], by_token[:, :, E:E1], ACT.Sigmoid).then_inc(scored, 1)
                tile(0, between=copy_coefficients)
                with act.Fori(0, ROUNDS) as g:
                    for r in range(2):
                        tile(Step(g, r + 1, 2))
                tile(NT - 1, more=False)
                act.wait_ge(down_done, 2 * NT)
                for o in range(NK):
                    nc.scalar.activation(y_t[:, o, 0:512], p_y[o][0][:], ACT.Copy).then_inc(y_copied, 1)

            @block.gpsimd
            def _(pool):
                def split(t, hi, lo, cols, hi_ready, lo_ready):
                    wait(pool, hi_ready, t, 1, 1)
                    nc.gpsimd.tensor_tensor(lo[slot(t, 2)][:], w[slot(t, 2)][:, cols], hi[slot(t, 2)][:],
                                            ALU.subtract).then_inc(lo_ready, 1)

                def split_up(t):
                    split(t, up_hi, up_lo, slice(0, UP), up_hi_ready, up_lo_ready)

                def split_down(t):
                    split(t, down_hi, down_lo, slice(UP, UP + D), down_hi_ready, down_lo_ready)

                def weigh(t, c):
                    if c == 0:
                        pool.wait_ge(coef_loaded[slot(t, 2)], uses(t, 2) * 32 + 32)
                    wait(pool, gated_done, t, 2, c + 1)
                    nc.gpsimd.tensor_tensor(hid[c][:], gated[c][:], coef[slot(t, 2)][:, c * 512:(c + 1) * 512],
                                            ALU.mult).then_inc(hid_done, 1)

                def tile(t, more=True):
                    weigh(t, 0)
                    if more:
                        split_up(t + 1)
                    weigh(t, 1)
                    if more:
                        split_down(t + 1)

                if SHARED:
                    for n in range(2):
                        nc.gpsimd.memset(coef[n][:], 1.0).then_inc(coef_loaded[n], 32)
                split_up(0)
                split_down(0)
                split_up(1)
                weigh(0, 0)
                weigh(0, 1)
                split_down(1)
                with pool.Fori(0, ROUNDS) as g:
                    for r in range(2):
                        tile(Step(g, r + 1, 2))
                tile(NT - 1, more=False)

            @block.vector
            def _(dve):
                def gate(t, c):
                    wait(dve, silu_done, t, 2, c + 1)
                    wait(dve, u_done, t, 2, c + 1)
                    nc.vector.tensor_tensor(gated[c][:], act_g[c][:], p_u[c][:], ALU.mult).then_inc(gated_done, 1)

                def low(t, c):
                    wait(dve, hid_hi_done, t, 2, c + 1)
                    nc.vector.tensor_tensor(hid_lo[slot(t, 2)][c][:], hid[c][:], hid_hi[slot(t, 2)][c][:],
                                            ALU.subtract).then_inc(hid_lo_done, 1)

                def tile(t):
                    gate(t, 0)
                    gate(t, 1)
                    low(t, 0)
                    low(t, 1)

                v = nc.vector
                link = Link(dve, chain)
                norm.vector(dve, link)
                if pad:
                    link(v.memset(ranked[:, :, E:E + pad], PAD))
                for n in range(2):
                    dve.wait_ge(turned, n + 1)
                    for k in range(NK):
                        v.tensor_copy(x_t[:, k, n * 512:(n + 1) * 512], p_x[k][n][:]).then_inc(x_t_ready, 1)
                for n in range(4):
                    at = (slice(None), n % 2, slice(n // 2 * 512, n // 2 * 512 + 512))
                    dve.wait_ge(x_hi_ready, n + 1)
                    v.tensor_tensor(x_lo[at], x_t[at], x_hi[at], ALU.subtract).then_inc(x_lo_ready, 1)
                sc = scores[:, :, 0:E]
                row = list(total[:].ap[0])
                total_b = bass.AP(total[:].tensor, total[:].offset, [row, [1, NI], [0, E]])
                dve.wait_ge(logits, 1)
                if layer != 2:
                    link(v.tensor_reduce(total[:], p_logits[:, :, 0:E], axis=AX.X, op=ALU.max))
                    if layer == 3:
                        link(v.tensor_copy(by_token[:, :, E:E1], p_logits[:, :, E:E1]))
                    v.tensor_tensor(sc, p_logits[:, :, 0:E], total_b, ALU.subtract).then_inc(shifted, 1)
                    dve.wait_ge(scored, 2 if layer == 3 else 1)
                    link(v.tensor_reduce(total[:], sc, axis=AX.X, op=ALU.add))
                    link(v.reciprocal(total[:], total[:]))
                    link(v.tensor_tensor(sc, sc, total_b, ALU.mult))
                    link(v.tensor_copy(ranked[:, :, 0:E], sc))
                    rank_top(nc, link, ranked, eight, picked, E, mx.top)
                    link(v.tensor_scalar(picked[:, :, 0:E], picked[:, :, 0:E], PAD / 2, None, ALU.is_lt))
                    ins = v.tensor_tensor(by_token[:, :, 0:E], picked[:, :, 0:E], sc, ALU.mult)
                else:
                    dve.wait_ge(scored, 1)
                    dve.wait_ge(loaded, 16 * n_loads)
                    bias_b = bass.AP(bias[:].tensor, bias[:].offset, [list(bias[:].ap[0]), [0, NI], [1, E]])
                    link(v.tensor_tensor(ranked[:], sc, bias_b, ALU.add))
                    quad = ranked[:].rearrange("p i (g q) -> p (i g) q", q=4)
                    link(v.tensor_tensor(pair_hi[:], quad[:, :, 0:2], quad[:, :, 2:4], ALU.max))
                    link(v.tensor_tensor(pair_lo[:], quad[:, :, 0:2], quad[:, :, 2:4], ALU.min))
                    link(v.tensor_tensor(best[:, :, 0:1], pair_hi[:, :, 0:1], pair_hi[:, :, 1:2], ALU.max))
                    link(v.tensor_tensor(best[:, :, 1:2], pair_hi[:, :, 0:1], pair_hi[:, :, 1:2], ALU.min))
                    link(v.tensor_tensor(best[:, :, 2:3], pair_lo[:, :, 0:1], pair_lo[:, :, 1:2], ALU.max))
                    link(v.tensor_tensor(best[:, :, 1:2], best[:, :, 1:2], best[:, :, 2:3], ALU.max))
                    link(v.memset(g_ranked[:, :, GROUPS:], PAD))
                    link(v.tensor_tensor(g_ranked[:, :, 0:GROUPS],
                                         best[:, :, 0].rearrange("p (i g) -> p i g", i=NI),
                                         best[:, :, 1].rearrange("p (i g) -> p i g", i=NI), ALU.add))
                    rank_top(nc, link, g_ranked, eight, g_picked, GROUPS, TOP_GROUPS)
                    link(v.tensor_scalar(g_picked[:], g_picked[:], PAD / 2, None, ALU.is_lt))
                    for q in range(4):
                        part = ranked[:].rearrange("p i (g q) -> p i g q", q=4)[:, :, :, q]
                        last = v.tensor_tensor(part, part, g_picked[:, :, 0:GROUPS], ALU.mult)
                    link(last)
                    link(v.tensor_scalar(ranked[:], ranked[:], 0.0, None, ALU.add))
                    rank_top(nc, link, ranked, eight, picked, E, mx.top)
                    link(v.tensor_scalar(picked[:], picked[:], PAD / 2, None, ALU.is_lt))
                    link(v.tensor_tensor(picked[:], picked[:], sc, ALU.mult))
                    link(v.tensor_reduce(total[:], picked[:], axis=AX.X, op=ALU.add))
                    link(v.reciprocal(total[:], total[:]))
                    link(v.tensor_scalar(total[:], total[:], ROUTED_SCALE, None, ALU.mult))
                    ins = v.tensor_tensor(by_token[:, :, 0:E], picked[:], total_b, ALU.mult)
                if layer != 3:
                    link(ins)
                    ins = v.memset(by_token[:, :, E:E1], 1.0)
                ins.then_inc(coef_ready, 1)
                tile(0)
                with dve.Fori(0, ROUNDS) as g:
                    for r in range(2):
                        tile(Step(g, r + 1, 2))
                tile(NT - 1)
                dve.wait_ge(down_done, 2 * NT + 1)
                dve.wait_ge(y_copied, 2)
                for o in range(NK):
                    nc.vector.tensor_copy(y_t[:, o, 512:1024], p_y[o][1][:]).then_inc(y_copied, 1)
                for n in range(4):
                    dve.wait_ge(y_turned, n + 1)
                    nc.vector.tensor_tensor(m.x[:, 2 * n:2 * n + 2, :], m.x[:, 2 * n:2 * n + 2, :],
                                            turn_in[n][:].rearrange("p (i d) -> p i d", i=2),
                                            ALU.add)



def turn_and_multiply(nc, st, src_bf, m, weights, n_out, emit):
    nk = src_bf.shape[2] // P
    turned_sb = [st.sb(f"turned{n}", [P, nk, P], BF16) for n in range(2)]
    p_t = [st.ctx.enter_context(nc.psum_tensor(f"{st.name}_p_t{n}", [P, nk, P], BF16)) for n in range(2)]
    p_y = [st.ps(f"p_y{n}") for n in range(2)]
    turned = st.sem("turned")
    copied = st.sem("copied")
    product = st.sem("product")
    emitted = st.sem("emitted")

    def tensor(pe, ready):
        def turn(i):
            pe.wait_ge(*ready(i))
            if i >= 2:
                pe.wait_ge(copied, i - 1)
            for k in range(nk):
                last = nc.tensor.transpose(p_t[i % 2][:, k, :], src_bf[:, i, k * P:(k + 1) * P], m.ident_bf[:])
            last.then_inc(turned, 1)

        turn(0)
        for i in range(NI):
            if i + 1 < NI:
                turn(i + 1)
            pe.wait_ge(copied, i + 1)
            if i >= 2:
                pe.wait_ge(emitted, i - 1)
            for k in range(nk):
                last = nc.tensor.matmul(p_y[i % 2][:, 0:n_out], turned_sb[i % 2][:, k, :], weights[:, k, :],
                                        start=(k == 0), stop=(k == nk - 1))
            last.then_inc(product, 1)

    def scalar(act, after=lambda i: None):
        for i in range(NI):
            act.wait_ge(turned, i + 1)
            if i >= 2:
                act.wait_ge(product, i - 1)
            nc.scalar.activation(turned_sb[i % 2][:], p_t[i % 2][:], ACT.Copy).then_inc(copied, 1)
            after(i)

    def vector(dve):
        for i in range(NI):
            dve.wait_ge(product, i + 1)
            emit(i, p_y[i % 2][:, 0:n_out]).then_inc(emitted, 1)

    return tensor, scalar, vector, emitted


def round_clip(nc, link, out, tmp, src, factor, low, high, last_inc=None):
    v = nc.vector
    link(v.tensor_scalar(tmp, src, factor, low, ALU.mult, ALU.max))
    link(v.tensor_scalar(tmp, tmp, high, ROUND, ALU.min, ALU.add))
    ins = v.tensor_scalar(out, tmp, -ROUND, None, ALU.add)
    if last_inc is None:
        link(ins)
    else:
        ins.then_inc(last_inc, 1)


def round_clip_shifted(nc, link, data, factor, low, high, done):
    link(nc.vector.tensor_scalar(data, data, factor, low, ALU.mult, ALU.max))
    nc.vector.tensor_scalar(data, data, high, ROUND, ALU.min, ALU.add).then_inc(done, 1)


def whole_numbers(act, nc, scalar, out, shifted, clipped, ready):
    def whole(i):
        act.wait_ge(clipped, i + 1)
        nc.scalar.activation(out[:, i, :], shifted[:, i, :], ACT.Copy, bias=-ROUND).then_inc(ready, 1)

    whole(0)
    whole(1)
    scalar(act, lambda i: whole(i + 2) if i + 2 < NI else None)


INNER = 4 * D
NH = INNER // P


def ternary_feed_forward(nc, m, a):
    with ExitStack() as outer:
        st0 = Stage(nc, outer, "b0")
        w1 = st0.sb("w1", [P, NK, INNER], BF16)
        w2 = st0.sb("w2", [P, NH, D], BF16)
        w_mean = st0.sb("w_mean", [P, 2])
        xq = st0.sb("xq", [P, NI, D], BF16)
        deq = st0.sb("deq", [P, NI])
        h = st0.sb("h", [P, NI, INNER])
        hq = st0.sb("hq", [P, NI, INNER], BF16)
        square_sum = st0.sb("square_sum", [P, NI])
        largest = st0.sb("largest", [P, NI])
        root = st0.sb("root", [P, NI])
        tmp_v = st0.sb("tmp_v", [P, NI])
        factor = st0.sb("factor", [P, NI])

        def activation_scale(link, root_in, root_ready, dve, width, w):
            v = nc.vector
            v.tensor_scalar(root_in[:], square_sum[:], 1e-24, None, ALU.max).then_inc(root_ready[0], 1)
            dve.wait_ge(root_ready[1], 1)
            link(v.reciprocal(tmp_v[:], root[:]))
            link(v.tensor_tensor(tmp_v[:], tmp_v[:], root_in[:], ALU.mult))
            link(v.tensor_tensor(tmp_v[:], tmp_v[:], root[:], ALU.add))
            link(v.tensor_scalar(tmp_v[:], tmp_v[:], 0.5, None, ALU.mult))
            link(v.reciprocal(tmp_v[:], tmp_v[:]))
            link(v.tensor_scalar(tmp_v[:], tmp_v[:], float(width) ** 0.5, None, ALU.mult))
            link(v.tensor_tensor(largest[:], largest[:], tmp_v[:], ALU.mult))
            link(v.tensor_scalar(largest[:], largest[:], 1e-5, None, ALU.max))
            link(v.reciprocal(factor[:], largest[:]))
            link(v.tensor_scalar(factor[:], factor[:], 127.0, None, ALU.mult))
            link(v.tensor_tensor(factor[:], factor[:], tmp_v[:], ALU.mult))
            link(v.tensor_scalar(deq[:], largest[:], 1.0 / 127.0, w_mean[:, w:w + 1], ALU.mult, ALU.mult))

        with ExitStack() as ctx:
            st = Stage(nc, ctx, "b1")
            raw = [st.sb(f"raw{n}", [P, 2 * INNER]) for n in range(2)]
            sums = st.sb("sums", [P, 2])
            ones = st.sb("ones", [P, P])
            tmp = st.sb("tmp", [P, 2 * INNER])
            junk = st.sb("junk", [P, INNER])
            turned_sb = [st.sb(f"turned{n}", [P, NK, P], BF16) for n in range(2)]
            norm = Norm(st, m.x, m.xn)
            p_mean = st.ps("p_mean")
            p_t = [ctx.enter_context(nc.psum_tensor(f"b1_p_t{n}", [P, NK, P], BF16)) for n in range(2)]
            p_h = [st.ps(f"p_h{n}", [P, 2, 512]) for n in range(2)]
            root_in = st.sb("root_in", [P, NI])
            chain = st.sem("chain")
            loaded = [st.sem(f"loaded{n}") for n in range(2)]
            ones_set = st.sem("ones_set")
            summed = st.sem("summed")
            meaned = st.sem("meaned")
            squared = st.sem("squared")
            to_root = (st.sem("root_in_ready"), st.sem("root_ready"))
            xq_ready = st.sem("xq_ready")
            turned = st.sem("turned")
            copied = st.sem("copied")
            product = st.sem("product")
            gelu1 = st.sem("gelu1")
            gelu2 = st.sem("gelu2")
            h_squared = st.sem("h_squared")
            with nc.Block() as block:
                @block.sync
                def _(sp):
                    for n in range(2):
                        sp.dma_start(raw[n][:], a[f"ternary{n}"]).then_inc(loaded[n], 16)

                @block.gpsimd
                def _(pool):
                    nc.gpsimd.memset(ones[:], 1.0).then_inc(ones_set, 1)

                @block.tensor
                def _(pe):
                    pe.wait_ge(ones_set, 1)
                    pe.wait_ge(summed, 2)
                    nc.tensor.matmul(p_mean[:, 0:2], ones[:], sums[:], start=True, stop=True).then_inc(meaned, 1)
                    for i in range(NI):
                        pe.wait_ge(xq_ready, i + 1)
                        if i >= 2:
                            pe.wait_ge(copied, i - 1)
                        for k in range(NK):
                            last = nc.tensor.transpose(p_t[i % 2][:, k, :], xq[:, i, k * P:(k + 1) * P], m.ident_bf[:])
                        last.then_inc(turned, 1)
                        pe.wait_ge(copied, i + 1)
                        if i >= 2:
                            pe.wait_ge(gelu1, i - 1)
                        for c in range(2):
                            for k in range(NK):
                                last = nc.tensor.matmul(p_h[i % 2][:, c, :], turned_sb[i % 2][:, k, :],
                                                        w1[:, k, c * 512:(c + 1) * 512],
                                                        start=(k == 0), stop=(k == NK - 1))
                        last.then_inc(product, 1)

                @block.scalar
                def _(act):
                    norm.scalar(act)
                    for n in range(2):
                        act.wait_ge(loaded[n], 16)
                        if n == 1:
                            act.wait_ge(summed, 1)
                        nc.scalar.activation(tmp[:], raw[n][:], ACT.Abs,
                                             accum_out=sums[:, n:n + 1]).then_inc(summed, 1)
                    for i in range(NI):
                        act.wait_ge(norm.xn_ready, i + 1)
                        nc.scalar.activation(junk[:, 0:D], m.xn[:, i, :], ACT.Square,
                                             accum_out=square_sum[:, i:i + 1]).then_inc(squared, 1)
                        act.wait_ge(squared, i + 1)
                    act.wait_ge(to_root[0], 1)
                    nc.scalar.activation(root[:], root_in[:], ACT.Sqrt).then_inc(to_root[1], 1)

                    def first(i):
                        act.wait_ge(product, i + 1)
                        nc.scalar.activation(h[:, i, :].rearrange("p (c n) -> p c n", c=2), p_h[i % 2][:], ACT.Gelu,
                                             scale=deq[:, i:i + 1]).then_inc(gelu1, 1)

                    def second(i):
                        act.wait_ge(gelu1, i + 1)
                        nc.scalar.activation(h[:, i, :], h[:, i, :], ACT.Gelu).then_inc(gelu2, 1)

                    def square(i):
                        act.wait_ge(gelu2, i + 1)
                        act.wait_ge(h_squared, i)
                        nc.scalar.activation(junk[:], h[:, i, :], ACT.Square,
                                             accum_out=square_sum[:, i:i + 1]).then_inc(h_squared, 1)

                    for i in range(NI + 1):
                        if i < NI:
                            first(i)
                        if i >= 1:
                            if i >= 2:
                                square(i - 2)
                            second(i - 1)
                    square(NI - 1)

                @block.vector
                def _(dve):
                    v = nc.vector
                    link = Link(dve, chain)
                    norm.vector(dve, link)
                    link(v.tensor_reduce(largest[:], m.xn[:], axis=AX.X, op=ALU.max, apply_absolute_value=True))
                    dve.wait_ge(meaned, 1)
                    link(v.tensor_scalar(w_mean[:], p_mean[:, 0:2], 1.0 / (D * INNER), 1e-5, ALU.mult, ALU.max))
                    link(v.reciprocal(sums[:], w_mean[:]))
                    def ternary(n, w):
                        round_clip(nc, link, w[:].rearrange("p k n -> p (k n)"), tmp[:], raw[n][:],
                                   sums[:, n:n + 1], -1.0, 1.0)

                    ternary(0, w1)
                    dve.wait_ge(squared, NI)
                    activation_scale(link, root_in, to_root, dve, D, 0)
                    for i in range(NI):
                        round_clip(nc, link, xq[:, i, :], tmp[:, 0:D], m.xn[:, i, :], factor[:, i:i + 1],
                                   -128.0, 127.0, xq_ready)
                        dve.wait_ge(turned, i + 1)
                        if i >= 2:
                            dve.wait_ge(product, i - 1)
                        v.tensor_copy(turned_sb[i % 2][:], p_t[i % 2][:]).then_inc(copied, 1)
                    ternary(1, w2)
                    for i in range(NI):
                        dve.wait_ge(gelu2, i + 1)
                        last = v.tensor_reduce(largest[:, i:i + 1], h[:, i, :], axis=AX.X, op=ALU.max,
                                               apply_absolute_value=True)
                    link(last)

        with ExitStack() as ctx:
            st = Stage(nc, ctx, "b2")
            clipped = st.sem("clipped")
            root_in = st.sb("root_in", [P, NI])
            chain = st.sem("chain")
            to_root = (st.sem("root_in_ready"), st.sem("root_ready"))
            hq_ready = st.sem("hq_ready")

            def emit(i, y):
                return nc.vector.scalar_tensor_tensor(m.x[:, i, :], y, deq[:, i:i + 1], m.x[:, i, :],
                                                      ALU.mult, ALU.add)

            tensor, scalar, vector, _ = turn_and_multiply(nc, st, hq, m, w2, D, emit)
            with nc.Block() as block:
                @block.tensor
                def _(pe):
                    tensor(pe, lambda i: (hq_ready, i + 1))

                @block.scalar
                def _(act):
                    act.wait_ge(to_root[0], 1)
                    nc.scalar.activation(root[:], root_in[:], ACT.Sqrt).then_inc(to_root[1], 1)

                    whole_numbers(act, nc, scalar, hq, h, clipped, hq_ready)

                @block.vector
                def _(dve):
                    link = Link(dve, chain)
                    activation_scale(link, root_in, to_root, dve, INNER, 1)
                    for i in range(NI):
                        round_clip_shifted(nc, link, h[:, i, :], factor[:, i:i + 1], -128.0, 127.0, clipped)
                    vector(dve)



XH, XC, L = 16, 16, 64
PAIR = 2 * XC + 2


def token_scale(nc, link, largest, deq, factor):
    link(nc.vector.tensor_scalar(deq, largest, 1.0 / 127.0, 1e-8, ALU.mult, ALU.max))
    link(nc.vector.reciprocal(factor, deq))


def quantized_attention(nc, m, a):
    with ExitStack() as outer:
        st0 = Stage(nc, outer, "c0")
        w_q = [st0.sb(f"w_q{n}", [P, NK, D], BF16) for n in range(2)]
        w_s = [st0.sb(f"w_s{n}", [P, D]) for n in range(2)]
        bias = [st0.sb(f"bias{n}", [P, D]) for n in range(3)]
        mask = st0.sb("mask", [P, NI, L])
        k_heads = st0.sb("k_heads", [P, NK, B, 8, L])
        v_pairs = st0.sb("v_pairs", [P, B, 8, PAIR])
        o = st0.sb("o", [P, NI, D])
        xq = st0.sb("xq", [P, NI, D], BF16)
        largest = st0.sb("largest", [P, NI])
        deq = st0.sb("deq", [P, NI])
        factor = st0.sb("factor", [P, NI])
        clipped = st0.sem("clipped")

        with ExitStack() as ctx:
            st = Stage(nc, ctx, "c1")
            raw, cond, wk, wv = m.raw, m.cond, m.wk, m.wv
            norm = Norm(st, m.x, m.xn)
            whole = [st.sb(f"whole{n}", [P, NK, D], BF16) for n in range(2)]
            tmp = st.sb("tmp", [P, NK, D])
            w_largest = st.sb("w_largest", [P, 2, NK])
            w_deq = st.sb("w_deq", [P, 2, NK])
            w_factor = st.sb("w_factor", [P, 2, NK])
            bk = st.sb("bk", [P, NK])
            own = st.sb("own", [P, 8])
            bk_own = st.sb("bk_own", [P, NK, 8])
            p_w = [ctx.enter_context(nc.psum_tensor(f"c1_p_w{n}", [P, NK, D], BF16)) for n in range(2)]
            p_k = [st.ps(f"p_k{n}") for n in range(4)]
            p_v = [st.ps(f"p_v{n}") for n in range(2)]
            chain = st.sem("chain")
            b_loaded = st.sem("b_loaded")
            whole_ready = st.sem("whole_ready")
            turned = st.sem("turned")
            scale_stored = st.sem("scale_stored")
            scale_ready = st.sem("scale_ready")
            k_done = st.sem("k_done")
            v_done = st.sem("v_done")
            v_copied = st.sem("v_copied")
            zeroed = st.sem("zeroed")
            bk_ready = st.sem("bk_ready")
            with nc.Block() as block:
                @block.sync
                def _(sp):
                    for t, name in ((bk, "xk_b"), (own, "own"), (mask, "mask")):
                        sp.dma_start(t[:], a[name]).then_inc(b_loaded, 16)
                    for n, name in enumerate(("xq_b", "xo_b", "xv_b")):
                        src = a[name]
                        sp.dma_start(bias[n][:], bass.AP(src.tensor, src.offset, [[0, P], [1, D]])
                                     ).then_inc(b_loaded, 16)
                    sp.wait_ge(scale_ready, 1)
                    with nc.allow_non_contiguous_dma(reason="512 scales, once"):
                        for n in range(2):
                            for k in range(NK):
                                dst = m.scales[n:n + 1, k * P:(k + 1) * P]
                                sp.dma_start(bass.AP(dst.tensor, dst.offset, [[1, P], [1, 1]]),
                                             w_deq[:, n, k:k + 1]).then_inc(scale_stored, 16)
                    sp.wait_ge(scale_stored, 4 * 16)
                    for n in range(2):
                        src = m.scales[n:n + 1, :]
                        sp.dma_start(w_s[n][:], bass.AP(src.tensor, src.offset, [[0, P], [1, D]])
                                     ).then_inc(scale_stored, 16)
                    sp.wait_ge(scale_stored, 6 * 16)

                @block.gpsimd
                def _(pool):
                    nc.gpsimd.memset(v_pairs[:], 0.0).then_inc(zeroed, 1)
                    pool.wait_ge(zeroed, 1)
                    for odd in range(2):
                        nc.gpsimd.memset(v_pairs[64 * odd:64 * odd + 64, :, :, 2 * XC + odd], 1.0).then_inc(zeroed, 1)

                @block.tensor
                def _(pe):
                    pe.wait_ge(m.cond_loaded, 3 * 16)
                    for k2 in range(NK):
                        for n in range(2):
                            for k in range(NK):
                                last = nc.tensor.matmul(p_k[2 * k2 + n][:], wk[:, k, k2 * P:(k2 + 1) * P],
                                                        cond[:, k, n * 512:(n + 1) * 512],
                                                        start=(k == 0), stop=(k == NK - 1))
                            last.then_inc(k_done, 1)
                    for pair in range(B // 2):
                        if pair >= 2:
                            pe.wait_ge(v_copied, 2 * (pair - 1))
                        for b2 in range(2):
                            b = 2 * pair + b2
                            for k in range(NK):
                                for odd in range(2):
                                    last = nc.tensor.matmul(p_v[pair % 2][64 * odd:64 * odd + 64, b2 * D:(b2 + 1) * D],
                                                            cond[:, k, b * L:(b + 1) * L], wv[:, k, :],
                                                            start=(k == 0), stop=(k == NK - 1))
                        last.then_inc(v_done, 1)
                    for n in range(2):
                        pe.wait_ge(whole_ready, n + 1)
                        for o2 in range(NK):
                            for k in range(NK):
                                last = nc.tensor.transpose(p_w[n][:, k, o2 * P:(o2 + 1) * P],
                                                           whole[n][:, o2, k * P:(k + 1) * P], m.ident_bf[:])
                        last.then_inc(turned, 1)

                @block.scalar
                def _(act):
                    norm.scalar(act)
                    act.wait_ge(b_loaded, 6 * 16)
                    act.wait_ge(bk_ready, 1)
                    for n4 in range(2 * NK):
                        k2, n = n4 // 2, n4 % 2
                        act.wait_ge(k_done, n4 + 1)
                        for h in range(8):
                            nc.scalar.activation(k_heads[:, k2, 8 * n:8 * n + 8, h, :],
                                                 p_k[n4][:].rearrange("p (b l) -> p b l", l=L), ACT.Identity,
                                                 bias=bk_own[:, k2, h:h + 1], scale=own[:, h:h + 1])

                @block.vector
                def _(dve):
                    v = nc.vector
                    link = Link(dve, chain)
                    norm.vector(dve, link)
                    dve.wait_ge(b_loaded, 6 * 16)
                    for k in range(NK):
                        last = v.tensor_scalar(bk_own[:, k, :], own[:], bk[:, k:k + 1], None, ALU.mult)
                    last.then_inc(bk_ready, 1)
                    link(v.tensor_reduce(largest[:], m.xn[:], axis=AX.X, op=ALU.max, apply_absolute_value=True))
                    token_scale(nc, link, largest[:], deq[:], factor[:])
                    dve.wait_ge(m.raw_loaded, 32)
                    for n in range(2):
                        last = v.tensor_reduce(w_largest[:, n, :], raw[n][:], axis=AX.X, op=ALU.max,
                                               apply_absolute_value=True)
                    link(last)
                    link(v.tensor_scalar(w_deq[:], w_largest[:], 1.0 / 127.0, 1e-8, ALU.mult, ALU.max))
                    v.reciprocal(w_factor[:], w_deq[:]).then_inc(scale_ready, 1)
                    dve.wait_ge(scale_ready, 1)
                    for n in range(2):
                        for k in range(NK):
                            inc = whole_ready if k == NK - 1 else None
                            round_clip(nc, link, whole[n][:, k, :], tmp[:, k, :], raw[n][:, k, :],
                                       w_factor[:, n, k:k + 1], -127.0, 127.0, inc)
                    dve.wait_ge(zeroed, 3)
                    for pair in range(B // 2):
                        dve.wait_ge(v_done, pair + 1)
                        for odd in range(2):
                            part = slice(64 * odd, 64 * odd + 64)
                            src = p_v[pair % 2][part, :].rearrange("p (b q s c) -> p b q s c", b=2, s=2, c=XC)
                            b_v = bias[2][part, :].rearrange("p (q s c) -> p q s c", s=2, c=XC)
                            for b2 in range(2):
                                last = v.tensor_tensor(v_pairs[part, 2 * pair + b2, :, XC * odd:XC * odd + XC],
                                                       src[:, b2, :, odd, :], b_v[:, :, odd, :], ALU.add)
                            last.then_inc(v_copied, 1)
                    for n in range(2):
                        dve.wait_ge(turned, n + 1)
                        v.tensor_copy(w_q[n][:], p_w[n][:])

        with ExitStack() as ctx:
            st = Stage(nc, ctx, "c2")
            chain = st.sem("chain")
            xn_clipped = st.sem("xn_clipped")
            xq_ready = st.sem("xq_ready")
            scaled = st.sem("scaled")

            def emit(i, y):
                return nc.vector.scalar_tensor_tensor(m.xn[:, i, :], y, deq[:, i:i + 1], w_s[0][:],
                                                      ALU.mult, ALU.mult)

            tensor, scalar, vector, emitted = turn_and_multiply(nc, st, xq, m, w_q[0], D, emit)
            with nc.Block() as block:
                @block.tensor
                def _(pe):
                    tensor(pe, lambda i: (xq_ready, i + 1))

                @block.scalar
                def _(act):
                    whole_numbers(act, nc, scalar, xq, m.xn, xn_clipped, xq_ready)

                @block.gpsimd
                def _(pool):
                    for i in range(NI):
                        pool.wait_ge(emitted, i + 1)
                        nc.gpsimd.tensor_tensor(m.xn[:, i, :], m.xn[:, i, :], bias[0][:], ALU.add)

                @block.vector
                def _(dve):
                    link = Link(dve, chain)
                    for i in range(NI):
                        round_clip_shifted(nc, link, m.xn[:, i, :], factor[:, i:i + 1], -127.0, 127.0, xn_clipped)
                    vector(dve)

        with ExitStack() as ctx:
            st = Stage(nc, ctx, "c3")
            q_t = [st.sb(f"q_t{n}", [P, NK, P]) for n in range(2)]
            s = [st.sb(f"s{n}", [P, XH, L]) for n in range(2)]
            top = [st.sb(f"top{n}", [P, XH]) for n in range(2)]
            probs_t = [st.sb(f"probs_t{n}", [P, 8, P]) for n in range(2)]
            inv = [st.sb(f"inv{n}", [P, 8, 2]) for n in range(2)]
            p_q = st.ps("p_q")
            p_s = st.ps("p_s", [P, NK, 512])
            p_p = [st.ps(f"p_p{n}") for n in range(4)]
            p_o = st.ps("p_o")
            chain = st.sem("chain")
            q_turned = st.sem("q_turned")
            q_copied = st.sem("q_copied")
            s_done = st.sem("s_done")
            masked = st.sem("masked")
            topped = st.sem("topped")
            shifted = st.sem("shifted")
            exped = st.sem("exped")
            p_turned = st.sem("p_turned")
            p_copied = st.sem("p_copied")
            weighed = st.sem("weighed")
            inverted = st.sem("inverted")
            o_done = st.sem("o_done")
            with nc.Block() as block:
                @block.tensor
                def _(pe):
                    def scores(i):
                        if i >= 1:
                            pe.wait_ge(q_copied, i)
                        for k in range(NK):
                            last = nc.tensor.transpose(p_q[:, k * P:(k + 1) * P], m.xn[:, i, k * P:(k + 1) * P],
                                                       m.ident[:])
                        last.then_inc(q_turned, 1)
                        pe.wait_ge(q_copied, i + 1)
                        if i >= 1:
                            pe.wait_ge(masked, 2 * i)
                        for k in range(NK):
                            for b2 in range(2):
                                last = nc.tensor.matmul(
                                    p_s[64 * b2:64 * b2 + 64, k, :], q_t[i % 2][:, k, 64 * b2:64 * b2 + 64],
                                    k_heads[:, k, 2 * i + b2, :, :].rearrange("p h l -> p (h l)"),
                                    start=True, stop=True)
                        last.then_inc(s_done, 1)

                    def weigh(i):
                        pe.wait_ge(exped, i + 1)
                        for n in range(2):
                            if i >= 2:
                                pe.wait_ge(p_copied, 2 * (i - 2) + n + 1)
                            for pair in range(4 * n, 4 * n + 4):
                                last = nc.tensor.transpose(
                                    p_p[2 * (i % 2) + n][:, pair % 4 * P:pair % 4 * P + P],
                                    s[i % 2][:, 2 * pair:2 * pair + 2, :].rearrange("p h l -> p (h l)"), m.ident[:])
                            last.then_inc(p_turned, 1)
                        if i >= 1:
                            pe.wait_ge(o_done, i)
                        pe.wait_ge(p_copied, 2 * i + 2)
                        for pair in range(8):
                            for b2 in range(2):
                                last = nc.tensor.matmul(p_o[64 * b2:64 * b2 + 64, pair * PAIR:(pair + 1) * PAIR],
                                                        probs_t[i % 2][:, pair, 64 * b2:64 * b2 + 64],
                                                        v_pairs[:, 2 * i + b2, pair, :], start=True, stop=True)
                        last.then_inc(weighed, 1)

                    scores(0)
                    for i in range(NI):
                        if i + 1 < NI:
                            scores(i + 1)
                        weigh(i)

                @block.scalar
                def _(act):
                    def copy_q(i):
                        act.wait_ge(q_turned, i + 1)
                        nc.scalar.activation(q_t[i % 2][:].rearrange("p k t -> p (k t)"), p_q[:, 0:D],
                                             ACT.Copy).then_inc(q_copied, 1)

                    def exps(i):
                        act.wait_ge(shifted, i + 1)
                        nc.scalar.activation(s[i % 2][:], s[i % 2][:], ACT.Exp).then_inc(exped, 1)

                    def copy_p(i):
                        for n in range(2):
                            act.wait_ge(p_turned, 2 * i + n + 1)
                            if i >= 2 and n == 0:
                                act.wait_ge(weighed, i - 1)
                            nc.scalar.activation(probs_t[i % 2][:, 4 * n:4 * n + 4, :],
                                                 p_p[2 * (i % 2) + n][:].rearrange("p (h t) -> p h t", h=4),
                                                 ACT.Copy).then_inc(p_copied, 1)

                    copy_q(0)
                    for i in range(NI):
                        if i + 1 < NI:
                            copy_q(i + 1)
                        exps(i)
                        copy_p(i)

                @block.vector
                def _(dve):
                    v = nc.vector
                    link = Link(dve, chain)

                    def soften(i):
                        n = i % 2
                        dve.wait_ge(s_done, i + 1)
                        if i >= 2:
                            dve.wait_ge(p_turned, 2 * (i - 1))
                        m_i = mask[:, i, :]
                        m_b = bass.AP(m_i.tensor, m_i.offset, [list(m_i.ap[0]), [0, 8], [1, L]])
                        for k in range(NK):
                            v.scalar_tensor_tensor(s[n][:, 8 * k:8 * k + 8, :],
                                                   p_s[:, k, :].rearrange("p (h l) -> p h l", h=8), XC ** -0.5,
                                                   m_b, ALU.mult, ALU.add).then_inc(masked, 1)
                        dve.wait_ge(masked, 2 * i + 2)
                        v.tensor_reduce(top[n][:], s[n][:], axis=AX.X, op=ALU.max).then_inc(topped, 1)
                        dve.wait_ge(topped, i + 1)
                        t = top[n][:]
                        v.tensor_tensor(s[n][:], s[n][:], bass.AP(t.tensor, t.offset, [list(t.ap[0]), [1, XH], [0, L]]),
                                        ALU.subtract).then_inc(shifted, 1)

                    def divide(i):
                        dve.wait_ge(weighed, i + 1)
                        y = p_o[:, 0:8 * PAIR].rearrange("p (q c) -> p q c", q=8)
                        r = inv[i % 2]
                        v.reciprocal(r[:], y[:, :, 2 * XC:PAIR]).then_inc(inverted, 1)
                        dve.wait_ge(inverted, i + 1)
                        for odd in range(2):
                            w = r[:, :, odd:odd + 1]
                            w = bass.AP(w.tensor, w.offset, [list(w.ap[0]), [2, 8], [0, XC]])
                            dst = o[:, i, :].rearrange("p (q s c) -> p q s c", s=2, c=XC)[:, :, odd, :]
                            last = v.tensor_tensor(dst, y[:, :, XC * odd:XC * odd + XC], w, ALU.mult)
                        last.then_inc(o_done, 1)

                    def quantize(i):
                        dve.wait_ge(o_done, i + 1)
                        t = slice(i, i + 1)
                        link(v.tensor_reduce(largest[:, t], o[:, i, :], axis=AX.X, op=ALU.max,
                                             apply_absolute_value=True))
                        token_scale(nc, link, largest[:, t], deq[:, t], factor[:, t])
                        round_clip_shifted(nc, link, o[:, i, :], factor[:, t], -127.0, 127.0, clipped)

                    soften(0)
                    for i in range(NI):
                        if i + 1 < NI:
                            soften(i + 1)
                        if i >= 1:
                            quantize(i - 1)
                        divide(i)
                    quantize(NI - 1)

        with ExitStack() as ctx:
            st = Stage(nc, ctx, "c4")
            y_sb = st.sb("y", [P, NI, D])
            oq_ready = st.sem("oq_ready")
            biased = st.sem("biased")

            def emit(i, y):
                return nc.vector.scalar_tensor_tensor(y_sb[:, i, :], y, deq[:, i:i + 1], w_s[1][:],
                                                      ALU.mult, ALU.mult)

            tensor, scalar, vector, emitted = turn_and_multiply(nc, st, xq, m, w_q[1], D, emit)
            with nc.Block() as block:
                @block.tensor
                def _(pe):
                    tensor(pe, lambda i: (oq_ready, i + 1))

                @block.scalar
                def _(act):
                    whole_numbers(act, nc, scalar, xq, o, clipped, oq_ready)

                @block.gpsimd
                def _(pool):
                    for i in range(NI):
                        nc.gpsimd.tensor_tensor(m.x[:, i, :], m.x[:, i, :], bias[1][:], ALU.add).then_inc(biased, 1)
                    for i in range(NI):
                        pool.wait_ge(biased, i + 1)
                        pool.wait_ge(emitted, i + 1)
                        nc.gpsimd.tensor_tensor(m.x[:, i, :], m.x[:, i, :], y_sb[:, i, :], ALU.add)

                @block.vector
                def _(dve):
                    vector(dve)



class Memory:

    def k_dram_of(self, layer):
        return self.k_unit if layer == 1 else self.k_plain


def program(nc, a, out, stages):
    with ExitStack() as ctx:
        st = Stage(nc, ctx, "all")
        m = Memory()
        m.x = st.sb("x", [P, NI, D])
        m.xn = st.sb("xn", [P, NI, D])
        m.ident = st.sb("ident", [P, P])
        m.ident_bf = st.sb("ident_bf", [P, P], BF16)
        m.select = st.sb("select", [P, 2, 2, P])
        m.gamma = st.sb("gamma", [P, 1])
        row = CH * HEADS * D
        m.k_plain = nc.dram_tensor("k_plain", [B, len(K_COPIES), row], BF16).ap()
        m.k_unit = nc.dram_tensor("k_unit", [B, len(K_COPIES), row], BF16).ap()
        m.q_parts = nc.dram_tensor("q_parts", [B, len(Q_COPIES), row], BF16).ap()
        m.coef = nc.dram_tensor("coef", [max(mx.experts for mx in MIXTURES.values()) + 1, T], F32).ap()
        m.scales = nc.dram_tensor("scales", [2, D], F32).ap()
        m.raw = [st.sb(f"raw{n}", [P, NK, D]) for n in range(2)]
        m.cond = st.sb("cond", [P, NK, T])
        m.wk = st.sb("wk", [P, NK, D])
        m.wv = st.sb("wv", [P, NK, D])
        m.raw_loaded = st.sem("raw_loaded")
        m.cond_loaded = st.sem("cond_loaded")
        m.x_loaded = st.sem("x_loaded")
        m.constants_loaded = st.sem("constants_loaded")
        Stage.held = []
        if stages[0] != STAGES[0]:
            with nc.Block() as block:
                @block.sync
                def _(sp):
                    load_inputs(sp, m, a)
                    if stages[0][1] == 3:
                        load_last_attention(sp, m, a)
                    sp.wait_ge(m.x_loaded, 16)

                @block.vector
                def _(dve):
                    dve.wait_ge(m.constants_loaded, 48)
                    nc.vector.tensor_copy(m.ident_bf[:], m.ident[:])
        for stage in stages:
            kind, layer = stage
            if kind == "xattn" and layer < 3:
                attention(nc, m, a, layer)
            elif kind == "xattn":
                quantized_attention(nc, m, a)
            elif layer == 0:
                ternary_feed_forward(nc, m, a)
            else:
                mixture(nc, m, a, layer)
            if kind == "ffn":
                Stage.recycle(nc)
        stored = st.sem("stored")
        with nc.Block() as block:
            @block.sync
            def _(sp):
                sp.dma_start(out, m.x[:]).then_inc(stored, 16)
                sp.wait_ge(stored, 16)



def tokens_in(x):
    n = x.shape[-1]
    return x.reshape(NI, 2, HEADS, CH, n).transpose(1, 3, 2, 0, 4).reshape(P, NI, n)


def tokens_out(y):
    return y.reshape(2, CH, HEADS, NI, D).transpose(3, 0, 2, 1, 4).reshape(B, S, D)


def pack_experts(layer, gate, up, down, s_gate, s_up, s_down):
    mx = MIXTURES[layer]
    gap = np.zeros((mx.shared_tiles * P - s_down.shape[0], D), np.float32)
    down = np.concatenate([s_down, gap, down], 0)
    gu = np.stack([np.concatenate([s_gate, gap.T, gate], 1), np.concatenate([s_up, gap.T, up], 1)], 0)
    gu = gu.reshape(2, NK, P, mx.tiles, P).transpose(3, 2, 1, 0, 4).reshape(mx.tiles, P, UP)
    return np.concatenate([gu, down.reshape(mx.tiles, P, D)], 2)


def width_first(w):
    return w.reshape(NK, P, -1).transpose(1, 0, 2)


def layout(inputs):
    f = np.float32
    I = {n: np.asarray(v) for n, v in inputs.items()}
    x, ctx = np.asarray(inputs["x"]), np.asarray(inputs["ctx_2048"])
    arrays = {"x": tokens_in(x), "ctx": tokens_in(ctx)}
    arrays["gamma"] = np.asarray(inputs["L2_xattn_gamma"]).reshape(1)
    arrays["ident"] = np.eye(P, dtype=f)
    p = np.arange(P)
    of_token = p // 64 * 8 + p % HEADS
    gather = np.zeros((P, 2 * P), f)
    gather[p, P - 16 + of_token] = 1.0
    arrays["gather"] = gather
    spread = np.zeros((P, NI, P), f)
    for i in range(NI):
        spread[16 * i + of_token, i, p] = 1.0
    arrays["spread"] = spread
    v = np.zeros((B, P, NK, HEADS, 32), f)
    c4 = ctx.reshape(B, HEADS, CH, NK, P)
    for h in range(HEADS):
        v[:, :, :, h, h % 2:16:2] = c4[:, h].transpose(0, 3, 2, 1)
        v[:, :, :, h, 16 + h % 2:32:2] = 1.0
    arrays["v"] = v.reshape(B, P, NK * HEADS * 32)
    select = np.zeros((P, 2, 2, P), f)
    for j in range(4):
        for c in range(CH):
            for odd in range(2):
                for b2 in range(2):
                    for part in range(2):
                        select[32 * j + 16 * part + 2 * c + odd, b2, part, 64 * b2 + 8 * c + 2 * j + odd] = 1.0
    arrays["select"] = select

    def stack_in(w):
        return w.transpose(1, 0, 2).reshape(D, -1)

    arrays["w1"] = pack_experts(1, stack_in(I["L1_ffn_w_gate"]), stack_in(I["L1_ffn_w_up"]),
                                I["L1_ffn_w_down"].reshape(-1, D), I["L1_ffn_sw_gate"], I["L1_ffn_sw_up"],
                                I["L1_ffn_sw_down"])
    arrays["w2"] = pack_experts(2, stack_in(I["L2_ffn_w_gate"]), stack_in(I["L2_ffn_w_up"]),
                                I["L2_ffn_w_down"].reshape(-1, D), I["L2_ffn_sw_gate"], I["L2_ffn_sw_up"],
                                I["L2_ffn_sw_down"])
    w13 = I["L3_ffn_w13"].reshape(16, 2, 176, D)
    shared = I["L3_ffn_shared_gate_up_w"].reshape(2, 704, D)
    arrays["w3"] = pack_experts(3, w13[:, 0].reshape(-1, D).T, w13[:, 1].reshape(-1, D).T,
                                I["L3_ffn_w2"].transpose(0, 2, 1).reshape(-1, D), shared[0].T, shared[1].T,
                                I["L3_ffn_shared_down_w"].T)
    arrays["ternary0"] = width_first(I["L0_ffn_w1"].T).reshape(P, -1)
    arrays["ternary1"] = I["L0_ffn_w2"].T.reshape(NH, P, D).transpose(1, 0, 2).reshape(P, -1)
    arrays["xq_w"], arrays["xo_w"] = width_first(I["L3_xattn_wq"]), width_first(I["L3_xattn_wo"])
    arrays["xk_w"], arrays["xv_w"] = width_first(I["L3_xattn_wk"].T), width_first(I["L3_xattn_wv"].T)
    arrays["xq_b"], arrays["xo_b"], arrays["xv_b"] = I["L3_xattn_bq"], I["L3_xattn_bo"], I["L3_xattn_bv"]
    arrays["xk_b"] = I["L3_xattn_bk"].reshape(NK, P).T
    arrays["own"] = (p[:, None] // XC == np.arange(8)[None]).astype(f)
    arrays["cond"] = width_first(ctx.reshape(T, D).T)
    arrays["mask"] = tokens_in(I["mask_BxSxS2_ff0"])
    arrays["router1"] = width_first(I["L1_ffn_gate_w"])
    arrays["router2"] = width_first(I["L2_ffn_router_w"])
    arrays["router3"] = width_first(np.concatenate([I["L3_ffn_gate_w"], I["L3_ffn_sgate_w"]], 0).T)
    arrays["router_bias"] = I["L2_ffn_router_bias"]
    return {n: np.ascontiguousarray(v) for n, v in arrays.items()}


STAGES = [("xattn", 0), ("ffn", 0), ("xattn", 1), ("ffn", 1), ("xattn", 2), ("ffn", 2), ("xattn", 3), ("ffn", 3)]


def kernel(**inputs):
    import concourse.bacc as bacc
    from concourse.bass_utils import run_bass_kernel_spmd

    nc = bacc.Bacc("TRN2", target_bir_lowering=False, num_devices=1)
    arrays = layout(inputs)
    args = {n: nc.dram_tensor(f"in_{n}", v.shape, mybir.dt.from_np(v.dtype), kind="ExternalInput").ap()
            for n, v in arrays.items()}
    out = nc.dram_tensor("out", (P, NI, D), F32, kind="ExternalOutput").ap()
    program(nc, args, out, STAGES)
    r = run_bass_kernel_spmd(nc, [{f"in_{n}": v for n, v in arrays.items()}], core_ids=[0])
    return tokens_out(np.asarray(r.results[0]["out"]))
```
